# Optimizing a Trainium2 kernel written in Bass

```python
import numpy as np
import jax
import jax.numpy as jnp

def _softmax(x, axis=-1):
    return jax.nn.softmax(x, axis=axis)

def _gelu(x):
    return jax.nn.gelu(x, approximate=True)

def _silu(x):
    return jax.nn.silu(x)

def _sigmoid(x):
    return jax.nn.sigmoid(x)

def _layernorm(x, axis=-1, eps=1e-05):
    m = jnp.mean(x, axis=axis, keepdims=True)
    v = jnp.var(x, axis=axis, keepdims=True)
    return (x - m) / jnp.sqrt(v + eps)

def _scatter_add(tgt, idx, src, axis=0):
    return tgt.at[idx].add(src)

def _segment_sum(src, seg, n):
    return jax.ops.segment_sum(src, seg, n)
kernel_name = 'mk_sandwich_d1_jaxref_r4_0b5ec1'

def setup_inputs(seed: int=0):
    np.random.seed(seed)
    _w = jnp.asarray

    def _L0_attn_setup():
        import jax, jax.numpy as jnp
        import numpy as np
        B, S, D, H, MLP = (2, 512, 256, 16, 1024)
        DH = D // H
        EPS_LN = 1e-06
        KERNEL_EPS = 0.001

        def layer_norm(x, scale, bias):
            m = jnp.mean(x, axis=-1, keepdims=True)
            v = jnp.mean(jnp.square(x - m), axis=-1, keepdims=True)
            return (x - m) * jax.lax.rsqrt(v + EPS_LN) * scale + bias

        def performer_causal_attention(q, k, v):
            phi_q = jax.nn.relu(q) + KERNEL_EPS
            phi_k = jax.nn.relu(k) + KERNEL_EPS
            kv = jnp.cumsum(jnp.einsum('bshm,bshd->bshmd', phi_k, v), axis=1)
            num = jnp.einsum('bshm,bshmd->bshd', phi_q, kv)
            den = jnp.einsum('bshm,bshm->bsh', phi_q, jnp.cumsum(phi_k, axis=1))
            return num / den[..., None]
        key = jax.random.key(seed)
        ks = jax.random.split(key, 7)

        def w(k, shape, scale):
            return jax.random.normal(k, shape, jnp.float32) * scale
        s_in = 1.0 / np.sqrt(D)
        return {'inputs': jax.random.normal(ks[0], (B, S, D), jnp.float32), 'ln1_scale': jnp.ones((D,), jnp.float32), 'ln1_bias': jnp.zeros((D,), jnp.float32), 'wq': w(ks[1], (D, H, DH), s_in), 'wk': w(ks[2], (D, H, DH), s_in), 'wv': w(ks[3], (D, H, DH), s_in), 'wo': w(ks[4], (H, DH, D), s_in), 'ln2_scale': jnp.ones((D,), jnp.float32), 'ln2_bias': jnp.zeros((D,), jnp.float32), 'w1': w(ks[5], (D, MLP), s_in), 'b1': jnp.zeros((MLP,), jnp.float32), 'w2': w(ks[6], (MLP, D), 1.0 / np.sqrt(MLP)), 'b2': jnp.zeros((D,), jnp.float32)}
    _L0_attn_in = _L0_attn_setup()

    def _L0_ffn_setup():
        import jax, jax.numpy as jnp
        import numpy as np
        H = 256
        I = 512
        E = 8
        B, S = (2, 256)

        def _swiglu(x, wg, wu, wd):
            return jax.nn.silu(x @ wg) * (x @ wu) @ wd
        key = jax.random.key(seed)
        ks = jax.random.split(key, 8)
        sc_h = 1.0 / np.sqrt(H)
        sc_i = 1.0 / np.sqrt(I)
        return {'hidden_states': jax.random.normal(ks[0], (B, S, H), jnp.float32), 'gate_w': jax.random.normal(ks[1], (H, E), jnp.float32) * sc_h, 'sh_gate': jax.random.normal(ks[2], (H, I), jnp.float32) * sc_h, 'sh_up': jax.random.normal(ks[3], (H, I), jnp.float32) * sc_h, 'sh_down': jax.random.normal(ks[4], (I, H), jnp.float32) * sc_i, 'rt_gate': jax.random.normal(ks[5], (E, H, I), jnp.float32) * sc_h, 'rt_up': jax.random.normal(ks[6], (E, H, I), jnp.float32) * sc_h, 'rt_down': jax.random.normal(ks[7], (E, I, H), jnp.float32) * sc_i}
    _L0_ffn_in = _L0_ffn_setup()
    _d = {'L0_attn_inputs': _L0_attn_in['inputs'], 'L0_attn_ln1_scale': _L0_attn_in['ln1_scale'], 'L0_attn_ln1_bias': _L0_attn_in['ln1_bias'], 'L0_attn_wq': _L0_attn_in['wq'], 'L0_attn_wk': _L0_attn_in['wk'], 'L0_attn_wv': _L0_attn_in['wv'], 'L0_attn_wo': _L0_attn_in['wo'], 'L0_attn_ln2_scale': _L0_attn_in['ln2_scale'], 'L0_attn_ln2_bias': _L0_attn_in['ln2_bias'], 'L0_attn_w1': _L0_attn_in['w1'], 'L0_attn_b1': _L0_attn_in['b1'], 'L0_attn_w2': _L0_attn_in['w2'], 'L0_attn_b2': _L0_attn_in['b2'], 'L0_ffn_gate_w': _L0_ffn_in['gate_w'], 'L0_ffn_sh_gate': _L0_ffn_in['sh_gate'], 'L0_ffn_sh_up': _L0_ffn_in['sh_up'], 'L0_ffn_sh_down': _L0_ffn_in['sh_down'], 'L0_ffn_rt_gate': _L0_ffn_in['rt_gate'], 'L0_ffn_rt_up': _L0_ffn_in['rt_up'], 'L0_ffn_rt_down': _L0_ffn_in['rt_down']}
    _x0 = _d['L0_attn_inputs']
    _d['L0_attn_inputs'] = jax.random.normal(jax.random.fold_in(jax.random.key(seed), 1), (4, 1024, 256), dtype=_x0.dtype)
    del _x0
    return _d

def reference(L0_attn_inputs, L0_attn_ln1_scale, L0_attn_ln1_bias, L0_attn_wq, L0_attn_wk, L0_attn_wv, L0_attn_wo, L0_attn_ln2_scale, L0_attn_ln2_bias, L0_attn_w1, L0_attn_b1, L0_attn_w2, L0_attn_b2, L0_ffn_gate_w, L0_ffn_sh_gate, L0_ffn_sh_up, L0_ffn_sh_down, L0_ffn_rt_gate, L0_ffn_rt_up, L0_ffn_rt_down):

    def _L0_attn_ref(inputs, ln1_scale, ln1_bias, wq, wk, wv, wo, ln2_scale, ln2_bias, w1, b1, w2, b2):
        import jax, jax.numpy as jnp
        import numpy as np
        B, S, D, H, MLP = (2, 512, 256, 16, 1024)
        DH = D // H
        EPS_LN = 1e-06
        KERNEL_EPS = 0.001

        def layer_norm(x, scale, bias):
            m = jnp.mean(x, axis=-1, keepdims=True)
            v = jnp.mean(jnp.square(x - m), axis=-1, keepdims=True)
            return (x - m) * jax.lax.rsqrt(v + EPS_LN) * scale + bias

        def performer_causal_attention(q, k, v):
            phi_q = jax.nn.relu(q) + KERNEL_EPS
            phi_k = jax.nn.relu(k) + KERNEL_EPS
            kv = jnp.cumsum(jnp.einsum('bshm,bshd->bshmd', phi_k, v), axis=1)
            num = jnp.einsum('bshm,bshmd->bshd', phi_q, kv)
            den = jnp.einsum('bshm,bshm->bsh', phi_q, jnp.cumsum(phi_k, axis=1))
            return num / den[..., None]
        x = layer_norm(inputs, ln1_scale, ln1_bias)
        q = jnp.einsum('bsd,dhm->bshm', x, wq)
        k = jnp.einsum('bsd,dhm->bshm', x, wk)
        v = jnp.einsum('bsd,dhm->bshm', x, wv)
        attn = performer_causal_attention(q, k, v)
        attn_out = jnp.einsum('bshm,hmd->bsd', attn, wo)
        x = attn_out + inputs
        y = layer_norm(x, ln2_scale, ln2_bias)
        y = jax.nn.gelu(y @ w1 + b1) @ w2 + b2
        return x + y

    def _L0_ffn_ref(hidden_states, gate_w, sh_gate, sh_up, sh_down, rt_gate, rt_up, rt_down):
        import jax, jax.numpy as jnp
        import numpy as np
        H = 256
        I = 512
        E = 8
        B, S = (2, 256)

        def _swiglu(x, wg, wu, wd):
            return jax.nn.silu(x @ wg) * (x @ wu) @ wd
        b, s, h = hidden_states.shape
        x = hidden_states.reshape(-1, h)
        logits = x @ gate_w
        top_val = jnp.max(logits, axis=-1, keepdims=True)
        top_id = jnp.argmax(logits, axis=-1)
        score = jax.nn.sigmoid(top_val)
        xs = x * score
        g = jnp.einsum('th,ehi->eti', xs, rt_gate)
        u = jnp.einsum('th,ehi->eti', xs, rt_up)
        act = jax.nn.silu(g) * u
        y = jnp.einsum('eti,eih->eth', act, rt_down)
        onehot = jax.nn.one_hot(top_id, E, dtype=x.dtype)
        routed = jnp.einsum('eth,te->th', y, onehot)
        shared = _swiglu(x, sh_gate, sh_up, sh_down)
        return (shared + routed).reshape(b, s, h)
    x = L0_attn_inputs
    x = x + _layernorm(_L0_attn_ref(_layernorm(x, axis=-1), L0_attn_ln1_scale, L0_attn_ln1_bias, L0_attn_wq, L0_attn_wk, L0_attn_wv, L0_attn_wo, L0_attn_ln2_scale, L0_attn_ln2_bias, L0_attn_w1, L0_attn_b1, L0_attn_w2, L0_attn_b2), axis=-1)
    x = x + _layernorm(_L0_ffn_ref(_layernorm(x, axis=-1), L0_ffn_gate_w, L0_ffn_sh_gate, L0_ffn_sh_up, L0_ffn_sh_down, L0_ffn_rt_gate, L0_ffn_rt_up, L0_ffn_rt_down), axis=-1)
    return x

_drawn_inputs = setup_inputs


def setup_inputs(seed=0):
    import zlib

    import numpy as np

    out = dict(_drawn_inputs(seed))
    spreads = {'L0_attn_ln1_scale': (1.0, 0.2),
     'L0_attn_ln1_bias': (0.0, 0.1),
     'L0_attn_ln2_scale': (1.0, 0.2),
     'L0_attn_ln2_bias': (0.0, 0.1),
     'L0_attn_b1': (0.0, 0.1),
     'L0_attn_b2': (0.0, 0.1)}
    factors = {}
    for name, (base, spread) in spreads.items():
        noise = np.random.default_rng([zlib.crc32(name.encode()), seed]).standard_normal(out[name].shape)
        drawn = base * np.exp(spread * noise) if base else spread * noise
        out[name] = jnp.asarray(drawn.astype(out[name].dtype))
    for name, factor in factors.items():
        out[name] = (out[name] * factor).astype(out[name].dtype)
    return out
```

```python
from contextlib import ExitStack

import concourse.bass as bass
from concourse import mybir

ALU = mybir.AluOpType
ACT = mybir.ActivationFunctionType
AX = mybir.AxisListType
F32 = mybir.dt.float32
I32 = mybir.dt.int32
U32 = mybir.dt.uint32

P = 128
B, S, D = 4, 1024, 256
H, DH, MLP = 16, 16, 1024
E, I = 8, 512
KC = D // P
TOK = B * S
STEP = 256
NS = TOK // STEP
NT = TOK // P
STEPS_PER_BATCH = S // STEP
VW = 32
VU = DH + 1
G = 4
NRT = NT + E - 1
EW = 2 * KC * I + (I // P) * D
EPS_OUTER, EPS_INNER, KERNEL_EPS = 1e-5, 1e-6, 1e-3

C_ID, C_CAUSAL, C_STRICT, C_ONES = 0, P, 2 * P, 3 * P
C_BLOCK = 4 * P
C_KEEP = C_BLOCK + 8 * VU
C_EREV = C_KEEP + NS
C_TILE = C_EREV + E
C_N = C_TILE + NRT * (E - 1)


def late(k, n):
    return not isinstance(k, int) or k >= n


def hold(eng, sem, value):
    eng.wait_ge(sem, value)
    eng.nop(nofuse=True)


class Chain:

    def __init__(self, eng, sem, per, rnd):
        self.eng, self.sem, self.base, self.n = eng, sem, rnd * per, 0

    def did(self, ins):
        self.n += 1
        ins.then_inc(self.sem, 1)

    def settle(self):
        self.eng.wait_ge(self.sem, self.base + self.n)


def build(nc, x, ln1s, ln1b, wq, wk, wv, wo, ln2s, ln2b, w1, b1, w2, b2, gw, shg, shu, shd, rtg, rtu, rtd, cst,
          h_d, xn_d, xt_d, xs_d, ysh_d, yr_d, out):
    with ExitStack() as ctx:
        def sb(name, shape, dt=F32):
            return ctx.enter_context(nc.sbuf_tensor(name, shape, dt))

        def sem(name):
            return ctx.enter_context(nc.semaphore(name))

        ew = sb("ew", [P, E, EW])
        first = ew[:, E - 2:E, :].rearrange("p e n -> p (e n)")
        wqkv_s = first[:, 0:KC * 3 * D].rearrange("p (c n) -> p c n", c=KC)
        o = KC * 3 * D
        wo_s = first[:, o:o + KC * D].rearrange("p (c n) -> p c n", c=KC)
        o += KC * D
        w1_s = first[:, o:o + KC * MLP].rearrange("p (c n) -> p c n", c=KC)
        o += KC * MLP
        w2_s = first[:, o:o + (MLP // P) * D].rearrange("p (c n) -> p c n", c=MLP // P)
        shw = sb("shw", [P, EW])

        def parts(w):
            return (w[:, 0:KC * I].rearrange("p (c n) -> p c n", c=KC),
                    w[:, KC * I:2 * KC * I].rearrange("p (c n) -> p c n", c=KC),
                    w[:, 2 * KC * I:EW].rearrange("p (c n) -> p c n", c=I // P))

        shg_s, shu_s, shd_s = parts(shw)
        gw_s = sb("gw_s", [P, KC, E])
        cols = sb("cols", [P, 4 * KC + MLP // P])
        ln1s_c, ln1b_c, ln2s_c, ln2b_c = (cols[:, i * KC:(i + 1) * KC] for i in range(4))
        b1_c = cols[:, 4 * KC:]
        b2_s = sb("b2_s", [P, D])
        cs = sb("cs", [P, C_TILE])
        ident = cs[:, C_ID:C_ID + P]
        causal = cs[:, C_CAUSAL:C_CAUSAL + P]
        strict = cs[:, C_STRICT:C_STRICT + P]
        ones = cs[:, C_ONES:C_ONES + P]
        block_mask = cs[:, C_BLOCK:C_BLOCK + 8 * VU].rearrange("p (h n) -> p h n", h=8)
        erev = cs[:, C_EREV:C_EREV + E]
        half = sb("half", [P, 2])
        eps_o = sb("eps_o", [P, 2])
        eps_i = sb("eps_i", [P, 2])

        xin = [sb(f"xin{i}", [P, 2, D]) for i in range(2)]
        xr = sb("xr", [P, 2, D])
        xn = [sb(f"xn{i}", [P, 2, D]) for i in range(2)]
        z = sb("z", [P, 2, D])
        x1t = sb("x1t", [P, KC, STEP])
        qt = sb("qt", [P, 2, STEP])
        kk = sb("kk", [P, 2, D])
        vx = sb("vx", [P, 2, H, VW])
        kt = sb("kt", [P, 2, STEP])
        qx = sb("qx", [P, 2, 2, 8, P])
        st = [sb(f"st{i}", [P, G, P]) for i in range(4)]
        sx = [sb(f"sx{i}", [P, 2, 8, VW]) for i in range(2)]
        su = sb("su", [P, 2, 8, VU])
        ot = [sb(f"ot{i}", [P, 4, P]) for i in range(2)]
        rden = sb("rden", [P, H])
        at = sb("at", [P, 2, D])
        att = sb("att", [P, KC, STEP])
        x2 = sb("x2", [P, 2, D])
        x2b = [sb(f"x2b{i}", [P, 2, D]) for i in range(2)]
        z2 = sb("z2", [P, 2, D])
        y2t = sb("y2t", [P, KC, STEP])
        ht = sb("ht", [P, MLP // P, STEP])
        x3 = sb("x3", [P, 2, D])
        hh = [sb(f"hh{i}", [P, 2, D]) for i in range(2)]
        zrow = hh[0][:, 0, :]
        xm = [sb(f"xm{i}", [P, 2, D]) for i in range(2)]
        x3t = [sb(f"x3t{i}", [P, KC, STEP]) for i in range(2)]
        lns = {n: (sb("bs_" + n, [P, 2, 6]), sb("mv_" + n, [P, 2, 2]), sb("ve_" + n, [P, 2]), sb("rs_" + n, [P, 2]))
               for n in ("x", "n", "a", "y", "h")}
        logit = sb("logit", [P, NT, E])
        lt = att[0:E, 0, :]

        top = sb("top", [P, NT])
        rt = [x2b[i // 2][:, i % 2, :].rearrange("p (t e) -> p t e", t=NT) for i in range(4)]
        rm = sb("rm", [P, NT])
        score = sb("score", [P, NT])
        cnt = [sb(f"cnt{i}", [P, E]) for i in range(4)]
        cnt_i = sb("cnt_i", [P, E], I32)
        slot = sb("slot", [P, NT], U32)
        tcmp = x2[0:1, :, :].rearrange("p a n -> p (a n)")[:, 0:NRT * (E - 1)].rearrange("p (t e) -> p t e", t=NRT)
        tnum = z2[0:1, :, :].rearrange("p a n -> p (a n)")[:, 0:NRT * (E - 1)].rearrange("p (t e) -> p t e", t=NRT)
        eid_f = sb("eid_f", [1, NRT])
        eid = sb("eid", [1, NRT], I32)
        idx = [sb(f"idx{i}", [P, 2], U32) for i in range(2)]

        bank = [ctx.enter_context(nc.psum_tensor(f"bank{i}", [P, 512], F32)) for i in range(8)]
        R0, R1, R2, S0, S1, X, Y, U = bank

        def two(b):
            return b[:, :].rearrange("p (a n) -> p a n", a=2)

        names = ("w_load ones_set zeroed sh_w c_load front_w x1t_done qt_done kk_done vx_done kt_done expanded masks o_done "
                 "norm att_done y2t_done gelu x3t_done logit_done lt_done pe_lt state pe_zt pe_q pe_k pe_v pe_y2t pe_kt pe_w1 pe_x3t pe_log pe_u pe_sc pe_av "
                 "pe_otr pe_att pe_wo pe_w2 lnx lnn lna lny rs_x rs_n rs_a rs_y rs_h x2b_done "
                 "h_st xm_st xt_st xr_ld pool_c small_c route tnum_ld eid_done route_pe route_act sh_g sh_silu sh_act sh_down sh_y "
                 "r_t r_xt r_gu r_silu r_act r_at r_att r_dn r_y ex_w front_free fin fin_a rs_xn fin_pool sc_x sc_sc").split()
        s_ = {n: sem(n) for n in names}
        par_names = "xin_ld h_s xm_s xt_s sld yst rld rst gat fld fst xsl idx_c sct".split()
        p_ = {n: [sem(f"{n}{i}") for i in range(2)] for n in par_names}

        xv = x.rearrange("b (s u p) d -> (b s) p u d", u=2, p=P)
        outv = out.rearrange("b (s u p) d -> (b s) p u d", u=2, p=P)
        hv = h_d.rearrange("(s u p) d -> s p u d", u=2, p=P)
        xnv = xn_d.rearrange("(s u p) d -> s p u d", u=2, p=P)
        yshv = ysh_d.rearrange("(s u p) d -> s p u d", u=2, p=P)
        xsv = xs_d.rearrange("(t p) d -> t p d", p=P)
        yrv = yr_d.rearrange("(t p) d -> t p d", p=P)

        C_LOADS, W_LOADS = 6, 8

        def pick(v, k):
            return v[bass.ds(k, 1)].rearrange("a p u d -> p (a u) d")

        def pick3(v, k):
            return v[bass.ds(k, 1)].rearrange("a p d -> p (a d)")

        ysh = [xin[0], xin[1]]
        sg = [z, x1t, qt, kk]
        actt = [ht[:, 0:4, :], ht[:, 4:8, :]]
        xs_t = [att[:, 0, :], att[:, 1, :]]
        xst = [y2t[:, :, 0:P], y2t[:, :, P:2 * P]]
        sgr = [x3[:, :, :].rearrange("p a n -> p (a n)"), z2[:, :, :].rearrange("p a n -> p (a n)")]
        act_r = [st[0][:, :, :].rearrange("p a n -> p (a n)"), st[1][:, :, :].rearrange("p a n -> p (a n)")]
        att_r = [st[2], st[3]]
        y_r = [ot[0][:, 0:2, :].rearrange("p a n -> p (a n)"), ot[1][:, 0:2, :].rearrange("p a n -> p (a n)")]

        block = ctx.enter_context(nc.Block())

        @block.sync
        def _(sp):
            def load_x(k, par, i):
                sp.dma_start(xin[par][:, :, :], pick(xv, k)).then_inc(p_["xin_ld"][par], 16)

            load_x(0, 0, 0)
            sp.dma_start(cs[:, :], cst[:, 0:C_TILE]).then_inc(s_["c_load"], 16)
            for src, dst in ((ln1s, ln1s_c), (ln1b, ln1b_c)):
                with nc.allow_non_contiguous_dma(reason="a vector into a column per chunk"):
                    sp.dma_start(dst, src.rearrange("(c p) -> p c", p=P)).then_inc(s_["c_load"], 16)
            for i, w in enumerate((wq, wk, wv)):
                sp.dma_start(wqkv_s[:, :, i * D:(i + 1) * D],
                             w.rearrange("(c p) h m -> p c (h m)", p=P)).then_inc(s_["c_load"], 16)
            load_x(1, 1, 0)
            sp.dma_start(wo_s, wo.rearrange("h m d -> (h m) d").rearrange("(c p) d -> p c d", p=P)).then_inc(s_["w_load"], 16)
            for src, dst in ((ln2s, ln2s_c), (ln2b, ln2b_c), (b1, b1_c)):
                with nc.allow_non_contiguous_dma(reason="a vector into a column per chunk"):
                    sp.dma_start(dst, src.rearrange("(c p) -> p c", p=P)).then_inc(s_["w_load"], 16)
            sp.dma_start(b2_s[:, :], b2.rearrange("(a d) -> a d", a=1).to_broadcast([P, D])).then_inc(s_["w_load"], 16)

            def later_weights():
                sp.dma_start(w1_s, w1.rearrange("(c p) n -> p c n", p=P)).then_inc(s_["w_load"], 16)
                sp.dma_start(w2_s, w2.rearrange("(c p) n -> p c n", p=P)).then_inc(s_["w_load"], 16)
                sp.dma_start(gw_s[:, :, :], gw.rearrange("(c p) n -> p c n", p=P)).then_inc(s_["w_load"], 16)

            def zero_rows(j):
                n = NRT // 3
                sp.dma_start(xs_d[j * n * P:(j + 1) * n * P, :].rearrange("(t p) d -> p t d", p=P),
                             zrow.rearrange("p (a d) -> p a d", a=1).to_broadcast([P, n, D])).then_inc(s_["zeroed"], 16)

            def shared_load():
                for w, dst in ((shg, shg_s), (shu, shu_s), (shd, shd_s)):
                    sp.dma_start(dst, w.rearrange("(c p) n -> p c n", p=P)).then_inc(s_["sh_w"], 16)

            def expert_load(e):
                dst = ew[:, bass.ds(e, 1), :].rearrange("p a n -> p (a n)")
                for d, w in zip(parts(dst), (rtg, rtu, rtd)):
                    sp.dma_start(d, w[bass.ds(e, 1)].rearrange("a (c p) n -> p (a c) n", p=P)).then_inc(s_["ex_w"], 16)

            def step(k, i, par, f, m, b, ahead):
                if f:
                    hold(sp, s_["qt_done"], k + 1)
                    if late(k, 1):
                        sp.wait_ge(s_["pe_sc"], 8 * k)
                    for g in range(2):
                        for h in range(8):
                            r = slice(h * DH, (h + 1) * DH)
                            sp.dma_start(qx[r, g, :, h, :],
                                         qt[r, g, :].rearrange("p (u n) -> p u n", u=2)).then_inc(s_["expanded"], 16)
                if ahead:
                    hold(sp, s_["lnx"], 6 * (k + 1))
                    sp.dma_start(xin[par][:, :, :], pick(xv, k + 2)).then_inc(p_["xin_ld"][par], 16)
                if b:
                    hold(sp, s_["lny"], 14 * (k - 1))
                    sp.dma_start(pick(hv, k - 2), hh[par][:, :, :]).then_inc(p_["h_s"][par], 16)
                    sp.dma_start(pick(xnv, k - 2), xm[par][:, :, :]).then_inc(p_["xm_s"][par], 16)
                if m:
                    sp.dma_start(xr[:, :, :], pick(xv, k - 1)).then_inc(s_["xr_ld"], 16)
                if b:
                    hold(sp, s_["x3t_done"], k - 1)
                    sp.dma_start(xt_d[bass.ds(k - 2, 1)].rearrange("a p n -> p (a n)"),
                                 x3t[par][:, :, :].rearrange("p a n -> p (a n)")).then_inc(p_["xt_s"][par], 16)

            sp.wait_ge(s_["pool_c"], 5)
            sp.wait_ge(s_["zeroed"], 1)
            for k in range(4):
                step(k, k // 2, k % 2, True, k >= 1, k >= 2, True)
                if k == 0:
                    later_weights()
                if k <= 1:
                    zero_rows(k)
                if k == 1:
                    zero_rows(2)
                if k == 2:
                    shared_load()
                if k == 3:
                    expert_load(E - 3)
            with sp.Fori(2, NS // 2 - 1) as i:
                for par in range(2):
                    step(2 * i + par, i, par, True, True, True, True)
                expert_load(i - 2)
            for k in range(NS - 2, NS):
                step(k, k // 2, k % 2, True, True, True, False)
            step(NS, NS // 2, 0, False, True, True, False)
            step(NS + 1, NS // 2, 1, False, False, True, False)

            sp.wait_ge(s_["pe_y2t"], NS)
            sp.dma_start(tnum, cst[0:1, C_TILE:C_N].rearrange("p (t e) -> p t e", t=NRT)).then_inc(s_["tnum_ld"], 16)


            def sh_load(s, par):
                sp.dma_start(x3t[par][:, :, :].rearrange("p a n -> p (a n)"),
                             xt_d[bass.ds(s, 1)].rearrange("a p n -> p (a n)")).then_inc(p_["sld"][par], 16)

            def row_load(s, par):
                sp.dma_start(xn[par][:, :, :], pick(xnv, s)).then_inc(p_["xsl"][par], 16)

            def sh_store(s, par):
                hold(sp, s_["sh_y"], s + 1)
                sp.dma_start(pick(yshv, s), ysh[par][:, :, :]).then_inc(p_["yst"][par], 16)

            sp.wait_ge(s_["pe_log"], NS)
            for par in range(2):
                sp.wait_ge(p_["xt_s"][par], 16 * (NS // 2))
                sh_load(par, par)
            for par in range(2):
                sp.wait_ge(p_["xm_s"][par], 16 * (NS // 2))
                sp.wait_ge(p_["h_s"][par], 16 * (NS // 2))
                row_load(par, par)
            sp.wait_ge(s_["pe_w2"], NS)
            for e in range(E - 2, E):
                expert_load(e)

            with sp.Fori(0, NS // 2 - 1) as i:
                for par in range(2):
                    s = 2 * i + par
                    hold(sp, s_["sh_g"], 4 * (s + 1))
                    sh_load(s + 2, par)
                    hold(sp, s_["sc_sc"], 4 * (s + 1))
                    row_load(s + 2, par)
                    sh_store(s, par)
            for s in (NS - 2, NS - 1):
                sh_store(s, s % 2)

            for par in range(2):
                sp.wait_ge(p_["sct"][par], 16 * NT // 2)
            def r_load(t, par):
                sp.dma_start(xs_t[par], pick3(xsv, t)).then_inc(p_["rld"][par], 16)

            def r_store(t, par):
                hold(sp, s_["r_y"], t + 1)
                sp.dma_start(pick3(yrv, t), y_r[par]).then_inc(p_["rst"][par], 16)

            def r_next(t, par):
                hold(sp, s_["r_t"], t - 1)
                r_load(t, par)

            r_load(0, 0)
            r_load(1, 1)
            for t in (2, 3):
                r_next(t, t % 2)
            with sp.Fori(2, (NRT - 1) // 2) as i:
                for par in range(2):
                    r_next(2 * i + par, par)
                    r_store(2 * i + par - 4, par)
            r_next(NRT - 1, 0)
            for t in range(NRT - 5, NRT):
                r_store(t, t % 2)
            sp.wait_ge(p_["rst"][0], 16 * ((NRT + 1) // 2))
            sp.wait_ge(p_["rst"][1], 16 * (NRT // 2))
            sp.sem_inc(s_["fin_pool"], 1)

            def f_load(s, par):
                sp.dma_start(xin[par][:, :, :], pick(yshv, s)).then_inc(p_["fld"][par], 16)
                sp.dma_start(hh[par][:, :, :], pick(hv, s)).then_inc(p_["fld"][par], 16)

            for par in range(2):
                sp.wait_ge(p_["yst"][par], 16 * (NS // 2))
                f_load(par, par)
            with sp.Fori(0, NS // 2 - 1) as i:
                for par in range(2):
                    s = 2 * i + par
                    hold(sp, s_["fin"], 3 * (s + 1))
                    sp.dma_start(pick(outv, s), xm[par][:, :, :]).then_inc(p_["fst"][par], 16)
                    f_load(s + 2, par)
            for s in (NS - 2, NS - 1):
                hold(sp, s_["fin"], 3 * (s + 1))
                sp.dma_start(pick(outv, s), xm[s % 2][:, :, :]).then_inc(p_["fst"][s % 2], 16)
            for par in range(2):
                sp.wait_ge(p_["fst"][par], 16 * (NS // 2))

        @block.gpsimd
        def _(pool):
            nc.gpsimd.memset(zrow, 0.0).then_inc(s_["zeroed"], 1)
            nc.gpsimd.memset(half[:, :], -0.5).then_inc(s_["small_c"], 1)
            nc.gpsimd.memset(eps_o[:, :], EPS_OUTER).then_inc(s_["small_c"], 1)
            nc.gpsimd.memset(eps_i[:, :], EPS_INNER).then_inc(s_["small_c"], 1)
            nc.gpsimd.memset(vx[:, :, :, :], 0.0).then_inc(s_["pool_c"], 1)
            nc.gpsimd.memset(sx[0][:, :, :, :], 0.0).then_inc(s_["pool_c"], 1)
            nc.gpsimd.memset(sx[1][:, :, :, :], 0.0).then_inc(s_["pool_c"], 1)
            pool.wait_ge(s_["small_c"], 3)
            pool.wait_ge(s_["pool_c"], 1)
            nc.gpsimd.memset(vx[:, :, :, DH:DH + 1], 1.0).then_inc(s_["pool_c"], 1)

            def rsqrt(which, eps, stats, n, rs, rnd):
                _, mv, ve, r = lns[which]
                pool.wait_ge(s_[stats], n)
                nc.gpsimd.tensor_tensor(ve[:, :], mv[:, :, 1], eps[:, :], ALU.add).then_inc(s_[rs], 1)
                pool.wait_ge(s_[rs], 2 * rnd + 1)
                nc.gpsimd.tensor_tensor(r[:, :], ve[:, :], half[:, :], ALU.pow).then_inc(s_[rs], 1)

            def step(k, par, f, b, ahead):
                if ahead:
                    rsqrt("x", eps_o, "lnx", 6 * (k + 1) + 4, "rs_x", k + 1)
                if b:
                    rsqrt("y", eps_o, "lny", 14 * (k - 2) + 5, "rs_y", k - 2)
                if ahead:
                    rsqrt("n", eps_i, "lnn", 6 * (k + 1) + 4, "rs_n", k + 1)
                if b:
                    rsqrt("h", eps_o, "lny", 14 * (k - 2) + 12, "rs_h", k - 2)
                if f:
                    rsqrt("a", eps_i, "lna", 7 * k + 5, "rs_a", k)
                    if late(k, 2):
                        pool.wait_ge(s_["lny"], 14 * (k - 2) + 1)
                    if not late(k, 1):
                        pool.wait_ge(s_["w_load"], 16 * W_LOADS)
                    nc.gpsimd.tensor_tensor(x2b[par][:, :, :], x2[:, :, :],
                                            b2_s[:, :].rearrange("p (a d) -> p a d", a=1).to_broadcast([P, 2, D]),
                                            ALU.add).then_inc(s_["x2b_done"], 1)

            rsqrt("x", eps_o, "lnx", 4, "rs_x", 0)
            rsqrt("n", eps_i, "lnn", 4, "rs_n", 0)
            nc.gpsimd.memset(qx[:, :, :, :, :], 0.0).then_inc(s_["pool_c"], 1)
            for k in range(4):
                step(k, k % 2, True, k >= 2, True)
            with pool.Fori(2, NS // 2 - 1) as i:
                for par in range(2):
                    step(2 * i + par, par, True, True, True)
            for k in range(NS - 2, NS):
                step(k, k % 2, True, True, k + 1 < NS)
            step(NS, 0, False, True, False)
            step(NS + 1, 1, False, True, False)

            pool.wait_ge(s_["zeroed"], 49)
            with pool.Fori(0, NS // 2) as i:
                for par in range(2):
                    hold(pool, s_["sc_sc"], 4 * (2 * i + par + 1))
                    for u in range(2):
                        nc.gpsimd.indirect_dma_start(
                            out=xs_d, out_offset=bass.IndirectOffsetOnAxis(ap=idx[par][:, u:u + 1], axis=0),
                            in_=xm[par][:, u, :], in_offset=None).then_inc(p_["sct"][par], 16)

            def gather(i, par):
                hold(pool, p_["idx_c"][par], i + 1)
                for u in range(2):
                    nc.gpsimd.indirect_dma_start(
                        out=xn[par][:, u, :], out_offset=None, in_=yr_d,
                        in_offset=bass.IndirectOffsetOnAxis(ap=idx[par][:, u:u + 1], axis=0)).then_inc(p_["gat"][par], 16)

            pool.wait_ge(s_["fin_pool"], 1)
            gather(0, 0)
            gather(0, 1)
            with pool.Fori(0, NS // 2 - 1) as i:
                for par in range(2):
                    s = 2 * i + par
                    rsqrt("xn"[s % 2 if isinstance(s, int) else par], eps_o, "fin_a", 5 * s + 5, "rs_xn", s)
                    gather(i + 1, par)
            for s in (NS - 2, NS - 1):
                rsqrt("xn"[s % 2 if isinstance(s, int) else par], eps_o, "fin_a", 5 * s + 5, "rs_xn", s)

        @block.scalar
        def _(act):
            def step(k, i, par, f, m, b):
                if f:
                    act.wait_ge(s_["pe_zt"], k + 1)
                    if late(k, 1):
                        act.wait_ge(s_["pe_v"], k)
                    for c in range(KC):
                        ins = nc.scalar.activation(x1t[:, c, :], two(R0)[:, c, :], ACT.Identity,
                                                   bias=ln1b_c[:, c:c + 1], scale=ln1s_c[:, c:c + 1])
                    ins.then_inc(s_["x1t_done"], 1)
                    act.wait_ge(s_["pe_v"], k + 1)
                    if late(k, 1):
                        act.wait_ge(s_["pe_av"], 8 * k)
                        act.wait_ge(s_["pe_u"], 2 * k)
                    nc.scalar.activation(vx[:, :, :, 0:DH], R0[:, :].rearrange("p (u h m) -> p u h m", u=2, h=H),
                                         ACT.Copy).then_inc(s_["vx_done"], 1)
                if m:
                    if not late(k, 2):
                        act.wait_ge(s_["w_load"], 16 * W_LOADS)
                    act.wait_ge(s_["pe_y2t"], k)
                    if late(k, 2):
                        act.wait_ge(s_["pe_w1"], 4 * (k - 1))
                    for c in range(KC):
                        ins = nc.scalar.activation(y2t[:, c, :], two(R1)[:, c, :], ACT.Identity,
                                                   bias=ln2b_c[:, c:c + 1], scale=ln2s_c[:, c:c + 1])
                    ins.then_inc(s_["y2t_done"], 1)
                if f:
                    act.wait_ge(s_["pe_kt"], k + 1)
                    if late(k, 1):
                        act.wait_ge(s_["pe_sc"], 8 * k)
                    nc.scalar.activation(kt[:, :, :], two(R2), ACT.Copy).then_inc(s_["kt_done"], 1)
                if m:
                    if late(k, 2):
                        act.wait_ge(s_["pe_w2"], k - 1)
                    for j in range(4):
                        act.wait_ge(s_["pe_w1"], 4 * (k - 1) + j + 1)
                        for c in range(2):
                            n = 2 * j + c
                            ins = nc.scalar.activation(ht[:, n, :], two((R0, R1, R2, R0)[j])[:, c, :],
                                                       ACT.Gelu_apprx_tanh, bias=b1_c[:, n:n + 1])
                        ins.then_inc(s_["gelu"], 1)
                if b:
                    act.wait_ge(s_["pe_x3t"], k - 2 + 1)
                    if late(k, 4):
                        act.wait_ge(p_["xt_s"][par], 16 * (i - 1))
                        act.wait_ge(s_["pe_log"], k - 3)
                    nc.scalar.activation(x3t[par][:, :, :], two(R1), ACT.Copy).then_inc(s_["x3t_done"], 1)
                if f:
                    for u in range(2):
                        act.wait_ge(s_["pe_av"], 8 * k + 4 * (u + 1))
                        if late(k, 1):
                            act.wait_ge(s_["pe_otr"], 2 * k)
                        nc.scalar.activation(ot[u][:, :, :].rearrange("p a n -> p (a n)"), (X, Y)[u][:, :],
                                             ACT.Copy).then_inc(s_["o_done"], 1)
                    act.wait_ge(s_["pe_att"], k + 1)
                    if late(k, 1):
                        act.wait_ge(s_["pe_wo"], k)
                    nc.scalar.activation(att[:, :, :], two(R1), ACT.Copy).then_inc(s_["att_done"], 1)

            act.wait_ge(s_["c_load"], 16 * C_LOADS)
            act.wait_ge(s_["pool_c"], 4)
            for k in range(4):
                step(k, k // 2, k % 2, True, k >= 1, k >= 2)
            with act.Fori(2, NS // 2) as i:
                for par in range(2):
                    step(2 * i + par, i, par, True, True, True)
            step(NS, NS // 2, 0, False, True, True)
            step(NS + 1, NS // 2, 1, False, False, True)

            act.wait_ge(s_["route"], 1)
            nc.scalar.activation(score[:, :], top[:, :], ACT.Sigmoid).then_inc(s_["route_act"], 1)

            def sh_up(s):
                for j in range(4):
                    act.wait_ge(s_["sh_g"], 4 * s + j + 1)
                    if late(s, 1):
                        act.wait_ge(s_["sh_act"], 4 * s - 4 + j + 1)
                    nc.scalar.activation(sg[j][:, 0, :], two(bank[j])[:, 0, :], ACT.Silu).then_inc(s_["sh_silu"], 1)

            def sh_down(s, i, par):
                act.wait_ge(s_["sh_down"], s + 1)
                if late(i, 1):
                    act.wait_ge(p_["yst"][par], 16 * i)
                nc.scalar.activation(ysh[par][:, :, :], two(bank[4 + par]), ACT.Copy).then_inc(s_["sh_y"], 1)

            sh_up(0)
            sh_up(1)
            sh_down(0, 0, 0)
            sh_up(2)
            sh_down(1, 0, 1)
            with act.Fori(1, NS // 2 - 1) as i:
                for par in range(2):
                    sh_up(2 * i + par + 1)
                    sh_down(2 * i + par, i, par)
            sh_up(NS - 1)
            sh_down(NS - 2, NS // 2 - 1, 0)
            sh_down(NS - 1, NS // 2 - 1, 1)

            def r_xt(t, par):
                act.wait_ge(s_["r_t"], t + 1)
                if late(t, 2):
                    act.wait_ge(s_["r_gu"], t - 1)
                nc.scalar.activation(xst[par], bank[6 + par][:, 0:2 * P].rearrange("p (c n) -> p c n", c=KC),
                                     ACT.Copy).then_inc(s_["r_xt"], 1)

            def r_silu(t, par):
                act.wait_ge(s_["r_gu"], t + 1)
                if late(t, 2):
                    act.wait_ge(s_["r_act"], t - 1)
                nc.scalar.activation(sgr[par], bank[par * 2][:, :], ACT.Silu).then_inc(s_["r_silu"], 1)

            def r_y(t, i, par):
                act.wait_ge(s_["r_dn"], t + 1)
                if late(i, 1):
                    act.wait_ge(p_["rst"][par], 16 * i)
                nc.scalar.activation(y_r[par], bank[5][:, 0:D], ACT.Copy).then_inc(s_["r_y"], 1)

            r_xt(0, 0)
            r_xt(1, 1)
            r_silu(0, 0)
            with act.Fori(1, (NRT - 1) // 2) as i:
                for par in range(2):
                    r_xt(2 * i + par, par)
                    r_silu(2 * i + par - 1, 1 - par)
                    r_y(2 * i + par - 2, i - 1, par)
            r_xt(NRT - 1, 0)
            r_silu(NRT - 2, 1)
            r_y(NRT - 3, NRT // 2 - 1, 0)
            r_silu(NRT - 1, 0)
            r_y(NRT - 2, NRT // 2 - 1, 1)
            r_y(NRT - 1, NRT // 2, 0)

        @block.vector
        def _(dve):
            def stats(c, which, src):
                bs, mv, _, _ = lns[which]
                for u in range(2):
                    c.did(nc.vector.bn_stats(bs[:, u, :], src[:, u, :]))
                hold(dve, c.sem, c.base + c.n)
                for u in range(2):
                    c.did(nc.vector.bn_aggr(mv[:, u, :], bs[:, u, :]))

            def normalise(c, which, dst, src):
                _, mv, _, r = lns[which]
                for u in range(2):
                    c.did(nc.vector.tensor_scalar(dst[:, u, :], src[:, u, :], mv[:, u, 0:1], r[:, u:u + 1],
                                                  ALU.subtract, ALU.mult))

            def in_stats(k, i, par):
                c = Chain(dve, s_["lnx"], 6, k)
                dve.wait_ge(p_["xin_ld"][par], 16 * (i + 1))
                if late(k, 1):
                    dve.wait_ge(s_["rs_x"], 2 * k)
                stats(c, "x", xin[par])
                return c

            def in_norm(c, k, par):
                dve.wait_ge(s_["rs_x"], 2 * k + 2)
                if late(k, 2):
                    dve.wait_ge(s_["lna"], 7 * (k - 2) + 1)
                normalise(c, "x", xn[par], xin[par])
                c.settle()
                c = Chain(dve, s_["lnn"], 6, k)
                if late(k, 1):
                    dve.wait_ge(s_["rs_n"], 2 * k)
                stats(c, "n", xn[par])
                return c

            def in_z(c, k, par):
                dve.wait_ge(s_["rs_n"], 2 * k + 2)
                if late(k, 1):
                    dve.wait_ge(s_["pe_zt"], k)
                normalise(c, "n", z, xn[par])

            def end_x3(k, par):
                c = Chain(dve, s_["lny"], 14, k)
                dve.wait_ge(s_["pe_w2"], k + 1)
                dve.wait_ge(s_["x2b_done"], k + 1)
                if late(k, 1):
                    dve.wait_ge(s_["rs_y"], 2 * k)
                c.did(nc.vector.tensor_tensor(x3[:, :, :], two(X), x2b[par][:, :, :], ALU.add))
                c.settle()
                stats(c, "y", x3)
                return c

            def end_h(c, k, i, par):
                dve.wait_ge(s_["rs_y"], 2 * k + 2)
                normalise(c, "y", x3, x3)
                c.settle()
                dve.wait_ge(s_["xr_ld"], 16 * (k + 1))
                if not late(k, 1):
                    dve.wait_ge(s_["zeroed"], 49)
                if late(k, 2):
                    dve.wait_ge(p_["h_s"][par], 16 * i)
                    dve.wait_ge(s_["rs_h"], 2 * k)
                c.did(nc.vector.tensor_tensor(hh[par][:, :, :], x3[:, :, :], xr[:, :, :], ALU.add))
                c.settle()
                stats(c, "h", hh[par])

            def end_xm(c, k, i, par):
                dve.wait_ge(s_["rs_h"], 2 * k + 2)
                if late(k, 2):
                    dve.wait_ge(p_["xm_s"][par], 16 * i)
                    dve.wait_ge(s_["pe_x3t"], k - 1)
                normalise(c, "h", xm[par], hh[par])

            def state(k, u):
                c = Chain(dve, s_["state"], 2, 2 * k + u)
                dve.wait_ge(s_["pe_u"], 2 * k + u + 1)
                c.did(nc.vector.tensor_tensor(su[:, :, :, :], sx[u][:, :, :, 0:VU],
                                              U[:, 0:2 * 8 * VU].rearrange("p (g h n) -> p g h n", g=2, h=8), ALU.add))
                c.settle()
                if late(k, 1) or u:
                    dve.wait_ge(s_["pe_av"], 8 * k + 4 * u)
                for g in range(2):
                    dst = sx[1 - u][:, g, :, 0:VU]
                    if u:
                        ins = nc.vector.scalar_tensor_tensor(out=dst, in0=su[:, g, :, :],
                                                             scalar=cs[:, bass.ds(C_KEEP + k, 1)], in1=block_mask,
                                                             op0=ALU.mult, op1=ALU.mult)
                    else:
                        ins = nc.vector.tensor_tensor(dst, su[:, g, :, :], block_mask, ALU.mult)
                c.did(ins)

            def mask(k, j):
                dve.wait_ge(s_["pe_sc"], 8 * k + j + 1)
                if late(k, 1) or j >= 4:
                    dve.wait_ge(s_["pe_av"], 8 * k + j - 3)
                nc.vector.tensor_tensor(st[j % 4][:, :, :], (S0, S1)[j % 2][:, :].rearrange("p (h n) -> p h n", h=G),
                                        causal.rearrange("p (a n) -> p a n", a=1).to_broadcast([P, G, P]),
                                        ALU.mult).then_inc(s_["masks"], 1)

            def norm(k, u):
                c = Chain(dve, s_["norm"], 2, 2 * k + u)
                if late(k, 1) or u:
                    c.settle()
                dve.wait_ge(s_["pe_otr"], 2 * k + u + 1)
                o = (R2, R0)[u][:, :].rearrange("p (h n) -> p h n", h=H)
                c.did(nc.vector.reciprocal(rden[:, :], o[:, :, DH]))
                c.settle()
                if late(k, 1):
                    dve.wait_ge(s_["pe_att"], k)
                c.did(nc.vector.tensor_tensor(at[:, u, :].rearrange("p (h m) -> p h m", h=H), o[:, :, 0:DH],
                                              rden[:, :].rearrange("p (h a) -> p h a", a=1).to_broadcast([P, H, DH]),
                                              ALU.mult))

            def mid(k, par):
                c = Chain(dve, s_["lna"], 7, k)
                dve.wait_ge(s_["pe_wo"], k + 1)
                if late(k, 1):
                    dve.wait_ge(s_["x2b_done"], k)
                    dve.wait_ge(s_["rs_a"], 2 * k)
                c.did(nc.vector.tensor_tensor(x2[:, :, :], two(R2), xn[par][:, :, :], ALU.add))
                c.settle()
                stats(c, "a", x2)
                dve.wait_ge(s_["rs_a"], 2 * k + 2)
                if late(k, 1):
                    dve.wait_ge(s_["pe_y2t"], k)
                normalise(c, "a", z2, x2)

            def step(k, i, par, f, b, ahead):
                if f:
                    dve.wait_ge(s_["pe_q"], k + 1)
                    if late(k, 1):
                        dve.wait_ge(s_["expanded"], 256 * k)
                        dve.wait_ge(s_["pe_av"], 8 * k)
                    nc.vector.tensor_scalar(qt[:, :, :], two(R1), 0.0, KERNEL_EPS, ALU.max, ALU.add).then_inc(s_["qt_done"], 1)
                    dve.wait_ge(s_["pe_k"], k + 1)
                    if late(k, 1):
                        dve.wait_ge(s_["pe_u"], 2 * k)
                    nc.vector.tensor_scalar(kk[:, :, :], two(R2), 0.0, KERNEL_EPS, ALU.max, ALU.add).then_inc(s_["kk_done"], 1)
                ip = i + par
                if ahead:
                    ca = in_stats(k + 1, ip, 1 - par)
                if b:
                    cb = end_x3(k - 2, par)
                if ahead:
                    ca = in_norm(ca, k + 1, 1 - par)
                if b:
                    end_h(cb, k - 2, i - 1, par)
                if ahead:
                    in_z(ca, k + 1, 1 - par)
                if b:
                    end_xm(cb, k - 2, i - 1, par)
                if f:
                    state(k, 0)
                    mask(k, 0)
                    mask(k, 1)
                if b:
                    dve.wait_ge(s_["pe_log"], k - 1)
                    if late(k, 3):
                        dve.wait_ge(s_["pe_lt"], k - 2)
                    dve.wait_ge(s_["pe_wo"], k if f else NS)
                    nc.vector.tensor_copy(lt, Y[0:E, 0:STEP]).then_inc(s_["lt_done"], 1)

                def keep_logits():
                    dve.wait_ge(s_["pe_lt"], k - 1)
                    nc.vector.tensor_copy(logit[:, bass.ds(2 * (k - 2), 2), :],
                                          Y[:, STEP:STEP + 2 * E].rearrange("p (u e) -> p u e", u=2)).then_inc(s_["logit_done"], 1)

                if b and not f:
                    keep_logits()
                if f:
                    for j in range(2, 8):
                        mask(k, j)
                        if j == 3 and b:
                            keep_logits()
                        if j == 5:
                            state(k, 1)
                    norm(k, 0)
                    norm(k, 1)
                    mid(k, par)

            dve.wait_ge(s_["pool_c"], 4)
            ca = in_norm(in_stats(0, 0, 0), 0, 0)
            in_z(ca, 0, 0)
            dve.wait_ge(s_["c_load"], 16 * C_LOADS)
            dve.wait_ge(s_["pool_c"], 4)
            for k in range(4):
                step(k, k // 2, k % 2, True, k >= 2, True)
            with dve.Fori(2, NS // 2 - 1) as i:
                for par in range(2):
                    step(2 * i + par, i, par, True, True, True)
            for k in range(NS - 2, NS):
                step(k, k // 2, k % 2, True, True, k + 1 < NS)
            step(NS, NS // 2, 0, False, True, False)
            step(NS + 1, NS // 2, 1, False, True, False)

            def sh_act(s, par):
                if late(s, 2):
                    dve.wait_ge(s_["sh_down"], s - 1)
                for j in range(4):
                    dve.wait_ge(s_["sh_silu"], 4 * s + j + 1)
                    nc.vector.tensor_tensor(actt[par][:, j, :], sg[j][:, 0, :], two(bank[j])[:, 1, :],
                                            ALU.mult).then_inc(s_["sh_act"], 1)

            def scale(s, i, par):
                dve.wait_ge(p_["xsl"][par], 16 * (i + 1))
                if late(i, 1):
                    dve.wait_ge(p_["sct"][par], 32 * i)
                for u in range(2):
                    nc.vector.tensor_scalar(xm[par][:, u, :], xn[par][:, u, :], score[:, bass.ds(2 * s + u, 1)], None,
                                            ALU.mult).then_inc(s_["sc_sc"], 1)
                    nc.vector.tensor_copy(idx[par][:, u:u + 1], slot[:, bass.ds(2 * s + u, 1)]).then_inc(s_["sc_sc"], 1)

            c = Chain(dve, s_["route"], 0, 0)

            def do(ins):
                c.did(ins)
                c.settle()

            def over_e(a):
                return a.rearrange("p (t a) -> p t a", a=1).to_broadcast([P, NT, E])

            def over_t(a):
                return a.rearrange("p (a e) -> p a e", a=1).to_broadcast([P, NT, E])

            r0, r1, r2, r3 = (r[:, :, :] for r in rt)
            dve.wait_ge(s_["logit_done"], NS)
            do(nc.vector.tensor_reduce(top[:, :], logit[:, :, :], AX.X, ALU.max))
            do(nc.vector.tensor_tensor(r1, logit[:, :, :], over_e(top[:, :]), ALU.is_equal))
            do(nc.vector.tensor_tensor(r1, r1, over_t(erev), ALU.mult))
            do(nc.vector.tensor_reduce(rm[:, :], r1, AX.X, ALU.max))
            do(nc.vector.tensor_tensor(r0, r1, over_e(rm[:, :]), ALU.is_equal))
            assert c.n == 5
            sh_act(0, 0)
            dve.wait_ge(s_["route_pe"], 1)
            rank = bank[6][:, 0:NT * E].rearrange("p (t e) -> p t e", t=NT)
            total = bank[6][:, NT * E:2 * NT * E].rearrange("p (t e) -> p t e", t=NT)
            do(nc.vector.tensor_copy(r1, total))
            src, dst = rt[1], rt[2]
            d = 1
            while d < NT:
                nc.vector.tensor_copy(dst[:, 0:d, :], src[:, 0:d, :])
                do(nc.vector.tensor_tensor(dst[:, d:, :], src[:, d:, :], src[:, 0:NT - d, :], ALU.add))
                src, dst = dst, src
                d *= 2
            upto = src[:, :, :]
            sh_act(1, 1)
            do(nc.vector.tensor_scalar(cnt_i[:, :], src[:, NT - 1, :], float(P - 1), None, ALU.add))
            do(nc.vector.tensor_scalar(cnt_i[:, :], cnt_i[:, :], 7, None, ALU.logical_shift_right))
            do(nc.vector.tensor_copy(cnt[0][:, :], cnt_i[:, :]))
            a, b_ = cnt[1], cnt[2]
            do(nc.vector.tensor_copy(a[:, :], cnt[0][:, :]))
            d = 1
            while d < E:
                nc.vector.tensor_copy(b_[:, 0:d], a[:, 0:d])
                do(nc.vector.tensor_tensor(b_[:, d:], a[:, d:], a[:, 0:E - d], ALU.add))
                a, b_ = b_, a
                d *= 2
            do(nc.vector.tensor_tensor(cnt[3][:, :], a[:, :], cnt[0][:, :], ALU.subtract))
            do(nc.vector.tensor_scalar(cnt[3][:, :], cnt[3][:, :], float(P), None, ALU.mult))
            do(nc.vector.tensor_tensor(r3, upto, total, ALU.subtract))
            do(nc.vector.tensor_tensor(r3, r3, rank, ALU.add))
            do(nc.vector.tensor_tensor(r3, r3, over_t(cnt[3][:, :]), ALU.add))
            do(nc.vector.tensor_tensor(r3, r3, r0, ALU.mult))
            do(nc.vector.tensor_reduce(rm[:, :], r3, AX.X, ALU.add))
            do(nc.vector.tensor_copy(slot[:, :], rm[:, :]))
            dve.wait_ge(s_["tnum_ld"], 16)
            do(nc.vector.tensor_tensor(tcmp, tnum,
                                       a[0:1, 0:E - 1].rearrange("p (a e) -> p a e", a=1).to_broadcast([1, NRT, E - 1]),
                                       ALU.is_ge))
            do(nc.vector.tensor_reduce(eid_f[:, :], tcmp, AX.X, ALU.add))
            nc.vector.tensor_copy(eid[:, :], eid_f[:, :]).then_inc(s_["eid_done"], 1)

            dve.wait_ge(s_["route_act"], 1)
            scale(0, 0, 0)
            scale(1, 0, 1)
            with dve.Fori(1, NS // 2) as i:
                for par in range(2):
                    sh_act(2 * i + par, par)
                    scale(2 * i + par, i, par)

            def r_att(t, par):
                dve.wait_ge(s_["r_at"], t + 1)
                if late(t, 2):
                    dve.wait_ge(s_["r_dn"], t - 1)
                nc.vector.tensor_copy(att_r[par][:, :, :], bank[4][:, :].rearrange("p (c n) -> p c n", c=4)).then_inc(s_["r_att"], 1)

            def r_act(t, par):
                dve.wait_ge(s_["r_silu"], t + 1)
                if late(t, 2):
                    dve.wait_ge(s_["r_at"], t - 1)
                nc.vector.tensor_tensor(act_r[par], sgr[par], bank[2 * par + 1][:, :], ALU.mult).then_inc(s_["r_act"], 1)

            r_act(0, 0)
            r_att(0, 0)
            r_act(1, 1)
            r_att(1, 1)
            r_act(2, 0)
            with dve.Fori(2, (NRT - 1) // 2) as i:
                for par in range(2):
                    r_att(2 * i + par - 2, par)
                    r_act(2 * i + par - 1, 1 - par)
            for t in (NRT - 3, NRT - 2):
                r_att(t, t % 2)
                r_act(t + 1, 1 - t % 2)
            r_att(NRT - 1, (NRT - 1) % 2)

            def put_idx(s, i, par):
                if late(i, 1):
                    dve.wait_ge(p_["gat"][par], 32 * i)
                nc.vector.tensor_copy(idx[par][:, :], slot[:, bass.ds(2 * s, 2)]).then_inc(p_["idx_c"][par], 1)

            f3 = (x3, x2)

            def fin_sum(s, i, par):
                c = Chain(dve, s_["fin_a"], 5, s)
                dve.wait_ge(p_["fld"][par], 32 * (i + 1))
                dve.wait_ge(p_["gat"][par], 32 * (i + 1))
                if late(i, 1):
                    dve.wait_ge(s_["fin"], 3 * (s - 1))
                c.did(nc.vector.tensor_tensor(f3[par][:, :, :], xin[par][:, :, :], xn[par][:, :, :], ALU.add))
                c.settle()
                stats(c, "xn"[par], f3[par])

            def fin_out(s, i, par):
                c = Chain(dve, s_["fin"], 3, s)
                dve.wait_ge(s_["rs_xn"], 2 * s + 2)
                normalise(c, "xn"[par], f3[par], f3[par])
                c.settle()
                if late(i, 1):
                    dve.wait_ge(p_["fst"][par], 16 * i)
                c.did(nc.vector.tensor_tensor(xm[par][:, :, :], f3[par][:, :, :], hh[par][:, :, :], ALU.add))

            for par in range(2):
                dve.wait_ge(p_["sct"][par], 16 * NT // 2)
                put_idx(par, 0, par)
            fin_sum(0, 0, 0)
            for s in range(2):
                put_idx(s + 2, 1, s)
                fin_sum(s + 1, (s + 1) // 2, (s + 1) % 2)
                fin_out(s, 0, s)
            with dve.Fori(1, NS // 2 - 1) as i:
                for par in range(2):
                    put_idx(2 * i + par + 2, i + 1, par)
                    fin_sum(2 * i + par + 1, i + par, 1 - par)
                    fin_out(2 * i + par, i, par)
            fin_sum(NS - 1, NS // 2 - 1, 1)
            fin_out(NS - 2, NS // 2 - 1, 0)
            fin_out(NS - 1, NS // 2 - 1, 1)

        @block.tensor
        def _(pe):
            mm = nc.tensor.matmul

            def tile(a, c, u):
                return a[:, c, u * P:(u + 1) * P]

            def score(k, j):
                u, q = divmod(j, 4)
                g = q // 2
                if late(k, 1) or j >= 2:
                    pe.wait_ge(s_["masks"], 8 * k + j - 1)
                mm((S0, S1)[j % 2][:, :], tile(kt, g, u), qx[:, g, u, 4 * (q % 2):4 * (q % 2) + 4, :].rearrange("p h n -> p (h n)"),
                   start=True, stop=True).then_inc(s_["pe_sc"], 1)

            def attend(k, j, b):
                u, q = divmod(j, 4)
                o = (X, Y)[u]
                if q == 0:
                    pe.wait_ge(s_["state"], 2 * (2 * k + u)) if late(k, 1) or u else pe.wait_ge(s_["pool_c"], 4)
                    if u == 0:
                        if b:
                            pe.wait_ge(s_["lny"], 14 * (k - 2) + 1)
                        elif late(k, 1):
                            pe.wait_ge(s_["o_done"], 2 * k - 1)
                    else:
                        if b:
                            pe.wait_ge(s_["logit_done"], k - 1)
                        elif late(k, 1):
                            pe.wait_ge(s_["o_done"], 2 * k)
                pe.wait_ge(s_["masks"], 8 * k + j + 1)
                g = q // 2
                mm(o[:, q * P:(q + 1) * P], sx[u][:, g, 4 * (q % 2):4 * (q % 2) + 4, :].rearrange("p h n -> p (h n)"),
                   tile(qt, g, u), start=True, stop=False, skip_group_check=True)
                for h in range(G):
                    ins = mm(o[h * VW:(h + 1) * VW, q * P:(q + 1) * P], vx[:, u, 4 * q + h, :], st[j % 4][:, h, :],
                             start=False, stop=True, skip_group_check=True)
                ins.then_inc(s_["pe_av"], 1)

            def update(k, u):
                if late(k, 1) or u:
                    pe.wait_ge(s_["state"], 2 * (2 * k + u) - 1)
                for g in range(2):
                    ins = mm(U[:, g * 8 * VU:(g + 1) * 8 * VU], kk[:, u, g * P:(g + 1) * P],
                             vx[:, u, 8 * g:8 * g + 8, 0:VU], start=True, stop=True, skip_group_check=True)
                ins.then_inc(s_["pe_u"], 1)

            def turn(dst, src):
                for c in range(2):
                    for u in range(2):
                        ins = nc.tensor.transpose(dst[:, c, u * P:(u + 1) * P], src[:, u, c * P:(c + 1) * P], ident)
                return ins

            def otr(k, u, m):
                pe.wait_ge(s_["o_done"], 2 * k + u + 1)
                if m:
                    pe.wait_ge(s_["gelu"], 4 * (k - 1) + 3 + u)
                for q in range(4):
                    ins = nc.tensor.transpose((R2, R0)[u][:, q * P:(q + 1) * P], ot[u][:, q, :], ident)
                ins.then_inc(s_["pe_otr"], 1)

            def logits_turn(k):
                hold(pe, s_["lt_done"], k - 1)
                for u in range(2):
                    ins = nc.tensor.transpose(Y[:, STEP + u * E:STEP + (u + 1) * E], lt[:, u * P:(u + 1) * P], ident[0:E, 0:E])
                ins.then_inc(s_["pe_lt"], 1)

            def w2_part(u, blocks):
                for n in blocks:
                    ins = mm(two(X)[:, u, :], tile(ht, n, u), w2_s[:, n, :], start=(n == 0), stop=(n == MLP // P - 1))
                return ins

            def z_turn(k):
                pe.wait_ge(s_["lnn"], 6 * (k + 1))
                if late(k, 1):
                    pe.wait_ge(s_["norm"], 4 * k)
                turn(two(R0), z).then_inc(s_["pe_zt"], 1)

            def step(k, par, f, m, b, ahead):
                if f:
                    pe.wait_ge(s_["x1t_done"], k + 1)
                    if late(k, 1):
                        pe.wait_ge(s_["att_done"], k)
                    for g in range(2):
                        for c in range(KC):
                            ins = mm(two(R1)[:, g, :], wqkv_s[:, c, g * P:(g + 1) * P], x1t[:, c, :],
                                     start=(c == 0), stop=(c == KC - 1))
                    ins.then_inc(s_["pe_q"], 1)
                    if late(k, 1):
                        pe.wait_ge(s_["lna"], 7 * (k - 1) + 1)
                    for n, bk, sm in ((1, R2, "pe_k"), (2, R0, "pe_v")):
                        for u in range(2):
                            for c in range(KC):
                                ins = mm(two(bk)[:, u, :], tile(x1t, c, u), wqkv_s[:, c, n * D:(n + 1) * D],
                                         start=(c == 0), stop=(c == KC - 1))
                        ins.then_inc(s_[sm], 1)
                if m:
                    pe.wait_ge(s_["lna"], 7 * k)
                    pe.wait_ge(s_["qt_done"], k + 1) if f else pe.wait_ge(s_["att_done"], k)
                    turn(two(R1), z2).then_inc(s_["pe_y2t"], 1)
                if f:
                    pe.wait_ge(s_["kk_done"], k + 1)
                    turn(two(R2), kk).then_inc(s_["pe_kt"], 1)
                    pe.wait_ge(s_["vx_done"], k + 1)
                    update(k, 0)
                if m:
                    pe.wait_ge(s_["y2t_done"], k)
                    for j in range(4):
                        if j == 0 and f:
                            pe.wait_ge(s_["vx_done"], k + 1)
                        if j == 2 and f:
                            pe.wait_ge(s_["kt_done"], k + 1)
                        if j == 3:
                            pe.wait_ge(s_["gelu"], 4 * (k - 1) + 1)
                        for a in range(2):
                            n = 2 * j + a
                            for c in range(KC):
                                ins = mm(two((R0, R1, R2, R0)[j])[:, a, :], w1_s[:, c, n * P:(n + 1) * P], y2t[:, c, :],
                                         start=(c == 0), stop=(c == KC - 1))
                        ins.then_inc(s_["pe_w1"], 1)
                if b:
                    pe.wait_ge(s_["lny"], 14 * (k - 1))
                    if m:
                        pe.wait_ge(s_["gelu"], 4 * (k - 1) + 2)
                    turn(two(R1), xm[par]).then_inc(s_["pe_x3t"], 1)
                if f:
                    pe.wait_ge(s_["expanded"], 256 * (k + 1))
                    pe.wait_ge(s_["kt_done"], k + 1)
                    score(k, 0)
                    score(k, 1)
                if b:
                    pe.wait_ge(s_["x3t_done"], k - 1)
                    if f:
                        pe.wait_ge(s_["o_done"], 2 * k)
                    else:
                        pe.wait_ge(s_["logit_done"], k - 2)
                    for c in range(KC):
                        ins = mm(Y[0:E, 0:STEP], gw_s[:, c, :], x3t[par][:, c, :], start=(c == 0), stop=(c == KC - 1))
                    ins.then_inc(s_["pe_log"], 1)
                if b and not f:
                    logits_turn(k)
                if f:
                    attend(k, 0, b)
                    for j in range(2, 8):
                        score(k, j)
                        if j == 3 and b:
                            logits_turn(k)
                        if j == 3:
                            update(k, 1)
                        attend(k, j - 1, b)
                    attend(k, 7, b)
                    otr(k, 0, m)
                if m:
                    if f:
                        pe.wait_ge(s_["o_done"], 2 * k + 1)
                    pe.wait_ge(s_["gelu"], 4 * k)
                    w2_part(0, range(8))
                if f:
                    otr(k, 1, m)
                if m:
                    ins = w2_part(1, range(4 if f else 8))
                if f:
                    pe.wait_ge(s_["norm"], 4 * k + 4)
                    if b:
                        pe.wait_ge(s_["x3t_done"], k - 1)
                    turn(two(R1), at).then_inc(s_["pe_att"], 1)
                    if m:
                        ins = w2_part(1, range(4, 8))
                if m:
                    ins.then_inc(s_["pe_w2"], 1)
                if ahead:
                    z_turn(k + 1)
                if f:
                    pe.wait_ge(s_["att_done"], k + 1)
                    if not late(k, 1):
                        pe.wait_ge(s_["w_load"], 16 * W_LOADS)
                    for u in range(2):
                        for c in range(KC):
                            ins = mm(two(R2)[:, u, :], tile(att, c, u), wo_s[:, c, :], start=(c == 0), stop=(c == KC - 1))
                    ins.then_inc(s_["pe_wo"], 1)

            pe.wait_ge(s_["c_load"], 16 * C_LOADS)
            z_turn(0)
            for k in range(4):
                step(k, k % 2, True, k >= 1, k >= 2, True)
            with pe.Fori(2, NS // 2 - 1) as i:
                for par in range(2):
                    step(2 * i + par, par, True, True, True, True)
            step(NS - 2, 0, True, True, True, True)
            step(NS - 1, 1, True, True, True, False)
            step(NS, 0, False, True, True, False)
            step(NS + 1, 1, False, False, True, False)

            def sh_gate(s, i, par):
                pe.wait_ge(p_["sld"][par], 16 * (i + 1))
                for j in range(4):
                    if late(s, 1):
                        pe.wait_ge(s_["sh_act"], 4 * s - 4 + j + 1)
                    for a, w in enumerate((shg_s, shu_s)):
                        for c in range(KC):
                            ins = mm(two(bank[j])[:, a, :], w[:, c, j * P:(j + 1) * P], x3t[par][:, c, :],
                                     start=(c == 0), stop=(c == KC - 1))
                    ins.then_inc(s_["sh_g"], 1)

            def sh_out(s, par):
                pe.wait_ge(s_["sh_act"], 4 * s + 4)
                if late(s, 2):
                    pe.wait_ge(s_["sh_y"], s - 1)
                for u in range(2):
                    for n in range(I // P):
                        ins = mm(two(bank[4 + par])[:, u, :], actt[par][:, n, u * P:(u + 1) * P], shd_s[:, n, :],
                                 start=(n == 0), stop=(n == I // P - 1))
                ins.then_inc(s_["sh_down"], 1)

            pe.wait_ge(s_["sh_w"], 48)
            sh_gate(0, 0, 0)
            sh_gate(1, 0, 1)
            pe.wait_ge(s_["route"], 5)
            hot = rt[0][:, :, :].rearrange("p t e -> p (t e)")
            mm(bank[6][:, 0:NT * E], strict, hot, start=True, stop=True)
            mm(bank[6][:, NT * E:2 * NT * E], ones, hot, start=True, stop=True).then_inc(s_["route_pe"], 1)
            sh_out(0, 0)
            sh_gate(2, 1, 0)
            sh_out(1, 1)
            with pe.Fori(1, NS // 2 - 1) as i:
                for par in range(2):
                    sh_gate(2 * i + par + 1, i + par, 1 - par)
                    sh_out(2 * i + par, par)
            sh_gate(NS - 1, NS // 2 - 1, 1)
            sh_out(NS - 2, 0)
            sh_out(NS - 1, 1)

            pe.wait_ge(s_["eid_done"], 1)
            pe.wait_ge(s_["ex_w"], 16 * 3 * E)

            def r_turn(t, i, par):
                pe.wait_ge(p_["rld"][par], 16 * (i + 1))
                if late(t, 2):
                    pe.wait_ge(s_["r_xt"], t - 1)
                for c in range(KC):
                    ins = nc.tensor.transpose(bank[6 + par][:, c * P:(c + 1) * P], xs_t[par][:, c * P:(c + 1) * P], ident)
                ins.then_inc(s_["r_t"], 1)

            def weights(t):
                return ew[:, bass.ds(pe.value_load(eid[0:1, bass.ds(t, 1)], min_val=0, max_val=E - 1), 1), :].rearrange("p a n -> p (a n)")

            def r_gu(t, par):
                g, up, _ = parts(weights(t))
                pe.wait_ge(s_["r_xt"], t + 1)
                if late(t, 2):
                    pe.wait_ge(s_["r_act"], t - 1)
                for a, w in enumerate((g, up)):
                    for c in range(KC):
                        ins = mm(bank[2 * par + a][:, :], xst[par][:, c, :], w[:, c, :], start=(c == 0), stop=(c == KC - 1))
                ins.then_inc(s_["r_gu"], 1)

            def r_at(t, par):
                pe.wait_ge(s_["r_act"], t + 1)
                if late(t, 1):
                    pe.wait_ge(s_["r_att"], t)
                for n in range(I // P):
                    ins = nc.tensor.transpose(bank[4][:, n * P:(n + 1) * P], act_r[par][:, n * P:(n + 1) * P], ident)
                ins.then_inc(s_["r_at"], 1)

            def r_dn(t, par):
                _, _, d = parts(weights(t))
                pe.wait_ge(s_["r_att"], t + 1)
                if late(t, 1):
                    pe.wait_ge(s_["r_y"], t)
                for n in range(I // P):
                    ins = mm(bank[5][:, 0:D], att_r[par][:, n, :], d[:, n, :], start=(n == 0), stop=(n == I // P - 1))
                ins.then_inc(s_["r_dn"], 1)

            r_turn(0, 0, 0)
            r_turn(1, 0, 1)
            r_gu(0, 0)
            for t in (2, 3):
                r_turn(t, 1, t % 2)
                r_at(t - 2, t % 2)
                r_gu(t - 1, 1 - t % 2)
                r_dn(t - 2, t % 2)
            with pe.Fori(2, (NRT - 1) // 2) as i:
                for par in range(2):
                    t = 2 * i + par
                    r_turn(t, i, par)
                    r_at(t - 2, par)
                    r_gu(t - 1, 1 - par)
                    r_dn(t - 2, par)
            t = NRT - 1
            r_turn(t, t // 2, t % 2)
            r_at(t - 2, t % 2)
            r_gu(t - 1, 1 - t % 2)
            r_dn(t - 2, t % 2)
            r_at(t - 1, 1 - t % 2)
            r_gu(t, t % 2)
            r_dn(t - 1, 1 - t % 2)
            r_at(t, t % 2)
            r_dn(t, t % 2)


_INS = ['L0_attn_inputs', 'L0_attn_ln1_scale', 'L0_attn_ln1_bias', 'L0_attn_wq', 'L0_attn_wk', 'L0_attn_wv', 'L0_attn_wo',
        'L0_attn_ln2_scale', 'L0_attn_ln2_bias', 'L0_attn_w1', 'L0_attn_b1', 'L0_attn_w2', 'L0_attn_b2', 'L0_ffn_gate_w',
        'L0_ffn_sh_gate', 'L0_ffn_sh_up', 'L0_ffn_sh_down', 'L0_ffn_rt_gate', 'L0_ffn_rt_up', 'L0_ffn_rt_down']


def _constants():
    import numpy as np
    c = np.zeros((P, C_N), np.float32)
    p = np.arange(P)
    c[:, C_ID:C_ID + P] = np.eye(P)
    c[:, C_CAUSAL:C_CAUSAL + P] = p[None, :] >= p[:, None]
    c[:, C_STRICT:C_STRICT + P] = p[:, None] < p[None, :]
    c[:, C_ONES:C_ONES + P] = 1
    c[:, C_BLOCK:C_BLOCK + 8 * VU] = np.arange(8 * VU)[None, :] // VU == p[:, None] // DH
    c[:, C_KEEP:C_KEEP + NS] = np.arange(NS) % STEPS_PER_BATCH != STEPS_PER_BATCH - 1
    c[:, C_EREV:C_EREV + E] = E - np.arange(E)
    c[:, C_TILE:] = np.arange(NRT * (E - 1)) // (E - 1)
    return c


def kernel(**inputs):
    import numpy as _np
    import concourse.bacc as _bacc
    from concourse.bass_utils import run_bass_kernel_spmd as _run

    nc = _bacc.Bacc("TRN2", target_bir_lowering=False, num_devices=1)
    arrays, args = {}, []
    for name in _INS:
        a = _np.ascontiguousarray(inputs[name])
        arrays[f"in_{name}"] = a
        args.append(nc.dram_tensor(f"in_{name}", a.shape, F32, kind="ExternalInput").ap())
    arrays["in_constants"] = _constants()
    args.append(nc.dram_tensor("in_constants", (P, C_N), F32, kind="ExternalInput").ap())
    for name, shape in (("h", (TOK, D)), ("xn2", (TOK, D)), ("xt", (NS, P, KC * STEP)), ("xs", (NRT * P, D)),
                        ("ysh", (TOK, D)), ("yr", (NRT * P, D))):
        args.append(nc.dram_tensor("scratch_" + name, shape, F32, kind="Internal").ap())
    args.append(nc.dram_tensor("out_0", (B, S, D), F32, kind="ExternalOutput").ap())
    build(nc, *args)
    r = _run(nc, [arrays], core_ids=[0])
    return r.results[0]["out_0"]
```

```python
from contextlib import ExitStack

import concourse.bass as bass
from concourse import mybir

ALU = mybir.AluOpType
ACT = mybir.ActivationFunctionType
AX = mybir.AxisListType
F32 = mybir.dt.float32
I32 = mybir.dt.int32
U32 = mybir.dt.uint32

P = 128
B, S, D = 4, 1024, 256
H, DH, MLP = 16, 16, 1024
E, I = 8, 512
KC = D // P
TOK = B * S
STEP = 256
NS = TOK // STEP
NT = TOK // P
NA = NS // 2
STEPS_PER_BATCH = S // STEP
VW = 32
VU = DH + 1
G = 4
NRT = NT + E - 1
EW = 2 * KC * I + (I // P) * D
EPS_OUTER, EPS_INNER, KERNEL_EPS = 1e-5, 1e-6, 1e-3

C_ID, C_CAUSAL, C_STRICT, C_ONES = 0, P, 2 * P, 3 * P
C_BLOCK = 4 * P
C_KEEP = C_BLOCK + 8 * VU
C_EREV = C_KEEP + NS
C_TILE = C_EREV + E
C_N = C_TILE + NRT * (E - 1)


def late(k, n):
    return not isinstance(k, int) or k >= n


def hold(eng, sem, value):
    eng.wait_ge(sem, value)
    eng.nop(nofuse=True)


class Chain:

    def __init__(self, eng, sem, per, rnd):
        self.eng, self.sem, self.base, self.n = eng, sem, rnd * per, 0

    def did(self, ins):
        self.n += 1
        ins.then_inc(self.sem, 1)

    def settle(self):
        self.eng.wait_ge(self.sem, self.base + self.n)


def build(nc, x, ln1s, ln1b, wq, wk, wv, wo, ln2s, ln2b, w1, b1, w2, b2, gw, shg, shu, shd, rtg, rtu, rtd, cst,
          h_d, xn_d, xt_d, xs_d, ysh_d, yr_d, out):
    with ExitStack() as ctx:
        def sb(name, shape, dt=F32):
            return ctx.enter_context(nc.sbuf_tensor(name, shape, dt))

        def sem(name):
            return ctx.enter_context(nc.semaphore(name))

        ew = sb("ew", [P, E, EW])
        first = ew[:, E - 2:E, :].rearrange("p e n -> p (e n)")
        wqkv_s = first[:, 0:KC * 3 * D].rearrange("p (c n) -> p c n", c=KC)
        o = KC * 3 * D
        wo_s = first[:, o:o + KC * D].rearrange("p (c n) -> p c n", c=KC)
        o += KC * D
        w1_s = first[:, o:o + KC * MLP].rearrange("p (c n) -> p c n", c=KC)
        o += KC * MLP
        w2_s = first[:, o:o + (MLP // P) * D].rearrange("p (c n) -> p c n", c=MLP // P)
        shw = sb("shw", [P, EW])

        def parts(w):
            return (w[:, 0:KC * I].rearrange("p (c n) -> p c n", c=KC),
                    w[:, KC * I:2 * KC * I].rearrange("p (c n) -> p c n", c=KC),
                    w[:, 2 * KC * I:EW].rearrange("p (c n) -> p c n", c=I // P))

        shg_s, shu_s, shd_s = parts(shw)
        gw_s = sb("gw_s", [P, KC, E])
        cols = sb("cols", [P, 4 * KC + MLP // P])
        ln1s_c, ln1b_c, ln2s_c, ln2b_c = (cols[:, i * KC:(i + 1) * KC] for i in range(4))
        b1_c = cols[:, 4 * KC:]
        b2_s = sb("b2_s", [P, D])
        cs = sb("cs", [P, C_TILE])
        ident = cs[:, C_ID:C_ID + P]
        causal = cs[:, C_CAUSAL:C_CAUSAL + P]
        strict = cs[:, C_STRICT:C_STRICT + P]
        ones = cs[:, C_ONES:C_ONES + P]
        block_mask = cs[:, C_BLOCK:C_BLOCK + 8 * VU].rearrange("p (h n) -> p h n", h=8)
        erev = cs[:, C_EREV:C_EREV + E]
        half = sb("half", [P, 2])
        eps_o = sb("eps_o", [P, 2])
        eps_i = sb("eps_i", [P, 2])

        xin = [sb(f"xin{i}", [P, 2, D]) for i in range(2)]
        xr = sb("xr", [P, 2, D])
        xn = [sb(f"xn{i}", [P, 2, D]) for i in range(2)]
        z = sb("z", [P, 2, D])
        x1t = sb("x1t", [P, KC, STEP])
        qt = sb("qt", [P, 2, STEP])
        kk = sb("kk", [P, 2, D])
        vx = sb("vx", [P, 2, H, VW])
        kt = sb("kt", [P, 2, STEP])
        qx = sb("qx", [P, 2, 2, 8, P])
        st = [sb(f"st{i}", [P, G, P]) for i in range(4)]
        sx = [sb(f"sx{i}", [P, 2, 8, VW]) for i in range(2)]
        su = sb("su", [P, 2, 8, VU])
        ot = [sb(f"ot{i}", [P, 4, P]) for i in range(2)]
        rden = sb("rden", [P, H])
        at = sb("at", [P, 2, D])
        att = sb("att", [P, KC, STEP])
        x2 = sb("x2", [P, 2, D])
        x2b = [sb(f"x2b{i}", [P, 2, D]) for i in range(2)]
        z2 = sb("z2", [P, 2, D])
        y2t = sb("y2t", [P, KC, STEP])
        ht = sb("ht", [P, MLP // P, STEP])
        x3 = sb("x3", [P, 2, D])
        hh = [sb(f"hh{i}", [P, 2, D]) for i in range(2)]
        zrow = hh[0][:, 0, :]
        xm = [sb(f"xm{i}", [P, 2, D]) for i in range(2)]
        x3t = [sb(f"x3t{i}", [P, KC, STEP]) for i in range(2)]
        lns = {n: (sb("bs_" + n, [P, 2, 6]), sb("mv_" + n, [P, 2, 2]), sb("ve_" + n, [P, 2]), sb("rs_" + n, [P, 2]))
               for n in ("x", "n", "a", "y", "h")}
        logit = sb("logit", [P, NT, E])
        lt = att[0:E, 0, :]

        top = sb("top", [P, NT])
        rt = [x2b[i // 2][:, i % 2, :].rearrange("p (t e) -> p t e", t=NT) for i in range(4)]
        rm = sb("rm", [P, NT])
        score = sb("score", [P, NT])
        cnt = [sb(f"cnt{i}", [P, E]) for i in range(4)]
        cnt_i = sb("cnt_i", [P, E], I32)
        slot = sb("slot", [P, NT], U32)
        tcmp = x2[0:1, :, :].rearrange("p a n -> p (a n)")[:, 0:NRT * (E - 1)].rearrange("p (t e) -> p t e", t=NRT)
        tnum = z2[0:1, :, :].rearrange("p a n -> p (a n)")[:, 0:NRT * (E - 1)].rearrange("p (t e) -> p t e", t=NRT)
        eid_f = sb("eid_f", [1, NRT])
        eid = sb("eid", [1, NRT], I32)
        idx = [sb(f"idx{i}", [P, 2], U32) for i in range(2)]

        bank = [ctx.enter_context(nc.psum_tensor(f"bank{i}", [P, 512], F32)) for i in range(8)]
        R0, R1, R2, S0, S1, X, Y, U = bank

        def two(b):
            return b[:, :].rearrange("p (a n) -> p a n", a=2)

        names = ("w_load zeroed sh_w c_load x1t_done qt_done kk_done vx_done kt_done expanded masks o_done "
                 "norm att_done y2t_done gelu x3t_done logit_done lt_done pe_lt state pe_zt pe_q pe_k pe_v pe_y2t pe_kt pe_w1 pe_x3t pe_log pe_u pe_sc pe_av "
                 "pe_otr pe_att pe_wo pe_w2 lnx lnn lna lny rs_x rs_n rs_a rs_y rs_h x2b_done "
                 "xr_ld pool_c small_c route tnum_ld eid_done route_pe route_act sh_g sh_silu sh_act sh_down sh_y "
                 "r_t r_xt r_gu r_silu r_act r_at r_att r_dn r_y ex_w fin_pool sc_sc ysh_ld").split()
        s_ = {n: sem(n) for n in names}
        par_names = "xin_ld h_s xm_s xt_s sld yst rld rst gat fld fst xsl idx_c sct fsum fout frs".split()
        p_ = {n: [sem(f"{n}{i}") for i in range(2)] for n in par_names}

        xv = x.rearrange("b (s u p) d -> (b s) p u d", u=2, p=P)
        outv = out.rearrange("b (s u p) d -> (b s) p u d", u=2, p=P)
        hv = h_d.rearrange("(s u p) d -> s p u d", u=2, p=P)
        xnv = xn_d.rearrange("(s u p) d -> s p u d", u=2, p=P)
        yshv = ysh_d.rearrange("(s u p) d -> s p u d", u=2, p=P)
        xsv = xs_d.rearrange("(t p) d -> t p d", p=P)
        yrv = yr_d.rearrange("(t p) d -> t p d", p=P)

        C_LOADS, W_LOADS = 6, 8

        def pick(v, k):
            return v[bass.ds(k, 1)].rearrange("a p u d -> p (a u) d")

        def pick3(v, k):
            return v[bass.ds(k, 1)].rearrange("a p d -> p (a d)")

        ysh = [xin[0], xin[1]]
        sg = [z, x1t, qt, kk]
        actt = [ht[:, 0:4, :], ht[:, 4:8, :]]
        xs_t = [att[:, 0, :], att[:, 1, :]]
        xst = [y2t[:, :, 0:P], y2t[:, :, P:2 * P]]
        sgr = [x3[:, :, :].rearrange("p a n -> p (a n)"), z2[:, :, :].rearrange("p a n -> p (a n)")]
        act_r = [st[0][:, :, :].rearrange("p a n -> p (a n)"), st[1][:, :, :].rearrange("p a n -> p (a n)")]
        att_r = [st[2], st[3]]
        y_r = [ot[0][:, 0:2, :].rearrange("p a n -> p (a n)"), ot[1][:, 0:2, :].rearrange("p a n -> p (a n)")]

        block = ctx.enter_context(nc.Block())

        @block.sync
        def _(sp):
            def load_x(k, par, i):
                sp.dma_start(xin[par][:, :, :], pick(xv, k)).then_inc(p_["xin_ld"][par], 16)

            load_x(0, 0, 0)
            sp.dma_start(cs[:, :], cst[:, 0:C_TILE]).then_inc(s_["c_load"], 16)
            for src, dst in ((ln1s, ln1s_c), (ln1b, ln1b_c)):
                with nc.allow_non_contiguous_dma(reason="a vector into a column per chunk"):
                    sp.dma_start(dst, src.rearrange("(c p) -> p c", p=P)).then_inc(s_["c_load"], 16)
            for i, w in enumerate((wq, wk, wv)):
                sp.dma_start(wqkv_s[:, :, i * D:(i + 1) * D],
                             w.rearrange("(c p) h m -> p c (h m)", p=P)).then_inc(s_["c_load"], 16)
            load_x(1, 1, 0)
            sp.dma_start(wo_s, wo.rearrange("h m d -> (h m) d").rearrange("(c p) d -> p c d", p=P)).then_inc(s_["w_load"], 16)
            for src, dst in ((ln2s, ln2s_c), (ln2b, ln2b_c), (b1, b1_c)):
                with nc.allow_non_contiguous_dma(reason="a vector into a column per chunk"):
                    sp.dma_start(dst, src.rearrange("(c p) -> p c", p=P)).then_inc(s_["w_load"], 16)
            sp.dma_start(b2_s[:, :], b2.rearrange("(a d) -> a d", a=1).to_broadcast([P, D])).then_inc(s_["w_load"], 16)

            def later_weights():
                sp.dma_start(w1_s, w1.rearrange("(c p) n -> p c n", p=P)).then_inc(s_["w_load"], 16)
                sp.dma_start(w2_s, w2.rearrange("(c p) n -> p c n", p=P)).then_inc(s_["w_load"], 16)
                sp.dma_start(gw_s[:, :, :], gw.rearrange("(c p) n -> p c n", p=P)).then_inc(s_["w_load"], 16)

            def zero_rows(j):
                n = NRT // 3
                sp.dma_start(xs_d[j * n * P:(j + 1) * n * P, :].rearrange("(t p) d -> p t d", p=P),
                             zrow.rearrange("p (a d) -> p a d", a=1).to_broadcast([P, n, D])).then_inc(s_["zeroed"], 16)

            def shared_load():
                for w, dst in ((shg, shg_s), (shu, shu_s), (shd, shd_s)):
                    sp.dma_start(dst, w.rearrange("(c p) n -> p c n", p=P)).then_inc(s_["sh_w"], 16)

            def expert_load(e):
                dst = ew[:, bass.ds(e, 1), :].rearrange("p a n -> p (a n)")
                for d, w in zip(parts(dst), (rtg, rtu, rtd)):
                    sp.dma_start(d, w[bass.ds(e, 1)].rearrange("a (c p) n -> p (a c) n", p=P)).then_inc(s_["ex_w"], 16)

            def step(k, i, par, f, m, b, ahead):
                if f:
                    hold(sp, s_["qt_done"], k + 1)
                    if late(k, 1):
                        sp.wait_ge(s_["pe_sc"], 8 * k)
                    for g in range(2):
                        for h in range(8):
                            r = slice(h * DH, (h + 1) * DH)
                            sp.dma_start(qx[r, g, :, h, :],
                                         qt[r, g, :].rearrange("p (u n) -> p u n", u=2)).then_inc(s_["expanded"], 16)
                if ahead:
                    hold(sp, s_["lnx"], 6 * (k + 1))
                    sp.dma_start(xin[par][:, :, :], pick(xv, k + 2)).then_inc(p_["xin_ld"][par], 16)
                if b:
                    hold(sp, s_["lny"], 14 * (k - 1))
                    sp.dma_start(pick(hv, k - 2), hh[par][:, :, :]).then_inc(p_["h_s"][par], 16)
                    sp.dma_start(pick(xnv, k - 2), xm[par][:, :, :]).then_inc(p_["xm_s"][par], 16)
                if m:
                    sp.dma_start(xr[:, :, :], pick(xv, k - 1)).then_inc(s_["xr_ld"], 16)
                if b:
                    hold(sp, s_["x3t_done"], k - 1)
                    sp.dma_start(xt_d[bass.ds(k - 2, 1)].rearrange("a p n -> p (a n)"),
                                 x3t[par][:, :, :].rearrange("p a n -> p (a n)")).then_inc(p_["xt_s"][par], 16)

            sp.wait_ge(s_["pool_c"], 5)
            sp.wait_ge(s_["zeroed"], 1)
            for k in range(4):
                step(k, k // 2, k % 2, True, k >= 1, k >= 2, True)
                if k == 0:
                    later_weights()
                if k <= 1:
                    zero_rows(k)
                if k == 1:
                    zero_rows(2)
                if k == 2:
                    shared_load()
                if k == 3:
                    expert_load(E - 3)
            with sp.Fori(2, NS // 2 - 1) as i:
                for par in range(2):
                    step(2 * i + par, i, par, True, True, True, True)
                expert_load(i - 2)
            for k in range(NS - 2, NS):
                step(k, k // 2, k % 2, True, True, True, False)
            step(NS, NS // 2, 0, False, True, True, False)
            step(NS + 1, NS // 2, 1, False, False, True, False)

            sp.wait_ge(s_["pe_y2t"], NS)
            sp.dma_start(tnum, cst[0:1, C_TILE:C_N].rearrange("p (t e) -> p t e", t=NRT)).then_inc(s_["tnum_ld"], 16)


            def sh_load(s, par):
                sp.dma_start(x3t[par][:, :, :].rearrange("p a n -> p (a n)"),
                             xt_d[bass.ds(s, 1)].rearrange("a p n -> p (a n)")).then_inc(p_["sld"][par], 16)

            def row_load(s, par):
                sp.dma_start(xn[par][:, :, :], pick(xnv, s)).then_inc(p_["xsl"][par], 16)

            def sh_store(s, par):
                hold(sp, s_["sh_y"], s + 1)
                sp.dma_start(pick(yshv, s), ysh[par][:, :, :]).then_inc(p_["yst"][par], 16)

            sp.wait_ge(s_["pe_log"], NS)
            for par in range(2):
                sp.wait_ge(p_["xt_s"][par], 16 * (NS // 2))
                sh_load(par, par)
            for par in range(2):
                sp.wait_ge(p_["xm_s"][par], 16 * (NS // 2))
                sp.wait_ge(p_["h_s"][par], 16 * (NS // 2))
                row_load(par, par)
            sp.wait_ge(s_["pe_w2"], NS)
            for e in range(E - 2, E):
                expert_load(e)

            def sh_step(s, i, par, rows):
                hold(sp, s_["sh_g"], 4 * (s + 1))
                sh_load(s + 2, par)
                for v in range(2):
                    if rows:
                        hold(sp, s_["sc_sc"], 4 * (2 * s + v + 1))
                        row_load(2 * s + v + 2, v)
                sh_store(s, par)

            with sp.Fori(0, NA // 2 - 1) as i:
                for par in range(2):
                    sh_step(2 * i + par, i, par, True)
            sh_step(NA - 2, NA // 2 - 1, 0, True)
            sh_step(NA - 1, NA // 2 - 1, 1, False)

            for par in range(2):
                sp.wait_ge(p_["sct"][par], 16 * NT // 2)

            def r_load(t, par):
                sp.dma_start(xs_t[par], pick3(xsv, t)).then_inc(p_["rld"][par], 16)

            def r_store(t, par):
                hold(sp, s_["r_y"], t + 1)
                sp.dma_start(pick3(yrv, t), y_r[par]).then_inc(p_["rst"][par], 16)

            def r_next(t, par):
                hold(sp, s_["r_t"], t - 1)
                r_load(t, par)

            r_load(0, 0)
            r_load(1, 1)
            for t in (2, 3):
                r_next(t, t % 2)
            with sp.Fori(2, (NRT - 1) // 2) as i:
                for par in range(2):
                    r_next(2 * i + par, par)
                    r_store(2 * i + par - 4, par)
            r_next(NRT - 1, 0)
            for t in range(NRT - 5, NRT):
                r_store(t, t % 2)
            sp.wait_ge(p_["rst"][0], 16 * ((NRT + 1) // 2))
            sp.wait_ge(p_["rst"][1], 16 * (NRT // 2))
            sp.sem_inc(s_["fin_pool"], 1)

            def half_of(v, j):
                return j + v * NA

            def ysh_load(j):
                sp.dma_start(xin[0][:, :, :], pick(yshv, j)).then_inc(s_["ysh_ld"], 16)

            def h_load(v, j):
                sp.dma_start(hh[v][:, :, :], pick(hv, half_of(v, j))).then_inc(p_["fld"][v], 16)

            def finish(v, j, more):
                hold(sp, p_["fout"][v], 3 * (j + 1))
                sp.dma_start(pick(outv, half_of(v, j)), xm[v][:, :, :]).then_inc(p_["fst"][v], 16)
                if more:
                    h_load(v, j + 1)

            def last_step(j, par, load, more):
                if load:
                    hold(sp, s_["sh_g"], 4 * (NA + j + 1))
                    sh_load(NA + j + 2, par)
                if more:
                    hold(sp, p_["fsum"][0], 5 * j + 1)
                    ysh_load(j + 1)
                if late(j, 1):
                    finish(1, j - 1, True)
                finish(0, j, more)

            for par in range(2):
                sp.wait_ge(p_["yst"][par], 16 * (NA // 2))
            ysh_load(0)
            for v in range(2):
                h_load(v, 0)
            last_step(0, 0, True, True)
            last_step(1, 1, True, True)
            with sp.Fori(1, NA // 2 - 1) as i:
                for par in range(2):
                    last_step(2 * i + par, par, True, True)
            last_step(NA - 2, 0, False, True)
            last_step(NA - 1, 1, False, False)
            finish(1, NA - 1, False)
            for v in range(2):
                sp.wait_ge(p_["fst"][v], 16 * NA)

        @block.gpsimd
        def _(pool):
            nc.gpsimd.memset(zrow, 0.0).then_inc(s_["zeroed"], 1)
            nc.gpsimd.memset(half[:, :], -0.5).then_inc(s_["small_c"], 1)
            nc.gpsimd.memset(eps_o[:, :], EPS_OUTER).then_inc(s_["small_c"], 1)
            nc.gpsimd.memset(eps_i[:, :], EPS_INNER).then_inc(s_["small_c"], 1)
            nc.gpsimd.memset(vx[:, :, :, :], 0.0).then_inc(s_["pool_c"], 1)
            nc.gpsimd.memset(sx[0][:, :, :, :], 0.0).then_inc(s_["pool_c"], 1)
            nc.gpsimd.memset(sx[1][:, :, :, :], 0.0).then_inc(s_["pool_c"], 1)
            pool.wait_ge(s_["small_c"], 3)
            pool.wait_ge(s_["pool_c"], 1)
            nc.gpsimd.memset(vx[:, :, :, DH:DH + 1], 1.0).then_inc(s_["pool_c"], 1)

            def rsqrt(which, eps, stats, n, rs, rnd):
                _, mv, ve, r = lns[which]
                pool.wait_ge(stats, n)
                nc.gpsimd.tensor_tensor(ve[:, :], mv[:, :, 1], eps[:, :], ALU.add).then_inc(rs, 1)
                pool.wait_ge(rs, 2 * rnd + 1)
                nc.gpsimd.tensor_tensor(r[:, :], ve[:, :], half[:, :], ALU.pow).then_inc(rs, 1)

            def step(k, par, f, b, ahead):
                if ahead:
                    rsqrt("x", eps_o, s_["lnx"], 6 * (k + 1) + 4, s_["rs_x"], k + 1)
                if b:
                    rsqrt("y", eps_o, s_["lny"], 14 * (k - 2) + 5, s_["rs_y"], k - 2)
                if ahead:
                    rsqrt("n", eps_i, s_["lnn"], 6 * (k + 1) + 4, s_["rs_n"], k + 1)
                if b:
                    rsqrt("h", eps_o, s_["lny"], 14 * (k - 2) + 12, s_["rs_h"], k - 2)
                if f:
                    rsqrt("a", eps_i, s_["lna"], 7 * k + 5, s_["rs_a"], k)
                    if late(k, 2):
                        pool.wait_ge(s_["lny"], 14 * (k - 2) + 1)
                    if not late(k, 1):
                        pool.wait_ge(s_["w_load"], 16 * W_LOADS)
                    nc.gpsimd.tensor_tensor(x2b[par][:, :, :], x2[:, :, :],
                                            b2_s[:, :].rearrange("p (a d) -> p a d", a=1).to_broadcast([P, 2, D]),
                                            ALU.add).then_inc(s_["x2b_done"], 1)

            rsqrt("x", eps_o, s_["lnx"], 4, s_["rs_x"], 0)
            rsqrt("n", eps_i, s_["lnn"], 4, s_["rs_n"], 0)
            nc.gpsimd.memset(qx[:, :, :, :, :], 0.0).then_inc(s_["pool_c"], 1)
            for k in range(4):
                step(k, k % 2, True, k >= 2, True)
            with pool.Fori(2, NS // 2 - 1) as i:
                for par in range(2):
                    step(2 * i + par, par, True, True, True)
            for k in range(NS - 2, NS):
                step(k, k % 2, True, True, k + 1 < NS)
            step(NS, 0, False, True, False)
            step(NS + 1, 1, False, True, False)

            pool.wait_ge(s_["zeroed"], 49)
            with pool.Fori(0, NS // 2) as i:
                for par in range(2):
                    hold(pool, s_["sc_sc"], 4 * (2 * i + par + 1))
                    for u in range(2):
                        nc.gpsimd.indirect_dma_start(
                            out=xs_d, out_offset=bass.IndirectOffsetOnAxis(ap=idx[par][:, u:u + 1], axis=0),
                            in_=xm[par][:, u, :], in_offset=None).then_inc(p_["sct"][par], 16)

            def gather(i, par):
                hold(pool, p_["idx_c"][par], i + 1)
                for u in range(2):
                    nc.gpsimd.indirect_dma_start(
                        out=xn[par][:, u, :], out_offset=None, in_=yr_d,
                        in_offset=bass.IndirectOffsetOnAxis(ap=idx[par][:, u:u + 1], axis=0)).then_inc(p_["gat"][par], 16)

            def fin_rsqrt(v, j):
                rsqrt("xn"[v], eps_o, p_["fsum"][v], 5 * j + 5, p_["frs"][v], j)

            pool.wait_ge(s_["fin_pool"], 1)
            gather(0, 0)
            gather(0, 1)
            fin_rsqrt(0, 0)
            gather(1, 0)
            with pool.Fori(1, NA - 1) as j:
                fin_rsqrt(0, j)
                gather(j + 1, 0)
                fin_rsqrt(1, j - 1)
                gather(j, 1)
            fin_rsqrt(0, NA - 1)
            fin_rsqrt(1, NA - 2)
            gather(NA - 1, 1)
            fin_rsqrt(1, NA - 1)

        @block.scalar
        def _(act):
            def step(k, i, par, f, m, b):
                if f:
                    act.wait_ge(s_["pe_zt"], k + 1)
                    if late(k, 1):
                        act.wait_ge(s_["pe_v"], k)
                    for c in range(KC):
                        ins = nc.scalar.activation(x1t[:, c, :], two(R0)[:, c, :], ACT.Identity,
                                                   bias=ln1b_c[:, c:c + 1], scale=ln1s_c[:, c:c + 1])
                    ins.then_inc(s_["x1t_done"], 1)
                    act.wait_ge(s_["pe_v"], k + 1)
                    if late(k, 1):
                        act.wait_ge(s_["pe_av"], 8 * k)
                        act.wait_ge(s_["pe_u"], 2 * k)
                    nc.scalar.activation(vx[:, :, :, 0:DH], R0[:, :].rearrange("p (u h m) -> p u h m", u=2, h=H),
                                         ACT.Copy).then_inc(s_["vx_done"], 1)
                if m:
                    if not late(k, 2):
                        act.wait_ge(s_["w_load"], 16 * W_LOADS)
                    act.wait_ge(s_["pe_y2t"], k)
                    if late(k, 2):
                        act.wait_ge(s_["pe_w1"], 4 * (k - 1))
                    for c in range(KC):
                        ins = nc.scalar.activation(y2t[:, c, :], two(R1)[:, c, :], ACT.Identity,
                                                   bias=ln2b_c[:, c:c + 1], scale=ln2s_c[:, c:c + 1])
                    ins.then_inc(s_["y2t_done"], 1)
                if f:
                    act.wait_ge(s_["pe_kt"], k + 1)
                    if late(k, 1):
                        act.wait_ge(s_["pe_sc"], 8 * k)
                    nc.scalar.activation(kt[:, :, :], two(R2), ACT.Copy).then_inc(s_["kt_done"], 1)
                if m:
                    if late(k, 2):
                        act.wait_ge(s_["pe_w2"], k - 1)
                    for j in range(4):
                        act.wait_ge(s_["pe_w1"], 4 * (k - 1) + j + 1)
                        for c in range(2):
                            n = 2 * j + c
                            ins = nc.scalar.activation(ht[:, n, :], two((R0, R1, R2, R0)[j])[:, c, :],
                                                       ACT.Gelu_apprx_tanh, bias=b1_c[:, n:n + 1])
                        ins.then_inc(s_["gelu"], 1)
                if b:
                    act.wait_ge(s_["pe_x3t"], k - 2 + 1)
                    if late(k, 4):
                        act.wait_ge(p_["xt_s"][par], 16 * (i - 1))
                        act.wait_ge(s_["pe_log"], k - 3)
                    nc.scalar.activation(x3t[par][:, :, :], two(R1), ACT.Copy).then_inc(s_["x3t_done"], 1)
                if f:
                    for u in range(2):
                        act.wait_ge(s_["pe_av"], 8 * k + 4 * (u + 1))
                        if late(k, 1):
                            act.wait_ge(s_["pe_otr"], 2 * k)
                        nc.scalar.activation(ot[u][:, :, :].rearrange("p a n -> p (a n)"), (X, Y)[u][:, :],
                                             ACT.Copy).then_inc(s_["o_done"], 1)
                    act.wait_ge(s_["pe_att"], k + 1)
                    if late(k, 1):
                        act.wait_ge(s_["pe_wo"], k)
                    nc.scalar.activation(att[:, :, :], two(R1), ACT.Copy).then_inc(s_["att_done"], 1)

            act.wait_ge(s_["c_load"], 16 * C_LOADS)
            act.wait_ge(s_["pool_c"], 4)
            for k in range(4):
                step(k, k // 2, k % 2, True, k >= 1, k >= 2)
            with act.Fori(2, NS // 2) as i:
                for par in range(2):
                    step(2 * i + par, i, par, True, True, True)
            step(NS, NS // 2, 0, False, True, True)
            step(NS + 1, NS // 2, 1, False, False, True)

            act.wait_ge(s_["route"], 1)
            nc.scalar.activation(score[:, :], top[:, :], ACT.Sigmoid).then_inc(s_["route_act"], 1)

            def sh_up(s):
                for j in range(4):
                    act.wait_ge(s_["sh_g"], 4 * s + j + 1)
                    if late(s, 1):
                        act.wait_ge(s_["sh_act"], 4 * s - 4 + j + 1)
                    nc.scalar.activation(sg[j][:, 0, :], two(bank[j])[:, 0, :], ACT.Silu).then_inc(s_["sh_silu"], 1)

            def sh_down(s, i, par):
                act.wait_ge(s_["sh_down"], s + 1)
                if late(i, 1):
                    act.wait_ge(p_["yst"][par], 16 * i)
                nc.scalar.activation(ysh[par][:, :, :], two(bank[4 + par]), ACT.Copy).then_inc(s_["sh_y"], 1)

            sh_up(0)
            sh_up(1)
            sh_down(0, 0, 0)
            sh_up(2)
            sh_down(1, 0, 1)
            with act.Fori(1, NA // 2 - 1) as i:
                for par in range(2):
                    sh_up(2 * i + par + 1)
                    sh_down(2 * i + par, i, par)
            sh_up(NA - 1)
            sh_down(NA - 2, NA // 2 - 1, 0)
            sh_down(NA - 1, NA // 2 - 1, 1)

            def r_xt(t, par):
                act.wait_ge(s_["r_t"], t + 1)
                if late(t, 2):
                    act.wait_ge(s_["r_gu"], t - 1)
                nc.scalar.activation(xst[par], bank[6 + par][:, 0:2 * P].rearrange("p (c n) -> p c n", c=KC),
                                     ACT.Copy).then_inc(s_["r_xt"], 1)

            def r_silu(t, par):
                act.wait_ge(s_["r_gu"], t + 1)
                if late(t, 2):
                    act.wait_ge(s_["r_act"], t - 1)
                nc.scalar.activation(sgr[par], bank[par * 2][:, :], ACT.Silu).then_inc(s_["r_silu"], 1)

            def r_y(t, i, par):
                act.wait_ge(s_["r_dn"], t + 1)
                if late(i, 1):
                    act.wait_ge(p_["rst"][par], 16 * i)
                nc.scalar.activation(y_r[par], bank[5][:, 0:D], ACT.Copy).then_inc(s_["r_y"], 1)

            r_xt(0, 0)
            r_xt(1, 1)
            r_silu(0, 0)
            with act.Fori(1, (NRT - 1) // 2) as i:
                for par in range(2):
                    r_xt(2 * i + par, par)
                    r_silu(2 * i + par - 1, 1 - par)
                    r_y(2 * i + par - 2, i - 1, par)
            r_xt(NRT - 1, 0)
            r_silu(NRT - 2, 1)
            r_y(NRT - 3, NRT // 2 - 1, 0)
            r_silu(NRT - 1, 0)
            r_y(NRT - 2, NRT // 2 - 1, 1)
            r_y(NRT - 1, NRT // 2, 0)

            with act.Fori(NA, NS) as s:
                sh_up(s)

        @block.vector
        def _(dve):
            def stats(c, which, src):
                bs, mv, _, _ = lns[which]
                for u in range(2):
                    c.did(nc.vector.bn_stats(bs[:, u, :], src[:, u, :]))
                hold(dve, c.sem, c.base + c.n)
                for u in range(2):
                    c.did(nc.vector.bn_aggr(mv[:, u, :], bs[:, u, :]))

            def normalise(c, which, dst, src):
                _, mv, _, r = lns[which]
                for u in range(2):
                    c.did(nc.vector.tensor_scalar(dst[:, u, :], src[:, u, :], mv[:, u, 0:1], r[:, u:u + 1],
                                                  ALU.subtract, ALU.mult))

            def in_stats(k, i, par):
                c = Chain(dve, s_["lnx"], 6, k)
                dve.wait_ge(p_["xin_ld"][par], 16 * (i + 1))
                if late(k, 1):
                    dve.wait_ge(s_["rs_x"], 2 * k)
                stats(c, "x", xin[par])
                return c

            def in_norm(c, k, par):
                dve.wait_ge(s_["rs_x"], 2 * k + 2)
                if late(k, 2):
                    dve.wait_ge(s_["lna"], 7 * (k - 2) + 1)
                normalise(c, "x", xn[par], xin[par])
                c.settle()
                c = Chain(dve, s_["lnn"], 6, k)
                if late(k, 1):
                    dve.wait_ge(s_["rs_n"], 2 * k)
                stats(c, "n", xn[par])
                return c

            def in_z(c, k, par):
                dve.wait_ge(s_["rs_n"], 2 * k + 2)
                if late(k, 1):
                    dve.wait_ge(s_["pe_zt"], k)
                normalise(c, "n", z, xn[par])

            def end_x3(k, par):
                c = Chain(dve, s_["lny"], 14, k)
                dve.wait_ge(s_["pe_w2"], k + 1)
                dve.wait_ge(s_["x2b_done"], k + 1)
                if late(k, 1):
                    dve.wait_ge(s_["rs_y"], 2 * k)
                c.did(nc.vector.tensor_tensor(x3[:, :, :], two(X), x2b[par][:, :, :], ALU.add))
                c.settle()
                stats(c, "y", x3)
                return c

            def end_h(c, k, i, par):
                dve.wait_ge(s_["rs_y"], 2 * k + 2)
                normalise(c, "y", x3, x3)
                c.settle()
                dve.wait_ge(s_["xr_ld"], 16 * (k + 1))
                if not late(k, 1):
                    dve.wait_ge(s_["zeroed"], 49)
                if late(k, 2):
                    dve.wait_ge(p_["h_s"][par], 16 * i)
                    dve.wait_ge(s_["rs_h"], 2 * k)
                c.did(nc.vector.tensor_tensor(hh[par][:, :, :], x3[:, :, :], xr[:, :, :], ALU.add))
                c.settle()
                stats(c, "h", hh[par])

            def end_xm(c, k, i, par):
                dve.wait_ge(s_["rs_h"], 2 * k + 2)
                if late(k, 2):
                    dve.wait_ge(p_["xm_s"][par], 16 * i)
                    dve.wait_ge(s_["pe_x3t"], k - 1)
                normalise(c, "h", xm[par], hh[par])

            def state(k, u):
                c = Chain(dve, s_["state"], 2, 2 * k + u)
                dve.wait_ge(s_["pe_u"], 2 * k + u + 1)
                c.did(nc.vector.tensor_tensor(su[:, :, :, :], sx[u][:, :, :, 0:VU],
                                              U[:, 0:2 * 8 * VU].rearrange("p (g h n) -> p g h n", g=2, h=8), ALU.add))
                c.settle()
                if late(k, 1) or u:
                    dve.wait_ge(s_["pe_av"], 8 * k + 4 * u)
                for g in range(2):
                    dst = sx[1 - u][:, g, :, 0:VU]
                    if u:
                        ins = nc.vector.scalar_tensor_tensor(out=dst, in0=su[:, g, :, :],
                                                             scalar=cs[:, bass.ds(C_KEEP + k, 1)], in1=block_mask,
                                                             op0=ALU.mult, op1=ALU.mult)
                    else:
                        ins = nc.vector.tensor_tensor(dst, su[:, g, :, :], block_mask, ALU.mult)
                c.did(ins)

            def mask(k, j):
                dve.wait_ge(s_["pe_sc"], 8 * k + j + 1)
                if late(k, 1) or j >= 4:
                    dve.wait_ge(s_["pe_av"], 8 * k + j - 3)
                nc.vector.tensor_tensor(st[j % 4][:, :, :], (S0, S1)[j % 2][:, :].rearrange("p (h n) -> p h n", h=G),
                                        causal.rearrange("p (a n) -> p a n", a=1).to_broadcast([P, G, P]),
                                        ALU.mult).then_inc(s_["masks"], 1)

            def norm(k, u):
                c = Chain(dve, s_["norm"], 2, 2 * k + u)
                if late(k, 1) or u:
                    c.settle()
                dve.wait_ge(s_["pe_otr"], 2 * k + u + 1)
                o = (R2, R0)[u][:, :].rearrange("p (h n) -> p h n", h=H)
                c.did(nc.vector.reciprocal(rden[:, :], o[:, :, DH]))
                c.settle()
                if late(k, 1):
                    dve.wait_ge(s_["pe_att"], k)
                c.did(nc.vector.tensor_tensor(at[:, u, :].rearrange("p (h m) -> p h m", h=H), o[:, :, 0:DH],
                                              rden[:, :].rearrange("p (h a) -> p h a", a=1).to_broadcast([P, H, DH]),
                                              ALU.mult))

            def mid(k, par):
                c = Chain(dve, s_["lna"], 7, k)
                dve.wait_ge(s_["pe_wo"], k + 1)
                if late(k, 1):
                    dve.wait_ge(s_["x2b_done"], k)
                    dve.wait_ge(s_["rs_a"], 2 * k)
                c.did(nc.vector.tensor_tensor(x2[:, :, :], two(R2), xn[par][:, :, :], ALU.add))
                c.settle()
                stats(c, "a", x2)
                dve.wait_ge(s_["rs_a"], 2 * k + 2)
                if late(k, 1):
                    dve.wait_ge(s_["pe_y2t"], k)
                normalise(c, "a", z2, x2)

            def step(k, i, par, f, b, ahead):
                if f:
                    dve.wait_ge(s_["pe_q"], k + 1)
                    if late(k, 1):
                        dve.wait_ge(s_["expanded"], 256 * k)
                        dve.wait_ge(s_["pe_av"], 8 * k)
                    nc.vector.tensor_scalar(qt[:, :, :], two(R1), 0.0, KERNEL_EPS, ALU.max, ALU.add).then_inc(s_["qt_done"], 1)
                    dve.wait_ge(s_["pe_k"], k + 1)
                    if late(k, 1):
                        dve.wait_ge(s_["pe_u"], 2 * k)
                    nc.vector.tensor_scalar(kk[:, :, :], two(R2), 0.0, KERNEL_EPS, ALU.max, ALU.add).then_inc(s_["kk_done"], 1)
                ip = i + par
                if ahead:
                    ca = in_stats(k + 1, ip, 1 - par)
                if b:
                    cb = end_x3(k - 2, par)
                if ahead:
                    ca = in_norm(ca, k + 1, 1 - par)
                if b:
                    end_h(cb, k - 2, i - 1, par)
                if ahead:
                    in_z(ca, k + 1, 1 - par)
                if b:
                    end_xm(cb, k - 2, i - 1, par)
                if f:
                    state(k, 0)
                    mask(k, 0)
                    mask(k, 1)
                if b:
                    dve.wait_ge(s_["pe_log"], k - 1)
                    if late(k, 3):
                        dve.wait_ge(s_["pe_lt"], k - 2)
                    dve.wait_ge(s_["pe_wo"], k if f else NS)
                    nc.vector.tensor_copy(lt, Y[0:E, 0:STEP]).then_inc(s_["lt_done"], 1)

                def keep_logits():
                    dve.wait_ge(s_["pe_lt"], k - 1)
                    nc.vector.tensor_copy(logit[:, bass.ds(2 * (k - 2), 2), :],
                                          Y[:, STEP:STEP + 2 * E].rearrange("p (u e) -> p u e", u=2)).then_inc(s_["logit_done"], 1)

                if b and not f:
                    keep_logits()
                if f:
                    for j in range(2, 8):
                        mask(k, j)
                        if j == 3 and b:
                            keep_logits()
                        if j == 5:
                            state(k, 1)
                    norm(k, 0)
                    norm(k, 1)
                    mid(k, par)

            dve.wait_ge(s_["pool_c"], 4)
            ca = in_norm(in_stats(0, 0, 0), 0, 0)
            in_z(ca, 0, 0)
            dve.wait_ge(s_["c_load"], 16 * C_LOADS)
            dve.wait_ge(s_["pool_c"], 4)
            for k in range(4):
                step(k, k // 2, k % 2, True, k >= 2, True)
            with dve.Fori(2, NS // 2 - 1) as i:
                for par in range(2):
                    step(2 * i + par, i, par, True, True, True)
            for k in range(NS - 2, NS):
                step(k, k // 2, k % 2, True, True, k + 1 < NS)
            step(NS, NS // 2, 0, False, True, False)
            step(NS + 1, NS // 2, 1, False, True, False)

            def sh_act(s, par, js=range(4)):
                if late(s, 2):
                    dve.wait_ge(s_["sh_down"], s - 1)
                for j in js:
                    dve.wait_ge(s_["sh_silu"], 4 * s + j + 1)
                    nc.vector.tensor_tensor(actt[par][:, j, :], sg[j][:, 0, :], two(bank[j])[:, 1, :],
                                            ALU.mult).then_inc(s_["sh_act"], 1)

            def scale(s, i, par):
                dve.wait_ge(p_["xsl"][par], 16 * (i + 1))
                if late(i, 1):
                    dve.wait_ge(p_["sct"][par], 32 * i)
                for u in range(2):
                    nc.vector.tensor_scalar(xm[par][:, u, :], xn[par][:, u, :], score[:, bass.ds(2 * s + u, 1)], None,
                                            ALU.mult).then_inc(s_["sc_sc"], 1)
                    nc.vector.tensor_copy(idx[par][:, u:u + 1], slot[:, bass.ds(2 * s + u, 1)]).then_inc(s_["sc_sc"], 1)

            c = Chain(dve, s_["route"], 0, 0)

            def do(ins):
                c.did(ins)
                c.settle()

            def over_e(a):
                return a.rearrange("p (t a) -> p t a", a=1).to_broadcast([P, NT, E])

            def over_t(a):
                return a.rearrange("p (a e) -> p a e", a=1).to_broadcast([P, NT, E])

            r0, r1, r2, r3 = (r[:, :, :] for r in rt)
            dve.wait_ge(s_["logit_done"], NS)
            do(nc.vector.tensor_reduce(top[:, :], logit[:, :, :], AX.X, ALU.max))
            do(nc.vector.tensor_tensor(r1, logit[:, :, :], over_e(top[:, :]), ALU.is_equal))
            do(nc.vector.tensor_tensor(r1, r1, over_t(erev), ALU.mult))
            do(nc.vector.tensor_reduce(rm[:, :], r1, AX.X, ALU.max))
            do(nc.vector.tensor_tensor(r0, r1, over_e(rm[:, :]), ALU.is_equal))
            assert c.n == 5
            sh_act(0, 0)
            dve.wait_ge(s_["route_pe"], 1)
            rank = bank[6][:, 0:NT * E].rearrange("p (t e) -> p t e", t=NT)
            total = bank[6][:, NT * E:2 * NT * E].rearrange("p (t e) -> p t e", t=NT)
            do(nc.vector.tensor_copy(r1, total))
            src, dst = rt[1], rt[2]
            d = 1
            while d < NT:
                nc.vector.tensor_copy(dst[:, 0:d, :], src[:, 0:d, :])
                do(nc.vector.tensor_tensor(dst[:, d:, :], src[:, d:, :], src[:, 0:NT - d, :], ALU.add))
                src, dst = dst, src
                d *= 2
            upto = src[:, :, :]
            sh_act(1, 1)
            do(nc.vector.tensor_scalar(cnt_i[:, :], src[:, NT - 1, :], float(P - 1), None, ALU.add))
            do(nc.vector.tensor_scalar(cnt_i[:, :], cnt_i[:, :], 7, None, ALU.logical_shift_right))
            do(nc.vector.tensor_copy(cnt[0][:, :], cnt_i[:, :]))
            a, b_ = cnt[1], cnt[2]
            do(nc.vector.tensor_copy(a[:, :], cnt[0][:, :]))
            d = 1
            while d < E:
                nc.vector.tensor_copy(b_[:, 0:d], a[:, 0:d])
                do(nc.vector.tensor_tensor(b_[:, d:], a[:, d:], a[:, 0:E - d], ALU.add))
                a, b_ = b_, a
                d *= 2
            do(nc.vector.tensor_tensor(cnt[3][:, :], a[:, :], cnt[0][:, :], ALU.subtract))
            do(nc.vector.tensor_scalar(cnt[3][:, :], cnt[3][:, :], float(P), None, ALU.mult))
            do(nc.vector.tensor_tensor(r3, upto, total, ALU.subtract))
            do(nc.vector.tensor_tensor(r3, r3, rank, ALU.add))
            do(nc.vector.tensor_tensor(r3, r3, over_t(cnt[3][:, :]), ALU.add))
            do(nc.vector.tensor_tensor(r3, r3, r0, ALU.mult))
            do(nc.vector.tensor_reduce(rm[:, :], r3, AX.X, ALU.add))
            do(nc.vector.tensor_copy(slot[:, :], rm[:, :]))
            dve.wait_ge(s_["tnum_ld"], 16)
            do(nc.vector.tensor_tensor(tcmp, tnum,
                                       a[0:1, 0:E - 1].rearrange("p (a e) -> p a e", a=1).to_broadcast([1, NRT, E - 1]),
                                       ALU.is_ge))
            do(nc.vector.tensor_reduce(eid_f[:, :], tcmp, AX.X, ALU.add))
            nc.vector.tensor_copy(eid[:, :], eid_f[:, :]).then_inc(s_["eid_done"], 1)

            dve.wait_ge(s_["route_act"], 1)
            for r in range(4):
                scale(r, r // 2, r % 2)
            with dve.Fori(1, NA // 2) as i:
                for par in range(2):
                    s = 2 * i + par
                    for v in range(2):
                        sh_act(s, par, range(2 * v, 2 * v + 2))
                        scale(2 * s + v, s, v)

            def r_att(t, par):
                dve.wait_ge(s_["r_at"], t + 1)
                if late(t, 2):
                    dve.wait_ge(s_["r_dn"], t - 1)
                nc.vector.tensor_copy(att_r[par][:, :, :], bank[4][:, :].rearrange("p (c n) -> p c n", c=4)).then_inc(s_["r_att"], 1)

            def r_act(t, par):
                dve.wait_ge(s_["r_silu"], t + 1)
                if late(t, 2):
                    dve.wait_ge(s_["r_at"], t - 1)
                nc.vector.tensor_tensor(act_r[par], sgr[par], bank[2 * par + 1][:, :], ALU.mult).then_inc(s_["r_act"], 1)

            r_act(0, 0)
            r_att(0, 0)
            r_act(1, 1)
            r_att(1, 1)
            r_act(2, 0)
            with dve.Fori(2, (NRT - 1) // 2) as i:
                for par in range(2):
                    r_att(2 * i + par - 2, par)
                    r_act(2 * i + par - 1, 1 - par)
            for t in (NRT - 3, NRT - 2):
                r_att(t, t % 2)
                r_act(t + 1, 1 - t % 2)
            r_att(NRT - 1, (NRT - 1) % 2)

            def put_idx(v, j):
                if late(j, 1):
                    dve.wait_ge(p_["gat"][v], 32 * j)
                nc.vector.tensor_copy(idx[v][:, :], slot[:, bass.ds(2 * (j + v * NA), 2)]).then_inc(p_["idx_c"][v], 1)

            f3 = (x3, x2)

            def fin_sum(v, j, par, more):
                c = Chain(dve, p_["fsum"][v], 5, j)
                if v:
                    dve.wait_ge(s_["sh_down"], NA + j + 1)
                    shared = two(bank[4 + par])
                else:
                    dve.wait_ge(s_["ysh_ld"], 16 * (j + 1))
                    shared = xin[0][:, :, :]
                dve.wait_ge(p_["gat"][v], 32 * (j + 1))
                if late(j, 1):
                    dve.wait_ge(p_["fout"][v], 3 * j)
                    dve.wait_ge(p_["frs"][v], 2 * j)
                c.did(nc.vector.tensor_tensor(f3[v][:, :, :], shared, xn[v][:, :, :], ALU.add))
                if more:
                    put_idx(v, j + 1)
                c.settle()
                stats(c, "xn"[v], f3[v])

            def fin_out(v, j):
                c = Chain(dve, p_["fout"][v], 3, j)
                dve.wait_ge(p_["frs"][v], 2 * j + 2)
                normalise(c, "xn"[v], f3[v], f3[v])
                c.settle()
                dve.wait_ge(p_["fld"][v], 16 * (j + 1))
                if late(j, 1):
                    dve.wait_ge(p_["fst"][v], 16 * j)
                c.did(nc.vector.tensor_tensor(xm[v][:, :, :], f3[v][:, :, :], hh[v][:, :, :], ALU.add))

            def last_step(j, par, acts, more):
                def part(n):
                    if acts:
                        sh_act(NA + j + 1, 1 - par, (n,))

                part(0)
                fin_sum(0, j, par, more)
                part(1)
                if late(j, 1):
                    fin_sum(1, j - 1, 1 - par, True)
                part(2)
                fin_out(0, j)
                part(3)
                if late(j, 1):
                    fin_out(1, j - 1)

            for v in range(2):
                dve.wait_ge(p_["sct"][v], 16 * NT // 2)
                put_idx(v, 0)
            sh_act(NA, 0)
            last_step(0, 0, True, True)
            last_step(1, 1, True, True)
            with dve.Fori(1, NA // 2 - 1) as i:
                for par in range(2):
                    last_step(2 * i + par, par, True, True)
            last_step(NA - 2, 0, True, True)
            last_step(NA - 1, 1, False, False)
            fin_sum(1, NA - 1, 1, False)
            fin_out(1, NA - 1)

        @block.tensor
        def _(pe):
            mm = nc.tensor.matmul

            def tile(a, c, u):
                return a[:, c, u * P:(u + 1) * P]

            def score(k, j):
                u, q = divmod(j, 4)
                g = q // 2
                if late(k, 1) or j >= 2:
                    pe.wait_ge(s_["masks"], 8 * k + j - 1)
                mm((S0, S1)[j % 2][:, :], tile(kt, g, u), qx[:, g, u, 4 * (q % 2):4 * (q % 2) + 4, :].rearrange("p h n -> p (h n)"),
                   start=True, stop=True).then_inc(s_["pe_sc"], 1)

            def attend(k, j, b):
                u, q = divmod(j, 4)
                o = (X, Y)[u]
                if q == 0:
                    pe.wait_ge(s_["state"], 2 * (2 * k + u)) if late(k, 1) or u else pe.wait_ge(s_["pool_c"], 4)
                    if u == 0:
                        if b:
                            pe.wait_ge(s_["lny"], 14 * (k - 2) + 1)
                        elif late(k, 1):
                            pe.wait_ge(s_["o_done"], 2 * k - 1)
                    else:
                        if b:
                            pe.wait_ge(s_["logit_done"], k - 1)
                        elif late(k, 1):
                            pe.wait_ge(s_["o_done"], 2 * k)
                pe.wait_ge(s_["masks"], 8 * k + j + 1)
                g = q // 2
                mm(o[:, q * P:(q + 1) * P], sx[u][:, g, 4 * (q % 2):4 * (q % 2) + 4, :].rearrange("p h n -> p (h n)"),
                   tile(qt, g, u), start=True, stop=False, skip_group_check=True)
                for h in range(G):
                    ins = mm(o[h * VW:(h + 1) * VW, q * P:(q + 1) * P], vx[:, u, 4 * q + h, :], st[j % 4][:, h, :],
                             start=False, stop=True, skip_group_check=True)
                ins.then_inc(s_["pe_av"], 1)

            def update(k, u):
                if late(k, 1) or u:
                    pe.wait_ge(s_["state"], 2 * (2 * k + u) - 1)
                for g in range(2):
                    ins = mm(U[:, g * 8 * VU:(g + 1) * 8 * VU], kk[:, u, g * P:(g + 1) * P],
                             vx[:, u, 8 * g:8 * g + 8, 0:VU], start=True, stop=True, skip_group_check=True)
                ins.then_inc(s_["pe_u"], 1)

            def turn(dst, src):
                for c in range(2):
                    for u in range(2):
                        ins = nc.tensor.transpose(dst[:, c, u * P:(u + 1) * P], src[:, u, c * P:(c + 1) * P], ident)
                return ins

            def otr(k, u, m):
                pe.wait_ge(s_["o_done"], 2 * k + u + 1)
                if m:
                    pe.wait_ge(s_["gelu"], 4 * (k - 1) + 3 + u)
                for q in range(4):
                    ins = nc.tensor.transpose((R2, R0)[u][:, q * P:(q + 1) * P], ot[u][:, q, :], ident)
                ins.then_inc(s_["pe_otr"], 1)

            def logits_turn(k):
                hold(pe, s_["lt_done"], k - 1)
                for u in range(2):
                    ins = nc.tensor.transpose(Y[:, STEP + u * E:STEP + (u + 1) * E], lt[:, u * P:(u + 1) * P], ident[0:E, 0:E])
                ins.then_inc(s_["pe_lt"], 1)

            def w2_part(u, blocks):
                for n in blocks:
                    ins = mm(two(X)[:, u, :], tile(ht, n, u), w2_s[:, n, :], start=(n == 0), stop=(n == MLP // P - 1))
                return ins

            def z_turn(k):
                pe.wait_ge(s_["lnn"], 6 * (k + 1))
                if late(k, 1):
                    pe.wait_ge(s_["norm"], 4 * k)
                turn(two(R0), z).then_inc(s_["pe_zt"], 1)

            def step(k, par, f, m, b, ahead):
                if f:
                    pe.wait_ge(s_["x1t_done"], k + 1)
                    if late(k, 1):
                        pe.wait_ge(s_["att_done"], k)
                    for g in range(2):
                        for c in range(KC):
                            ins = mm(two(R1)[:, g, :], wqkv_s[:, c, g * P:(g + 1) * P], x1t[:, c, :],
                                     start=(c == 0), stop=(c == KC - 1))
                    ins.then_inc(s_["pe_q"], 1)
                    if late(k, 1):
                        pe.wait_ge(s_["lna"], 7 * (k - 1) + 1)
                    for n, bk, sm in ((1, R2, "pe_k"), (2, R0, "pe_v")):
                        for u in range(2):
                            for c in range(KC):
                                ins = mm(two(bk)[:, u, :], tile(x1t, c, u), wqkv_s[:, c, n * D:(n + 1) * D],
                                         start=(c == 0), stop=(c == KC - 1))
                        ins.then_inc(s_[sm], 1)
                if m:
                    pe.wait_ge(s_["lna"], 7 * k)
                    pe.wait_ge(s_["qt_done"], k + 1) if f else pe.wait_ge(s_["att_done"], k)
                    turn(two(R1), z2).then_inc(s_["pe_y2t"], 1)
                if f:
                    pe.wait_ge(s_["kk_done"], k + 1)
                    turn(two(R2), kk).then_inc(s_["pe_kt"], 1)
                    pe.wait_ge(s_["vx_done"], k + 1)
                    update(k, 0)
                if m:
                    pe.wait_ge(s_["y2t_done"], k)
                    for j in range(4):
                        if j == 0 and f:
                            pe.wait_ge(s_["vx_done"], k + 1)
                        if j == 2 and f:
                            pe.wait_ge(s_["kt_done"], k + 1)
                        if j == 3:
                            pe.wait_ge(s_["gelu"], 4 * (k - 1) + 1)
                        for a in range(2):
                            n = 2 * j + a
                            for c in range(KC):
                                ins = mm(two((R0, R1, R2, R0)[j])[:, a, :], w1_s[:, c, n * P:(n + 1) * P], y2t[:, c, :],
                                         start=(c == 0), stop=(c == KC - 1))
                        ins.then_inc(s_["pe_w1"], 1)
                if b:
                    pe.wait_ge(s_["lny"], 14 * (k - 1))
                    if m:
                        pe.wait_ge(s_["gelu"], 4 * (k - 1) + 2)
                    turn(two(R1), xm[par]).then_inc(s_["pe_x3t"], 1)
                if f:
                    pe.wait_ge(s_["expanded"], 256 * (k + 1))
                    pe.wait_ge(s_["kt_done"], k + 1)
                    score(k, 0)
                    score(k, 1)
                if b:
                    pe.wait_ge(s_["x3t_done"], k - 1)
                    if f:
                        pe.wait_ge(s_["o_done"], 2 * k)
                    else:
                        pe.wait_ge(s_["logit_done"], k - 2)
                    for c in range(KC):
                        ins = mm(Y[0:E, 0:STEP], gw_s[:, c, :], x3t[par][:, c, :], start=(c == 0), stop=(c == KC - 1))
                    ins.then_inc(s_["pe_log"], 1)
                if b and not f:
                    logits_turn(k)
                if f:
                    attend(k, 0, b)
                    for j in range(2, 8):
                        score(k, j)
                        if j == 3 and b:
                            logits_turn(k)
                        if j == 3:
                            update(k, 1)
                        attend(k, j - 1, b)
                    attend(k, 7, b)
                    otr(k, 0, m)
                if m:
                    if f:
                        pe.wait_ge(s_["o_done"], 2 * k + 1)
                    pe.wait_ge(s_["gelu"], 4 * k)
                    w2_part(0, range(8))
                if f:
                    otr(k, 1, m)
                if m:
                    ins = w2_part(1, range(4 if f else 8))
                if f:
                    pe.wait_ge(s_["norm"], 4 * k + 4)
                    if b:
                        pe.wait_ge(s_["x3t_done"], k - 1)
                    turn(two(R1), at).then_inc(s_["pe_att"], 1)
                    if m:
                        ins = w2_part(1, range(4, 8))
                if m:
                    ins.then_inc(s_["pe_w2"], 1)
                if ahead:
                    z_turn(k + 1)
                if f:
                    pe.wait_ge(s_["att_done"], k + 1)
                    if not late(k, 1):
                        pe.wait_ge(s_["w_load"], 16 * W_LOADS)
                    for u in range(2):
                        for c in range(KC):
                            ins = mm(two(R2)[:, u, :], tile(att, c, u), wo_s[:, c, :], start=(c == 0), stop=(c == KC - 1))
                    ins.then_inc(s_["pe_wo"], 1)

            pe.wait_ge(s_["c_load"], 16 * C_LOADS)
            z_turn(0)
            for k in range(4):
                step(k, k % 2, True, k >= 1, k >= 2, True)
            with pe.Fori(2, NS // 2 - 1) as i:
                for par in range(2):
                    step(2 * i + par, par, True, True, True, True)
            step(NS - 2, 0, True, True, True, True)
            step(NS - 1, 1, True, True, True, False)
            step(NS, 0, False, True, True, False)
            step(NS + 1, 1, False, False, True, False)

            def sh_gate(s, i, par):
                pe.wait_ge(p_["sld"][par], 16 * (i + 1))
                for j in range(4):
                    if late(s, 1):
                        pe.wait_ge(s_["sh_act"], 4 * s - 4 + j + 1)
                    for a, w in enumerate((shg_s, shu_s)):
                        for c in range(KC):
                            ins = mm(two(bank[j])[:, a, :], w[:, c, j * P:(j + 1) * P], x3t[par][:, c, :],
                                     start=(c == 0), stop=(c == KC - 1))
                    ins.then_inc(s_["sh_g"], 1)

            def sh_out(s, par, bank_read=None):
                pe.wait_ge(s_["sh_act"], 4 * s + 4)
                if bank_read:
                    pe.wait_ge(*bank_read)
                elif late(s, 2):
                    pe.wait_ge(s_["sh_y"], s - 1)
                for u in range(2):
                    for n in range(I // P):
                        ins = mm(two(bank[4 + par])[:, u, :], actt[par][:, n, u * P:(u + 1) * P], shd_s[:, n, :],
                                 start=(n == 0), stop=(n == I // P - 1))
                ins.then_inc(s_["sh_down"], 1)

            pe.wait_ge(s_["sh_w"], 48)
            sh_gate(0, 0, 0)
            sh_gate(1, 0, 1)
            pe.wait_ge(s_["route"], 5)
            hot = rt[0][:, :, :].rearrange("p t e -> p (t e)")
            mm(bank[6][:, 0:NT * E], strict, hot, start=True, stop=True)
            mm(bank[6][:, NT * E:2 * NT * E], ones, hot, start=True, stop=True).then_inc(s_["route_pe"], 1)
            sh_out(0, 0)
            sh_gate(2, 1, 0)
            sh_out(1, 1)
            with pe.Fori(1, NA // 2 - 1) as i:
                for par in range(2):
                    sh_gate(2 * i + par + 1, i + par, 1 - par)
                    sh_out(2 * i + par, par)
            sh_gate(NA - 1, NA // 2 - 1, 1)
            sh_out(NA - 2, 0)
            sh_out(NA - 1, 1)

            pe.wait_ge(s_["eid_done"], 1)
            pe.wait_ge(s_["ex_w"], 16 * 3 * E)

            def r_turn(t, i, par):
                pe.wait_ge(p_["rld"][par], 16 * (i + 1))
                if late(t, 2):
                    pe.wait_ge(s_["r_xt"], t - 1)
                for c in range(KC):
                    ins = nc.tensor.transpose(bank[6 + par][:, c * P:(c + 1) * P], xs_t[par][:, c * P:(c + 1) * P], ident)
                ins.then_inc(s_["r_t"], 1)

            def weights(t):
                return ew[:, bass.ds(pe.value_load(eid[0:1, bass.ds(t, 1)], min_val=0, max_val=E - 1), 1), :].rearrange("p a n -> p (a n)")

            def r_gu(t, par):
                g, up, _ = parts(weights(t))
                pe.wait_ge(s_["r_xt"], t + 1)
                if late(t, 2):
                    pe.wait_ge(s_["r_act"], t - 1)
                for a, w in enumerate((g, up)):
                    for c in range(KC):
                        ins = mm(bank[2 * par + a][:, :], xst[par][:, c, :], w[:, c, :], start=(c == 0), stop=(c == KC - 1))
                ins.then_inc(s_["r_gu"], 1)

            def r_at(t, par):
                pe.wait_ge(s_["r_act"], t + 1)
                if late(t, 1):
                    pe.wait_ge(s_["r_att"], t)
                for n in range(I // P):
                    ins = nc.tensor.transpose(bank[4][:, n * P:(n + 1) * P], act_r[par][:, n * P:(n + 1) * P], ident)
                ins.then_inc(s_["r_at"], 1)

            def r_dn(t, par):
                _, _, d = parts(weights(t))
                pe.wait_ge(s_["r_att"], t + 1)
                if late(t, 1):
                    pe.wait_ge(s_["r_y"], t)
                for n in range(I // P):
                    ins = mm(bank[5][:, 0:D], att_r[par][:, n, :], d[:, n, :], start=(n == 0), stop=(n == I // P - 1))
                ins.then_inc(s_["r_dn"], 1)

            r_turn(0, 0, 0)
            r_turn(1, 0, 1)
            r_gu(0, 0)
            for t in (2, 3):
                r_turn(t, 1, t % 2)
                r_at(t - 2, t % 2)
                r_gu(t - 1, 1 - t % 2)
                r_dn(t - 2, t % 2)
            with pe.Fori(2, (NRT - 1) // 2) as i:
                for par in range(2):
                    t = 2 * i + par
                    r_turn(t, i, par)
                    r_at(t - 2, par)
                    r_gu(t - 1, 1 - par)
                    r_dn(t - 2, par)
            t = NRT - 1
            r_turn(t, t // 2, t % 2)
            r_at(t - 2, t % 2)
            r_gu(t - 1, 1 - t % 2)
            r_dn(t - 2, t % 2)
            r_at(t - 1, 1 - t % 2)
            r_gu(t, t % 2)
            r_dn(t - 1, 1 - t % 2)
            r_at(t, t % 2)
            r_dn(t, t % 2)

            def summed(s):
                return p_["fsum"][1], 5 * (s - 2 - NA) + 1

            sh_gate(NA, NA // 2, 0)
            sh_gate(NA + 1, NA // 2, 1)
            sh_out(NA, 0, (s_["r_att"], NRT))
            sh_gate(NA + 2, NA // 2 + 1, 0)
            sh_out(NA + 1, 1, (s_["r_y"], NRT))
            with pe.Fori(NA // 2 + 1, NS // 2 - 1) as i:
                for par in range(2):
                    s = 2 * i + par
                    sh_gate(s + 1, i + par, 1 - par)
                    sh_out(s, par, summed(s))
            sh_gate(NS - 1, NS // 2 - 1, 1)
            sh_out(NS - 2, 0, summed(NS - 2))
            sh_out(NS - 1, 1, summed(NS - 1))


_INS = ['L0_attn_inputs', 'L0_attn_ln1_scale', 'L0_attn_ln1_bias', 'L0_attn_wq', 'L0_attn_wk', 'L0_attn_wv', 'L0_attn_wo',
        'L0_attn_ln2_scale', 'L0_attn_ln2_bias', 'L0_attn_w1', 'L0_attn_b1', 'L0_attn_w2', 'L0_attn_b2', 'L0_ffn_gate_w',
        'L0_ffn_sh_gate', 'L0_ffn_sh_up', 'L0_ffn_sh_down', 'L0_ffn_rt_gate', 'L0_ffn_rt_up', 'L0_ffn_rt_down']


def _constants():
    import numpy as np
    c = np.zeros((P, C_N), np.float32)
    p = np.arange(P)
    c[:, C_ID:C_ID + P] = np.eye(P)
    c[:, C_CAUSAL:C_CAUSAL + P] = p[None, :] >= p[:, None]
    c[:, C_STRICT:C_STRICT + P] = p[:, None] < p[None, :]
    c[:, C_ONES:C_ONES + P] = 1
    c[:, C_BLOCK:C_BLOCK + 8 * VU] = np.arange(8 * VU)[None, :] // VU == p[:, None] // DH
    c[:, C_KEEP:C_KEEP + NS] = np.arange(NS) % STEPS_PER_BATCH != STEPS_PER_BATCH - 1
    c[:, C_EREV:C_EREV + E] = E - np.arange(E)
    c[:, C_TILE:] = np.arange(NRT * (E - 1)) // (E - 1)
    return c


def kernel(**inputs):
    import numpy as _np
    import concourse.bacc as _bacc
    from concourse.bass_utils import run_bass_kernel_spmd as _run

    nc = _bacc.Bacc("TRN2", target_bir_lowering=False, num_devices=1)
    arrays, args = {}, []
    for name in _INS:
        a = _np.ascontiguousarray(inputs[name])
        arrays[f"in_{name}"] = a
        args.append(nc.dram_tensor(f"in_{name}", a.shape, F32, kind="ExternalInput").ap())
    arrays["in_constants"] = _constants()
    args.append(nc.dram_tensor("in_constants", (P, C_N), F32, kind="ExternalInput").ap())
    for name, shape in (("h", (TOK, D)), ("xn2", (TOK, D)), ("xt", (NS, P, KC * STEP)), ("xs", (NRT * P, D)),
                        ("ysh", (TOK, D)), ("yr", (NRT * P, D))):
        args.append(nc.dram_tensor("scratch_" + name, shape, F32, kind="Internal").ap())
    args.append(nc.dram_tensor("out_0", (B, S, D), F32, kind="ExternalOutput").ap())
    build(nc, *args)
    r = _run(nc, [arrays], core_ids=[0])
    return r.results[0]["out_0"]
```

```python
from contextlib import ExitStack

import concourse.bass as bass
from concourse import mybir

ALU = mybir.AluOpType
ACT = mybir.ActivationFunctionType
AX = mybir.AxisListType
F32 = mybir.dt.float32
R32 = mybir.dt.float32r
KB = 1024
I32 = mybir.dt.int32
U32 = mybir.dt.uint32

P = 128
B, S, D = 4, 1024, 256
H, DH, MLP = 16, 16, 1024
E, I = 8, 512
KC = D // P
TOK = B * S
STEP = 256
NS = TOK // STEP
NT = TOK // P
NA = NS // 2
STEPS_PER_BATCH = S // STEP
VW = 32
VU = DH + 1
G = 4
NRT = NT + E - 1
EW = 2 * KC * I + (I // P) * D
EPS_OUTER, EPS_INNER, KERNEL_EPS = 1e-5, 1e-6, 1e-3

C_ID, C_CAUSAL, C_STRICT, C_ONES = 0, P, 2 * P, 3 * P
C_BLOCK = 4 * P
C_KEEP = C_BLOCK + 8 * VU
C_EREV = C_KEEP + NS
C_TOKEN = C_EREV + E
C_SLOT = C_TOKEN + NT
C_TILE = C_SLOT + NRT
C_N = C_TILE + NRT * (E - 1)
DX = D + 1


def late(k, n):
    return not isinstance(k, int) or k >= n


def hold(eng, sem, value):
    eng.wait_ge(sem, value)
    eng.nop(nofuse=True)


class Chain:

    def __init__(self, eng, sem, per, rnd):
        self.eng, self.sem, self.base, self.n = eng, sem, rnd * per, 0

    def did(self, ins):
        self.n += 1
        ins.then_inc(self.sem, 1)

    def settle(self):
        self.eng.wait_ge(self.sem, self.base + self.n)


def build(nc, x, ln1s, ln1b, wq, wk, wv, wo, ln2s, ln2b, w1, b1, w2, b2, gw, shg, shu, shd, rtg, rtu, rtd, cst,
          h_d, xn_d, xt_d, xs_d, ysh_d, yr_d, out):
    with ExitStack() as ctx:
        def sb(name, shape, dt=F32):
            return ctx.enter_context(nc.sbuf_tensor(name, shape, dt))

        def sem(name):
            return ctx.enter_context(nc.semaphore(name))

        def at(name, shape, offset, dt=F32):
            return nc.alloc_sbuf_tensor_at(name, shape, dt, offset=base + offset)

        def pair(name, shape, offset, lo_offset=None):
            if lo_offset is None:
                size = 4
                for n in shape[1:]:
                    size *= n
                lo_offset = offset + size
            return at(name + "_hi", shape, offset, R32), at(name + "_lo", shape, lo_offset, R32), at(name + "_x", shape, lo_offset)

        base = (nc.sbuf_base + 31) // 32 * 32
        arena = sb("arena", [P, 148 * KB // 4])
        assert nc.sbuf_base == base + 148 * KB
        ew = at("ew", [P, E, EW], 0)
        wqkv, wo_p = pair("wqkv", [P, KC, 3 * D], 0)[:2], pair("wo", [P, KC, D], 12 * KB)[:2]
        w1_p, w2_p = pair("w1", [P, KC, MLP], 16 * KB)[:2], pair("w2", [P, MLP // P, D], 32 * KB)[:2]
        qx = at("qx", [P, 2, 2, 2, 8, P], 48 * KB, R32)
        ht_h, ht_l, ht_x = pair("ht", [P, MLP // P, STEP], 80 * KB)
        wqkv_raw, wo_raw = at("wqkv_raw", [P, KC, 3 * D], 80 * KB), at("wo_raw", [P, KC, D], 86 * KB)
        w1_raw, w2_raw = at("w1_raw", [P, KC, MLP], 88 * KB), at("w2_raw", [P, MLP // P, D], 96 * KB)
        sgu = pair("sgu", [P, 2, KC, I], 96 * KB)[:2]
        sd = pair("sd", [P, I // P, D], 112 * KB)[:2]
        sgu_raw = at("sgu_raw", [P, 2, KC, I], 112 * KB)
        sd_raw = at("sd_raw", [P, I // P, D], 76 * KB)
        x1_h, x1_l, x1_x = pair("x1t", [P, KC, STEP], 120 * KB)
        y2_h, y2_l, y2_x = pair("y2t", [P, KC, STEP], 124 * KB)
        att_h, att_l, _ = pair("att", [P, KC, STEP], 128 * KB)
        kt_h, kt_l, _ = pair("kt", [P, 2, STEP], 132 * KB)
        q_hl = at("q_hl", [P, 2, 2, STEP], 136 * KB, R32)
        q_h, q_l = q_hl[:, 0, :, :], q_hl[:, 1, :, :]
        st = [at(f"st{i}", [P, G, P], 140 * KB + i * 2 * KB) for i in range(4)]
        sx_p = [pair("sx3_0", [P, KC, STEP], 132 * KB)[:2], pair("sx3_1", [P, KC, STEP], 136 * KB)[:2]]
        act_p = [pair("act_0", [P, I // P, STEP], 140 * KB, 124 * KB), pair("act_1", [P, I // P, STEP], 144 * KB, 128 * KB)]

        def parts(w):
            return (w[:, 0:KC * I].rearrange("p (c n) -> p c n", c=KC),
                    w[:, KC * I:2 * KC * I].rearrange("p (c n) -> p c n", c=KC),
                    w[:, 2 * KC * I:EW].rearrange("p (c n) -> p c n", c=I // P))

        gw_s = sb("gw_s", [P, KC, E])
        cols = sb("cols", [P, 4 * KC + MLP // P])
        ln1s_c, ln1b_c, ln2s_c, ln2b_c = (cols[:, i * KC:(i + 1) * KC] for i in range(4))
        b1_c = cols[:, 4 * KC:]
        b2_s = sb("b2_s", [P, D])
        cs = sb("cs", [P, C_TILE])
        ident = cs[:, C_ID:C_ID + P]
        causal = cs[:, C_CAUSAL:C_CAUSAL + P]
        strict = cs[:, C_STRICT:C_STRICT + P]
        ones = cs[:, C_ONES:C_ONES + P]
        block_mask = cs[:, C_BLOCK:C_BLOCK + 8 * VU].rearrange("p (h n) -> p h n", h=8)
        erev = cs[:, C_EREV:C_EREV + E]
        half = sb("half", [P, 2])
        eps_o = sb("eps_o", [P, 2])
        eps_i = sb("eps_i", [P, 2])

        xin = [sb(f"xin{i}", [P, 2, D]) for i in range(2)]
        xr = sb("xr", [P, 2, D])
        xn = [sb(f"xn{i}", [P, 2, D]) for i in range(2)]
        z = sb("z", [P, 2, D])
        qt = sb("qt", [P, 2, STEP])
        kk = sb("kk", [P, 2, D])
        vx = sb("vx", [P, 2, H, VW])
        sx_all = sb("sx", [P, 2, 2, 8, VW])
        sx = [sx_all[:, i, :, :, :] for i in range(2)]
        su = sb("su", [P, 2, 8, VU])
        ot = [sb(f"ot{i}", [P, 4, P]) for i in range(2)]
        rden = sb("rden", [P, H])
        av = sb("av", [P, 2, D])
        x2 = sb("x2", [P, 2, D])
        x2b_all = sb("x2b", [P, 2, 2, D])
        x2b = [x2b_all[:, i, :, :] for i in range(2)]
        z2 = sb("z2", [P, 2, D])
        x3 = sb("x3", [P, 2, D])
        hh_all = sb("hh", [P, 2, 2, D])
        hh = [hh_all[:, i, :, :] for i in range(2)]
        zrow = hh[0].rearrange("p u d -> p (u d)")[:, 0:DX]
        xm = [sb(f"xm{i}", [P, 2, D]) for i in range(2)]
        x3t = [sb(f"x3t{i}", [P, KC, STEP]) for i in range(2)]
        lns = {n: (sb("bs_" + n, [P, 2, 6]), sb("mv_" + n, [P, 2, 2]), sb("ve_" + n, [P, 2]), sb("rs_" + n, [P, 2]))
               for n in ("x", "n", "a", "y", "h")}
        logit = sb("logit", [P, NT, E])
        lt = at("lt", [P, STEP], 128 * KB)[0:E, :]

        top = xr[:, 1, 0:NT]
        rt = [x2b[i // 2][:, i % 2, :].rearrange("p (t e) -> p t e", t=NT) for i in range(4)]
        rm = xr[:, 1, NT:2 * NT]
        score = sb("score", [P, NT])
        cnt = [xr[:, 1, (8 + i) * E:(9 + i) * E] for i in range(4)]
        cnt_i = sb("cnt_i", [P, E], I32)
        slot = sb("slot", [P, NT], U32)
        tcmp = x2[0:1, :, :].rearrange("p a n -> p (a n)")[:, 0:NRT * (E - 1)].rearrange("p (t e) -> p t e", t=NRT)
        tnum = z2[0:1, :, :].rearrange("p a n -> p (a n)")[:, 0:NRT * (E - 1)].rearrange("p (t e) -> p t e", t=NRT)
        rid = xr[:, 0, NRT:2 * NRT]
        rid_a = xr[:, 0, 2 * NRT:3 * NRT]
        idx_r = [sb(f"idx_r{i}", [P, 1], U32) for i in range(2)]
        eid_f = xr[0:1, 0, 0:NRT]
        eid = sb("eid", [1, NRT], I32)
        idx_all = sb("idx", [P, 4, 2], U32)
        idx = [idx_all[:, i, :] for i in range(4)]

        bank = [ctx.enter_context(nc.psum_tensor(f"bank{i}", [P, 512], F32)) for i in range(8)]
        R0, R1, R2, S0, S1, X, Y, U = bank

        def two(b):
            return b[:, :].rearrange("p (a n) -> p a n", a=2)

        LG = 2 * 8 * VU

        names = (
            "c_load w_load xr_ld expanded zeroed sh_w ex_w tnum_ld ysh_ld "
            "small_c pool_c x2b_done htl_done rs_x rs_n rs_a rs_y rs_h "
            "w_hi x1x_done x1t_done qh_done y2x_done y2t_done kt_done gelu hth_done x3t_done o_done att_done "
            "w_lo x1l_done y2l_done kl_done al_done ql_done qt_done kk_done vx_done masks state norm lnx lnn "
            "lna lny lt_done logit_done "
            "pe_zt pe_q pe_k pe_v pe_y2t pe_kt pe_w1 pe_x3t pe_log pe_lt pe_u pe_sc pe_av pe_otr pe_att "
            "pe_wo pe_w2 "
            "route route_pe route_act eid_done sc_sc "
            "sx_hi sx_lo sh_g sh_silu sh_f sh_hi sh_lo sh_down sh_y "
            "r_t r_xt r_gu r_silu r_act r_at r_att r_dn r_y rid_f rid idx_r "
        ).split()
        s_ = {n: sem(n) for n in names}
        par_names = "xin_ld h_s xm_s xt_s sld yst rld rst gat fld fst xsl fsum fout fadd frs".split()
        p_ = {n: [sem(f"{n}{i}") for i in range(2)] for n in par_names}

        sct = [sem(f"sct{i}") for i in range(4)]

        xv = x.rearrange("b (s u p) d -> (b s) p u d", u=2, p=P)
        outv = out.rearrange("b (s u p) d -> (b s) p u d", u=2, p=P)
        hv = h_d.rearrange("(s u p) d -> s p u d", u=2, p=P)
        xnv = xn_d.rearrange("(s u p) d -> s p u d", u=2, p=P)
        yshv = ysh_d.rearrange("(s u p) d -> s p u d", u=2, p=P)
        xsv = xs_d.rearrange("(t p) d -> t p d", p=P)
        yrv = yr_d[0:TOK, :].rearrange("(s u p) d -> s p u d", u=2, p=P)

        C_LOADS, W_LOADS = 6, 8

        def pick(v, k):
            return v[bass.ds(k, 1)].rearrange("a p u d -> p (a u) d")

        def pick3(v, k):
            return v[bass.ds(k, 1)].rearrange("a p d -> p (a d)")

        ysh = [xin[0], xin[1]]
        sg = [z[:, 0, :], z[:, 1, :], kk[:, 0, :], kk[:, 1, :]]
        xrow = [at("xrow0", [P, 2, DX], 120 * KB)]
        xrow += [a.rearrange("p i u d -> p (i u d)")[:, 0:2 * DX].rearrange("p (u d) -> p u d", u=2)
                 for a in (x2b_all[:, :, :, :], hh_all[:, :, :, :], sx_all[:, :, :, :, :].rearrange("p i g h n -> p i g (h n)"))]
        xs_t = [at(f"xs_t{i}", [P, DX], 120 * KB + i * 2 * KB)[:, :] for i in range(2)]
        xst = [qt[:, :, 0:P], qt[:, :, P:2 * P]]
        sgr = [x3[:, :, :].rearrange("p a n -> p (a n)"), z2[:, :, :].rearrange("p a n -> p (a n)")]
        act_r = [xin[0][:, :, :].rearrange("p a n -> p (a n)"), xin[1][:, :, :].rearrange("p a n -> p (a n)")]
        att_r = [st[2], st[3]]
        f3 = (x3, x2)
        y_r = [ot[0][:, 0:2, :].rearrange("p a n -> p (a n)"), ot[1][:, 0:2, :].rearrange("p a n -> p (a n)")]

        block = ctx.enter_context(nc.Block())

        @block.sync
        def _(sp):
            def load_x(k, par, i):
                sp.dma_start(xin[par][:, :, :], pick(xv, k)).then_inc(p_["xin_ld"][par], 16)

            load_x(0, 0, 0)
            sp.dma_start(cs[:, :], cst[:, 0:C_TILE]).then_inc(s_["c_load"], 16)
            for src, dst in ((ln1s, ln1s_c), (ln1b, ln1b_c)):
                with nc.allow_non_contiguous_dma(reason="a vector into a column per chunk"):
                    sp.dma_start(dst, src.rearrange("(c p) -> p c", p=P)).then_inc(s_["c_load"], 16)
            for i, w in enumerate((wq, wk, wv)):
                sp.dma_start(wqkv_raw[:, :, i * D:(i + 1) * D],
                             w.rearrange("(c p) h m -> p c (h m)", p=P)).then_inc(s_["c_load"], 16)
            load_x(1, 1, 0)
            sp.dma_start(wo_raw[:, :, :], wo.rearrange("h m d -> (h m) d").rearrange("(c p) d -> p c d", p=P)).then_inc(s_["w_load"], 16)
            for src, dst in ((ln2s, ln2s_c), (ln2b, ln2b_c), (b1, b1_c)):
                with nc.allow_non_contiguous_dma(reason="a vector into a column per chunk"):
                    sp.dma_start(dst, src.rearrange("(c p) -> p c", p=P)).then_inc(s_["w_load"], 16)
            sp.dma_start(b2_s[:, :], b2.rearrange("(a d) -> a d", a=1).to_broadcast([P, D])).then_inc(s_["w_load"], 16)

            def later_weights():
                sp.dma_start(w1_raw[:, :, :], w1.rearrange("(c p) n -> p c n", p=P)).then_inc(s_["w_load"], 16)
                sp.dma_start(w2_raw[:, :, :], w2.rearrange("(c p) n -> p c n", p=P)).then_inc(s_["w_load"], 16)
                sp.dma_start(gw_s[:, :, :], gw.rearrange("(c p) n -> p c n", p=P)).then_inc(s_["w_load"], 16)

            def zero_rows(j):
                n = NRT // 3
                sp.dma_start(xs_d[j * n * P:(j + 1) * n * P, :].rearrange("(t p) d -> p t d", p=P),
                             zrow.rearrange("p (a d) -> p a d", a=1).to_broadcast([P, n, DX])).then_inc(s_["zeroed"], 16)

            def shared_load():
                for j, w in enumerate((shg, shu)):
                    sp.dma_start(sgu_raw[:, j, :, :], w.rearrange("(c p) n -> p c n", p=P)).then_inc(s_["sh_w"], 16)

            def expert_load(e):
                dst = ew[:, bass.ds(e, 1), :].rearrange("p a n -> p (a n)")
                for d, w in zip(parts(dst), (rtg, rtu, rtd)):
                    sp.dma_start(d, w[bass.ds(e, 1)].rearrange("a (c p) n -> p (a c) n", p=P)).then_inc(s_["ex_w"], 16)

            def step(k, i, par, f, m, b, ahead):
                if f:
                    hold(sp, s_["ql_done"], k + 1)
                    if late(k, 1):
                        sp.wait_ge(s_["pe_sc"], 8 * k)
                    for h in range(8):
                        r = slice(h * DH, (h + 1) * DH)
                        sp.dma_start(qx[r, :, :, :, h, :].rearrange("p a g u n -> p (a g u) n").bitcast(F32),
                                     q_hl[r, :, :, :].rearrange("p a g (u n) -> p (a g u) n", u=2).bitcast(F32)).then_inc(s_["expanded"], 16)
                if ahead:
                    hold(sp, s_["lnx"], 6 * (k + 1))
                    sp.dma_start(xin[par][:, :, :], pick(xv, k + 2)).then_inc(p_["xin_ld"][par], 16)
                if b:
                    hold(sp, s_["lny"], 14 * (k - 1))
                    sp.dma_start(pick(hv, k - 2), hh[par][:, :, :]).then_inc(p_["h_s"][par], 16)
                    sp.dma_start(pick(xnv, k - 2), xm[par][:, :, :]).then_inc(p_["xm_s"][par], 16)
                if m:
                    sp.dma_start(xr[:, :, :], pick(xv, k - 1)).then_inc(s_["xr_ld"], 16)
                if b:
                    hold(sp, s_["x3t_done"], k - 1)
                    sp.dma_start(xt_d[bass.ds(k - 2, 1)].rearrange("a p n -> p (a n)"),
                                 x3t[par][:, :, :].rearrange("p a n -> p (a n)")).then_inc(p_["xt_s"][par], 16)

            later_weights()
            sp.wait_ge(s_["pool_c"], 5)
            sp.wait_ge(s_["zeroed"], 1)
            for k in range(4):
                step(k, k // 2, k % 2, True, k >= 1, k >= 2, True)
                if k <= 1:
                    zero_rows(k)
                if k == 1:
                    zero_rows(2)
                if k == 2:
                    sp.wait_ge(s_["w_lo"], 4)
                    shared_load()
            with sp.Fori(2, NS // 2 - 1) as i:
                for par in range(2):
                    step(2 * i + par, i, par, True, True, True, True)
            for k in range(NS - 2, NS):
                step(k, k // 2, k % 2, True, True, True, False)
            step(NS, NS // 2, 0, False, True, True, False)

            def sh_load(s, par):
                sp.dma_start(x3t[par][:, :, :].rearrange("p a n -> p (a n)"),
                             xt_d[bass.ds(s, 1)].rearrange("a p n -> p (a n)")).then_inc(p_["sld"][par], 16)

            sp.wait_ge(p_["xt_s"][0], 16 * (NS // 2))
            sp.wait_ge(s_["pe_log"], NS - 1)
            sh_load(0, 0)
            step(NS + 1, NS // 2, 1, False, False, True, False)
            sp.wait_ge(s_["pe_sc"], 8 * NS)
            sp.dma_start(sd_raw[:, :, :], shd.rearrange("(c p) n -> p c n", p=P)).then_inc(s_["sh_w"], 16)

            sp.wait_ge(s_["pe_y2t"], NS)
            sp.dma_start(tnum, cst[0:1, C_TILE:C_N].rearrange("p (t e) -> p t e", t=NRT)).then_inc(s_["tnum_ld"], 16)


            def row_load(s, par):
                sp.dma_start(xn[par][:, :, :], pick(xnv, s)).then_inc(p_["xsl"][par], 16)

            def sh_store(s, par):
                hold(sp, s_["sh_y"], s + 1)
                sp.dma_start(pick(yshv, s), ysh[par][:, :, :]).then_inc(p_["yst"][par], 16)

            sp.wait_ge(s_["pe_log"], NS)
            sp.wait_ge(p_["xt_s"][1], 16 * (NS // 2))
            sh_load(1, 1)
            for par in range(2):
                sp.wait_ge(p_["xm_s"][par], 16 * (NS // 2))
                sp.wait_ge(p_["h_s"][par], 16 * (NS // 2))
                row_load(par, par)
            hold(sp, s_["sx_lo"], 1)
            sh_load(2, 0)
            sp.wait_ge(s_["pe_w2"], NS)
            expert_load(0)

            def sh_step(s, i, par, rows, expert):
                hold(sp, s_["sx_lo"], s + 2)
                sh_load(s + 3, 1 - par)
                for v in range(2):
                    if rows:
                        hold(sp, s_["sc_sc"], 4 * (2 * s + v + 1))
                        row_load(2 * s + v + 2, v)
                if expert:
                    expert_load(s + 1)
                sh_store(s, par)

            with sp.Fori(0, 2) as i:
                for par in range(2):
                    sh_step(2 * i + par, i, par, True, True)
            sp.wait_ge(s_["w_lo"], 6)
            for s in range(4, NA):
                sh_step(s, s // 2, s % 2, s < NA - 1, s < E - 1)

            for n in range(4):
                sp.wait_ge(sct[n], 16 * NT // 4)

            def r_load(t, par):
                sp.dma_start(xs_t[par], pick3(xsv, t)).then_inc(p_["rld"][par], 16)

            def r_next(t, par):
                sp.wait_ge(s_["r_t"], t - 1)
                hold(sp, s_["rid"], t - 1)
                r_load(t, par)

            r_load(0, 0)
            r_load(1, 1)
            for t in (2, 3):
                r_next(t, t % 2)
            with sp.Fori(2, (NRT - 1) // 2) as i:
                for par in range(2):
                    r_next(2 * i + par, par)
            r_next(NRT - 1, 0)
            sp.wait_ge(p_["rst"][0], 16 * ((NRT + 1) // 2))
            sp.wait_ge(p_["rst"][1], 16 * (NRT // 2))

            def half_of(v, j):
                return j + v * NA

            def ysh_load(j):
                sp.dma_start(xin[0][:, :, :], pick(yshv, j)).then_inc(s_["ysh_ld"], 16)

            def h_load(v, j):
                sp.dma_start(hh[v][:, :, :], pick(hv, half_of(v, j))).then_inc(p_["fld"][v], 16)

            def y_load(v, j):
                sp.dma_start(xn[v][:, :, :], pick(yrv, half_of(v, j))).then_inc(p_["gat"][v], 16)

            def finish(v, j, more):
                hold(sp, p_["fadd"][v], j + 1)
                sp.dma_start(pick(outv, half_of(v, j)), xm[v][:, :, :]).then_inc(p_["fst"][v], 16)
                if more:
                    h_load(v, j + 1)

            def last_step(j, par, load, more):
                if load:
                    hold(sp, s_["sx_lo"], NA + j + 2)
                    sh_load(NA + j + 3, 1 - par)
                if more:
                    hold(sp, p_["fsum"][0], 5 * j + 1)
                    ysh_load(j + 1)
                    y_load(0, j + 1)
                if late(j, 1):
                    hold(sp, p_["fsum"][1], 5 * (j - 1) + 1)
                    y_load(1, j)
                finish(0, j, more)
                if late(j, 1):
                    finish(1, j - 1, True)

            for par in range(2):
                sp.wait_ge(p_["yst"][par], 16 * (NA // 2))
            ysh_load(0)
            for v in range(2):
                y_load(v, 0)
                h_load(v, 0)
            last_step(0, 0, True, True)
            last_step(1, 1, True, True)
            with sp.Fori(1, NA // 2 - 2) as i:
                for par in range(2):
                    last_step(2 * i + par, par, True, True)
            last_step(NA - 4, 0, True, True)
            last_step(NA - 3, 1, False, True)
            last_step(NA - 2, 0, False, True)
            last_step(NA - 1, 1, False, False)
            finish(1, NA - 1, False)
            for v in range(2):
                sp.wait_ge(p_["fst"][v], 16 * NA)

        @block.gpsimd
        def _(pool):
            nc.gpsimd.memset(zrow, 0.0).then_inc(s_["zeroed"], 1)
            nc.gpsimd.memset(half[:, :], -0.5).then_inc(s_["small_c"], 1)
            nc.gpsimd.memset(eps_o[:, :], EPS_OUTER).then_inc(s_["small_c"], 1)
            nc.gpsimd.memset(eps_i[:, :], EPS_INNER).then_inc(s_["small_c"], 1)
            nc.gpsimd.memset(vx[:, :, :, :], 0.0).then_inc(s_["pool_c"], 1)
            nc.gpsimd.memset(sx[0][:, :, :, :], 0.0).then_inc(s_["pool_c"], 1)
            nc.gpsimd.memset(sx[1][:, :, :, :], 0.0).then_inc(s_["pool_c"], 1)
            pool.wait_ge(s_["small_c"], 3)
            pool.wait_ge(s_["pool_c"], 1)
            nc.gpsimd.memset(vx[:, :, :, DH:DH + 1], 1.0).then_inc(s_["pool_c"], 1)

            def rsqrt(which, eps, stats, n, rs, rnd):
                _, mv, ve, r = lns[which]
                pool.wait_ge(stats, n)
                nc.gpsimd.tensor_tensor(ve[:, :], mv[:, :, 1], eps[:, :], ALU.add).then_inc(rs, 1)
                pool.wait_ge(rs, 2 * rnd + 1)
                nc.gpsimd.tensor_tensor(r[:, :], ve[:, :], half[:, :], ALU.pow).then_inc(rs, 1)

            def step(k, par, f, m, b, ahead):
                if ahead:
                    rsqrt("x", eps_o, s_["lnx"], 6 * (k + 1) + 4, s_["rs_x"], k + 1)
                if b:
                    rsqrt("y", eps_o, s_["lny"], 14 * (k - 2) + 5, s_["rs_y"], k - 2)
                if b:
                    rsqrt("h", eps_o, s_["lny"], 14 * (k - 2) + 12, s_["rs_h"], k - 2)
                if m:
                    for j in range(4):
                        pool.wait_ge(s_["hth_done"], 4 * (k - 1) + j + 1)
                        n = slice(2 * j, 2 * j + 2)
                        nc.gpsimd.tensor_tensor(ht_l[:, n, :], ht_x[:, n, :], ht_h[:, n, :].bitcast(F32),
                                                ALU.subtract).then_inc(s_["htl_done"], 1)
                if ahead:
                    rsqrt("n", eps_i, s_["lnn"], 6 * (k + 1) + 4, s_["rs_n"], k + 1)
                if f:
                    rsqrt("a", eps_i, s_["lna"], 7 * k + 5, s_["rs_a"], k)
                if f:
                    if late(k, 2):
                        pool.wait_ge(s_["lny"], 14 * (k - 2) + 1)
                    if not late(k, 1):
                        pool.wait_ge(s_["w_load"], 16 * W_LOADS)
                    nc.gpsimd.tensor_tensor(x2b[par][:, :, :], x2[:, :, :],
                                            b2_s[:, :].rearrange("p (a d) -> p a d", a=1).to_broadcast([P, 2, D]),
                                            ALU.add).then_inc(s_["x2b_done"], 1)

            rsqrt("x", eps_o, s_["lnx"], 4, s_["rs_x"], 0)
            rsqrt("n", eps_i, s_["lnn"], 4, s_["rs_n"], 0)
            nc.gpsimd.memset(qx[:, :, :, :, :, :].bitcast(F32), 0.0).then_inc(s_["pool_c"], 1)
            for k in range(4):
                step(k, k % 2, True, k >= 1, k >= 2, True)
            with pool.Fori(2, NS // 2 - 1) as i:
                for par in range(2):
                    step(2 * i + par, par, True, True, True, True)
            for k in range(NS - 2, NS):
                step(k, k % 2, True, True, True, k + 1 < NS)
            step(NS, 0, False, True, True, False)
            step(NS + 1, 1, False, False, True, False)

            pool.wait_ge(s_["zeroed"], 49)
            with pool.Fori(0, NS // 4) as i:
                for n in range(4):
                    hold(pool, s_["sc_sc"], 4 * (4 * i + n + 1))
                    for u in range(2):
                        nc.gpsimd.indirect_dma_start(
                            out=xs_d, out_offset=bass.IndirectOffsetOnAxis(ap=idx[n][:, u:u + 1], axis=0),
                            in_=xrow[n][:, u, :], in_offset=None).then_inc(sct[n], 16)

            def y_scatter(t, par):
                pool.wait_ge(s_["idx_r"], t + 1)
                hold(pool, s_["r_y"], t + 1)
                nc.gpsimd.indirect_dma_start(
                    out=yr_d, out_offset=bass.IndirectOffsetOnAxis(ap=idx_r[par][:, 0:1], axis=0),
                    in_=y_r[par], in_offset=None).then_inc(p_["rst"][par], 16)

            with pool.Fori(0, NRT // 2) as i:
                for par in range(2):
                    y_scatter(2 * i + par, par)
            y_scatter(NRT - 1, (NRT - 1) % 2)

            def fin_add(v, j):
                pool.wait_ge(p_["fout"][v], 2 * j + 2)
                pool.wait_ge(p_["fld"][v], 16 * (j + 1))
                if late(j, 1):
                    pool.wait_ge(p_["fst"][v], 16 * j)
                nc.gpsimd.tensor_tensor(xm[v][:, :, :], f3[v][:, :, :], hh[v][:, :, :], ALU.add).then_inc(p_["fadd"][v], 1)

            def fin_rsqrt(v, j):
                rsqrt("xn"[v], eps_o, p_["fsum"][v], 5 * j + 5, p_["frs"][v], j)

            fin_rsqrt(0, 0)
            fin_add(0, 0)
            with pool.Fori(1, NA) as j:
                fin_rsqrt(0, j)
                fin_rsqrt(1, j - 1)
                fin_add(0, j)
                fin_add(1, j - 1)
            fin_rsqrt(1, NA - 1)
            fin_add(1, NA - 1)

        @block.scalar
        def _(act):
            def x3_hi(s, i, par):
                act.wait_ge(p_["sld"][par], 16 * (i + 1))
                if late(s, 2):
                    act.wait_ge(s_["sh_g"], 4 * (s - 1))
                nc.scalar.activation(sx_p[par][0][:, :, :], x3t[par][:, :, :], ACT.Copy).then_inc(s_["sx_hi"], 1)

            def act_hi(s, par, j):
                act.wait_ge(s_["sh_f"], 4 * s + j + 1)
                nc.scalar.activation(act_p[par][0][:, j, :], act_p[par][2][:, j, :], ACT.Copy).then_inc(s_["sh_hi"], 1)

            def sh_up(s, par):
                for j in range(4):
                    act.wait_ge(s_["sh_g"], 4 * s + j + 1)
                    if late(s, 1):
                        act.wait_ge(s_["sh_f"], 4 * s - 4 + j + 1)
                    nc.scalar.activation(sg[j], two(bank[j])[:, 0, :], ACT.Silu).then_inc(s_["sh_silu"], 1)
                    if j:
                        act_hi(s, par, j - 1)
                act_hi(s, par, 3)

            def split_hi(hi, x):
                nc.scalar.activation(hi, x, ACT.Copy).then_inc(s_["w_hi"], 1)

            def step(k, i, par, f, m, b):
                if f:
                    act.wait_ge(s_["pe_zt"], k + 1)
                    if late(k, 1):
                        act.wait_ge(s_["pe_v"], k)
                    for c in range(KC):
                        ins = nc.scalar.activation(x1_x[:, c, :], two(R0)[:, c, :], ACT.Identity,
                                                   bias=ln1b_c[:, c:c + 1], scale=ln1s_c[:, c:c + 1])
                    ins.then_inc(s_["x1x_done"], 1)
                    act.wait_ge(s_["x1x_done"], k + 1)
                    nc.scalar.activation(x1_h[:, :, :], x1_x[:, :, :], ACT.Copy).then_inc(s_["x1t_done"], 1)
                    act.wait_ge(s_["qt_done"], k + 1)
                    if late(k, 1):
                        act.wait_ge(s_["expanded"], 128 * k)
                    nc.scalar.activation(q_h[:, :, :], qt[:, :, :], ACT.Copy).then_inc(s_["qh_done"], 1)
                    if not late(k, 1):
                        act.wait_ge(s_["w_load"], 16 * W_LOADS)
                        split_hi(wo_p[0][:, :, :], wo_raw[:, :, :])
                if m:
                    if not late(k, 2):
                        act.wait_ge(s_["w_load"], 16 * W_LOADS)
                    act.wait_ge(s_["pe_y2t"], k)
                    if late(k, 2):
                        act.wait_ge(s_["pe_w1"], 4 * (k - 1))
                    for c in range(KC):
                        ins = nc.scalar.activation(y2_x[:, c, :], two(R1)[:, c, :], ACT.Identity,
                                                   bias=ln2b_c[:, c:c + 1], scale=ln2s_c[:, c:c + 1])
                    ins.then_inc(s_["y2x_done"], 1)
                    act.wait_ge(s_["y2x_done"], k)
                    nc.scalar.activation(y2_h[:, :, :], y2_x[:, :, :], ACT.Copy).then_inc(s_["y2t_done"], 1)
                if f:
                    act.wait_ge(s_["pe_kt"], k + 1)
                    if late(k, 1):
                        act.wait_ge(s_["pe_sc"], 8 * k)
                    nc.scalar.activation(kt_h[:, :, :], two(R2), ACT.Copy).then_inc(s_["kt_done"], 1)
                    if not late(k, 1):
                        split_hi(w1_p[0][:, :, :], w1_raw[:, :, :])
                        split_hi(w2_p[0][:, :, :], w2_raw[:, :, :])
                if m:
                    if late(k, 2):
                        act.wait_ge(s_["pe_w2"], k - 1)
                    for j in range(4):
                        act.wait_ge(s_["pe_w1"], 4 * (k - 1) + j + 1)
                        for c in range(2):
                            n = 2 * j + c
                            ins = nc.scalar.activation(ht_x[:, n, :], two((R0, R1, R2, R0)[j])[:, c, :],
                                                       ACT.Gelu_apprx_tanh, bias=b1_c[:, n:n + 1])
                        ins.then_inc(s_["gelu"], 1)
                        act.wait_ge(s_["gelu"], 4 * (k - 1) + j + 1)
                        nc.scalar.activation(ht_h[:, 2 * j:2 * j + 2, :], ht_x[:, 2 * j:2 * j + 2, :],
                                             ACT.Copy).then_inc(s_["hth_done"], 1)
                def o_copy(u):
                    act.wait_ge(s_["pe_av"], 8 * k + 4 * (u + 1))
                    if late(k, 1):
                        act.wait_ge(s_["pe_otr"], 2 * k)
                    nc.scalar.activation(ot[u][:, :, :].rearrange("p a n -> p (a n)"), (X, Y)[u][:, :],
                                         ACT.Copy).then_inc(s_["o_done"], 1)

                if b and not f and not m:
                    x3_hi(0, 0, 0)
                    sh_up(0, 0)
                if f:
                    o_copy(0)
                if b:
                    act.wait_ge(s_["pe_x3t"], k - 2 + 1)
                    if late(k, 4):
                        act.wait_ge(p_["xt_s"][par], 16 * (i - 1))
                        act.wait_ge(s_["pe_log"], k - 3)
                    nc.scalar.activation(x3t[par][:, :, :], two(R1 if m else Y), ACT.Copy).then_inc(s_["x3t_done"], 1)
                if f:
                    o_copy(1)
                    act.wait_ge(s_["pe_att"], k + 1)
                    if late(k, 1):
                        act.wait_ge(s_["pe_wo"], k)
                    nc.scalar.activation(att_h[:, :, :], two(R1), ACT.Copy).then_inc(s_["att_done"], 1)

            act.wait_ge(s_["c_load"], 16 * C_LOADS)
            act.wait_ge(s_["pool_c"], 4)
            split_hi(wqkv[0][:, :, :], wqkv_raw[:, :, :])
            for k in range(4):
                step(k, k // 2, k % 2, True, k >= 1, k >= 2)
                if k == 3:
                    act.wait_ge(s_["sh_w"], 32)
                    split_hi(sgu[0][:, :, :, :], sgu_raw[:, :, :, :])
            with act.Fori(2, NS // 2) as i:
                for par in range(2):
                    step(2 * i + par, i, par, True, True, True)
            step(NS, NS // 2, 0, False, True, True)
            step(NS + 1, NS // 2, 1, False, False, True)

            act.wait_ge(s_["route"], 1)
            nc.scalar.activation(score[:, :], top, ACT.Sigmoid).then_inc(s_["route_act"], 1)

            def sh_down(s, i, par):
                act.wait_ge(s_["sh_down"], s + 1)
                if late(i, 1):
                    act.wait_ge(p_["yst"][par], 16 * i)
                nc.scalar.activation(ysh[par][:, :, :], two(bank[4 + par]), ACT.Copy).then_inc(s_["sh_y"], 1)

            x3_hi(1, 0, 1)
            act.wait_ge(s_["sh_w"], 48)
            split_hi(sd[0][:, :, :], sd_raw[:, :, :])
            x3_hi(2, 1, 0)
            sh_up(1, 1)
            sh_down(0, 0, 0)
            x3_hi(3, 1, 1)
            sh_up(2, 0)
            sh_down(1, 0, 1)
            with act.Fori(1, NA // 2 - 1) as i:
                for par in range(2):
                    x3_hi(2 * i + par + 2, i + 1, par)
                    sh_up(2 * i + par + 1, 1 - par)
                    sh_down(2 * i + par, i, par)
            x3_hi(NA, NA // 2, 0)
            sh_up(NA - 1, 1)
            sh_down(NA - 2, NA // 2 - 1, 0)
            sh_up(NA, 0)
            sh_down(NA - 1, NA // 2 - 1, 1)

            def r_xt(t, par):
                act.wait_ge(s_["r_t"], t + 1)
                if late(t, 2):
                    act.wait_ge(s_["r_gu"], t - 1)
                nc.scalar.activation(xst[par], bank[6 + par][:, 0:2 * P].rearrange("p (c n) -> p c n", c=KC),
                                     ACT.Copy).then_inc(s_["r_xt"], 1)

            def r_silu(t, par):
                act.wait_ge(s_["r_gu"], t + 1)
                if late(t, 2):
                    act.wait_ge(s_["r_act"], t - 1)
                nc.scalar.activation(sgr[par], bank[par * 2][:, :], ACT.Silu).then_inc(s_["r_silu"], 1)

            def r_y(t, i, par):
                act.wait_ge(s_["r_dn"], t + 1)
                if late(i, 1):
                    act.wait_ge(p_["rst"][par], 16 * i)
                nc.scalar.activation(y_r[par], bank[5][:, 0:D], ACT.Copy).then_inc(s_["r_y"], 1)

            r_xt(0, 0)
            r_xt(1, 1)
            r_silu(0, 0)
            with act.Fori(1, (NRT - 1) // 2) as i:
                for par in range(2):
                    r_xt(2 * i + par, par)
                    r_silu(2 * i + par - 1, 1 - par)
                    r_y(2 * i + par - 2, i - 1, par)
            r_xt(NRT - 1, 0)
            r_silu(NRT - 2, 1)
            r_y(NRT - 3, NRT // 2 - 1, 0)
            r_silu(NRT - 1, 0)
            r_y(NRT - 2, NRT // 2 - 1, 1)
            r_y(NRT - 1, NRT // 2, 0)

            x3_hi(NA + 1, NA // 2, 1)
            x3_hi(NA + 2, NA // 2 + 1, 0)
            sh_up(NA + 1, 1)
            with act.Fori(NA // 2 + 1, NS // 2 - 1) as i:
                for par in range(2):
                    x3_hi(2 * i + par + 1, i + par, 1 - par)
                    sh_up(2 * i + par, par)
            x3_hi(NS - 1, NS // 2 - 1, 1)
            sh_up(NS - 2, 0)
            sh_up(NS - 1, 1)

        @block.vector
        def _(dve):
            def stats(c, which, src):
                raw_stats(c, which, src)
                mean_var(c, which)

            def raw_stats(c, which, src):
                bs = lns[which][0]
                for u in range(2):
                    c.did(nc.vector.bn_stats(bs[:, u, :], src[:, u, :]))

            def mean_var(c, which):
                bs, mv, _, _ = lns[which]
                hold(dve, c.sem, c.base + c.n)
                for u in range(2):
                    c.did(nc.vector.bn_aggr(mv[:, u, :], bs[:, u, :]))

            def normalise(c, which, dst, src):
                _, mv, _, r = lns[which]
                for u in range(2):
                    c.did(nc.vector.tensor_scalar(dst[:, u, :], src[:, u, :], mv[:, u, 0:1], r[:, u:u + 1],
                                                  ALU.subtract, ALU.mult))

            def in_stats(k, i, par):
                c = Chain(dve, s_["lnx"], 6, k)
                dve.wait_ge(p_["xin_ld"][par], 16 * (i + 1))
                if late(k, 1):
                    dve.wait_ge(s_["rs_x"], 2 * k)
                stats(c, "x", xin[par])
                return c

            def in_norm(c, k, par):
                dve.wait_ge(s_["rs_x"], 2 * k + 2)
                if late(k, 2):
                    dve.wait_ge(s_["lna"], 7 * (k - 2) + 1)
                normalise(c, "x", xn[par], xin[par])
                c.settle()
                c = Chain(dve, s_["lnn"], 6, k)
                if late(k, 1):
                    dve.wait_ge(s_["rs_n"], 2 * k)
                stats(c, "n", xn[par])
                return c

            def in_z(c, k, par):
                dve.wait_ge(s_["rs_n"], 2 * k + 2)
                if late(k, 1):
                    dve.wait_ge(s_["pe_zt"], k)
                normalise(c, "n", z, xn[par])

            def end_x3(k, par):
                c = Chain(dve, s_["lny"], 14, k)
                dve.wait_ge(s_["pe_w2"], k + 1)
                dve.wait_ge(s_["x2b_done"], k + 1)
                if late(k, 1):
                    dve.wait_ge(s_["rs_y"], 2 * k)
                c.did(nc.vector.tensor_tensor(x3[:, :, :], two(X), x2b[par][:, :, :], ALU.add))

            def end_stats(k):
                c = Chain(dve, s_["lny"], 14, k)
                c.n = 1
                c.settle()
                stats(c, "y", x3)

            def end_h(k):
                c = Chain(dve, s_["lny"], 14, k)
                c.n = 5
                dve.wait_ge(s_["rs_y"], 2 * k + 2)
                normalise(c, "y", x3, x3)
                return c

            def end_sum(c, k, i, par):
                c.settle()
                dve.wait_ge(s_["xr_ld"], 16 * (k + 1))
                if not late(k, 1):
                    dve.wait_ge(s_["zeroed"], 49)
                if late(k, 2):
                    dve.wait_ge(p_["h_s"][par], 16 * i)
                    dve.wait_ge(s_["rs_h"], 2 * k)
                c.did(nc.vector.tensor_tensor(hh[par][:, :, :], x3[:, :, :], xr[:, :, :], ALU.add))

            def end_xm(c, k, i, par):
                dve.wait_ge(s_["rs_h"], 2 * k + 2)
                if late(k, 2):
                    dve.wait_ge(p_["xm_s"][par], 16 * i)
                    dve.wait_ge(s_["pe_x3t"], k - 1)
                normalise(c, "h", xm[par], hh[par])

            def state(k, u):
                c = Chain(dve, s_["state"], 2, 2 * k + u)
                dve.wait_ge(s_["pe_u"], 2 * k + u + 1)
                c.did(nc.vector.tensor_tensor(su[:, :, :, :], sx[u][:, :, :, 0:VU],
                                              U[:, 0:2 * 8 * VU].rearrange("p (g h n) -> p g h n", g=2, h=8), ALU.add))
                c.settle()
                if late(k, 1) or u:
                    dve.wait_ge(s_["pe_av"], 8 * k + 4 * u)
                for g in range(2):
                    dst = sx[1 - u][:, g, :, 0:VU]
                    if u:
                        ins = nc.vector.scalar_tensor_tensor(out=dst, in0=su[:, g, :, :],
                                                             scalar=cs[:, bass.ds(C_KEEP + k, 1)], in1=block_mask,
                                                             op0=ALU.mult, op1=ALU.mult)
                    else:
                        ins = nc.vector.tensor_tensor(dst, su[:, g, :, :], block_mask, ALU.mult)
                c.did(ins)

            def mask(k, j):
                dve.wait_ge(s_["pe_sc"], 8 * k + j + 1)
                if late(k, 1) or j >= 4:
                    dve.wait_ge(s_["pe_av"], 8 * k + j - 3)
                nc.vector.tensor_tensor(st[j % 4][:, :, :], (S0, S1)[j % 2][:, :].rearrange("p (h n) -> p h n", h=G),
                                        causal.rearrange("p (a n) -> p a n", a=1).to_broadcast([P, G, P]),
                                        ALU.mult).then_inc(s_["masks"], 1)

            def norm(k, u):
                c = Chain(dve, s_["norm"], 2, 2 * k + u)
                if late(k, 1) or u:
                    c.settle()
                dve.wait_ge(s_["pe_otr"], 2 * k + u + 1)
                o = (R2, R0)[u][:, :].rearrange("p (h n) -> p h n", h=H)
                c.did(nc.vector.reciprocal(rden[:, :], o[:, :, DH]))
                c.settle()
                if late(k, 1):
                    dve.wait_ge(s_["pe_att"], k)
                c.did(nc.vector.tensor_tensor(av[:, u, :].rearrange("p (h m) -> p h m", h=H), o[:, :, 0:DH],
                                              rden[:, :].rearrange("p (h a) -> p h a", a=1).to_broadcast([P, H, DH]),
                                              ALU.mult))

            def mid(k, par):
                c = Chain(dve, s_["lna"], 7, k)
                dve.wait_ge(s_["pe_wo"], k + 1)
                if late(k, 1):
                    dve.wait_ge(s_["x2b_done"], k)
                    dve.wait_ge(s_["rs_a"], 2 * k)
                c.did(nc.vector.tensor_tensor(x2[:, :, :], two(R2), xn[par][:, :, :], ALU.add))
                c.settle()
                stats(c, "a", x2)
                return c

            def mid_z(c, k):
                dve.wait_ge(s_["rs_a"], 2 * k + 2)
                if late(k, 1):
                    dve.wait_ge(s_["pe_y2t"], k)
                normalise(c, "a", z2, x2)

            def lo(dst, src, hi, done, n, sm):
                dve.wait_ge(s_[done], n)
                src = src if dst is kt_l or dst is att_l else src[:, :, :]
                nc.vector.tensor_tensor(dst[:, :, :], src, hi[:, :, :].bitcast(F32), ALU.subtract).then_inc(s_[sm], 1)

            def split_lo(w, raw, n):
                dve.wait_ge(s_["w_hi"], n)
                nc.vector.tensor_tensor(w[1][:, :, :], raw[:, :, :], w[0][:, :, :].bitcast(F32), ALU.subtract).then_inc(s_["w_lo"], 1)

            def q(k):
                dve.wait_ge(s_["pe_q"], k + 1)
                if late(k, 1):
                    dve.wait_ge(s_["pe_av"], 8 * k)
                nc.vector.tensor_scalar(qt[:, :, :], two(R1), 0.0, KERNEL_EPS, ALU.max, ALU.add).then_inc(s_["qt_done"], 1)

            def q_lo(k):
                lo(q_l, qt, q_h, "qh_done", k + 1, "ql_done")

            def step(k, i, par, f, m, b, ahead):
                if f:
                    dve.wait_ge(s_["pe_k"], k + 1)
                    if late(k, 1):
                        dve.wait_ge(s_["pe_u"], 2 * k)
                    nc.vector.tensor_scalar(kk[:, :, :], two(R2), 0.0, KERNEL_EPS, ALU.max, ALU.add).then_inc(s_["kk_done"], 1)
                    dve.wait_ge(s_["pe_v"], k + 1)
                    nc.vector.tensor_copy(vx[:, :, :, 0:DH],
                                          R0[:, :].rearrange("p (u h m) -> p u h m", u=2, h=H)).then_inc(s_["vx_done"], 1)
                if m:
                    lo(y2_l, y2_x, y2_h, "y2t_done", k, "y2l_done")
                    if not late(k, 2):
                        split_lo(w2_p, w2_raw, 4)
                if f:
                    lo(kt_l, two(R2), kt_h, "kt_done", k + 1, "kl_done")
                    state(k, 0)
                if b:
                    end_x3(k - 2, par)
                if ahead:
                    ca = in_stats(k + 1, i + par, 1 - par)
                if b:
                    end_stats(k - 2)
                if b and not f and not m:
                    x3_lo(0, 0)
                if b:
                    cb = end_h(k - 2)

                ENDS = (2, 3, 4, 6)

                def end(n):
                    if not b:
                        return
                    if n == 0:
                        end_sum(cb, k - 2, i - 1, par)
                    elif n == 1:
                        cb.settle()
                        raw_stats(cb, "h", hh[par])
                    elif n == 2:
                        mean_var(cb, "h")
                    else:
                        end_xm(cb, k - 2, i - 1, par)

                if not late(k, 1):
                    split_lo(wo_p, wo_raw, 2)
                    ca = in_norm(ca, k + 1, 1 - par)
                    in_z(ca, k + 1, 1 - par)
                if f:
                    mask(k, 0)
                    mask(k, 1)
                def turn_logits():
                    dve.wait_ge(s_["pe_log"], k - 1)
                    if late(k, 3):
                        dve.wait_ge(s_["pe_lt"], k - 2)
                    dve.wait_ge(s_["pe_wo"], k if f else NS)
                    nc.vector.tensor_copy(lt, (R1 if m else Y)[0:E, 0:STEP]).then_inc(s_["lt_done"], 1)

                def keep_logits():
                    dve.wait_ge(s_["pe_lt"], k - 1)
                    nc.vector.tensor_copy(logit[:, bass.ds(2 * (k - 2), 2), :],
                                          U[:, LG:LG + 2 * E].rearrange("p (u e) -> p u e", u=2)).then_inc(s_["logit_done"], 1)

                if not f:
                    for n in range(4):
                        end(n)
                    if not m:
                        sh_act(0, 0)
                        sh_act_lo(0, 0, 3)
                if b and not f:
                    turn_logits()
                    keep_logits()
                if f:
                    for j in range(2, 8):
                        if j in ENDS:
                            end(ENDS.index(j))
                        mask(k, j)
                    state(k, 1)
                    if b:
                        turn_logits()
                    if ahead and late(k, 1):
                        ca = in_norm(ca, k + 1, 1 - par)
                    norm(k, 0)
                    if ahead and late(k, 1):
                        in_z(ca, k + 1, 1 - par)
                    if b:
                        keep_logits()
                    norm(k, 1)
                    lo(att_l, two(R1), att_h, "att_done", k + 1, "al_done")
                if ahead:
                    lo(x1_l, x1_x, x1_h, "x1t_done", k + 2, "x1l_done")
                if f:
                    cm = mid(k, par)
                if ahead:
                    q(k + 1)
                if f:
                    mid_z(cm, k)
                if ahead:
                    q_lo(k + 1)

            dve.wait_ge(s_["pool_c"], 4)
            ca = in_norm(in_stats(0, 0, 0), 0, 0)
            in_z(ca, 0, 0)
            def x3_lo(s, par):
                dve.wait_ge(s_["sx_hi"], s + 1)
                nc.vector.tensor_tensor(sx_p[par][1][:, :, :], x3t[par][:, :, :], sx_p[par][0][:, :, :].bitcast(F32),
                                        ALU.subtract).then_inc(s_["sx_lo"], 1)

            def sh_act_lo(s, par, j):
                dve.wait_ge(s_["sh_hi"], 4 * s + j + 1)
                nc.vector.tensor_tensor(act_p[par][1][:, j, :], act_p[par][2][:, j, :], act_p[par][0][:, j, :].bitcast(F32),
                                        ALU.subtract).then_inc(s_["sh_lo"], 1)

            def sh_act(s, par, js=range(4)):
                if late(s, 2):
                    dve.wait_ge(s_["sh_down"], s - 1)
                for j in js:
                    dve.wait_ge(s_["sh_silu"], 4 * s + j + 1)
                    nc.vector.tensor_tensor(act_p[par][2][:, j, :], sg[j], two(bank[j])[:, 1, :],
                                            ALU.mult).then_inc(s_["sh_f"], 1)
                    if j:
                        sh_act_lo(s, par, j - 1)

            dve.wait_ge(s_["c_load"], 16 * C_LOADS)
            split_lo(wqkv, wqkv_raw, 1)
            lo(x1_l, x1_x, x1_h, "x1t_done", 1, "x1l_done")
            q(0)
            q_lo(0)
            dve.wait_ge(s_["pool_c"], 4)
            for k in range(4):
                step(k, k // 2, k % 2, True, k >= 1, k >= 2, True)
                if k == 0:
                    split_lo(w1_p, w1_raw, 3)
                if k == 3:
                    dve.wait_ge(s_["w_hi"], 5)
                    nc.vector.tensor_tensor(sgu[1][:, :, :, :], sgu_raw[:, :, :, :], sgu[0][:, :, :, :].bitcast(F32),
                                            ALU.subtract).then_inc(s_["w_lo"], 1)
            with dve.Fori(2, NS // 2 - 1) as i:
                for par in range(2):
                    step(2 * i + par, i, par, True, True, True, True)
            for k in range(NS - 2, NS):
                step(k, k // 2, k % 2, True, True, True, k + 1 < NS)
            step(NS, NS // 2, 0, False, True, True, False)
            step(NS + 1, NS // 2, 1, False, False, True, False)

            def scale(s, i, n, loads):
                par = n % 2
                dve.wait_ge(p_["xsl"][par], 16 * loads)
                if late(i, 1):
                    dve.wait_ge(sct[n], 32 * i)
                for u in range(2):
                    nc.vector.tensor_scalar(xrow[n][:, u, 0:D], xn[par][:, u, :], score[:, bass.ds(2 * s + u, 1)], None,
                                            ALU.mult)
                    nc.vector.tensor_copy(xrow[n][:, u, D:DX], cs[:, bass.ds(C_TOKEN + 2 * s + u, 1)]).then_inc(s_["sc_sc"], 1)
                    nc.vector.tensor_copy(idx[n][:, u:u + 1], slot[:, bass.ds(2 * s + u, 1)]).then_inc(s_["sc_sc"], 1)

            c = Chain(dve, s_["route"], 0, 0)

            def do(ins):
                c.did(ins)
                c.settle()

            def over_e(a):
                return a.rearrange("p (t a) -> p t a", a=1).to_broadcast([P, NT, E])

            def over_t(a):
                return a.rearrange("p (a e) -> p a e", a=1).to_broadcast([P, NT, E])

            r0, r1, r2, r3 = (r[:, :, :] for r in rt)
            dve.wait_ge(s_["logit_done"], NS)
            do(nc.vector.tensor_reduce(top, logit[:, :, :], AX.X, ALU.max))
            do(nc.vector.tensor_tensor(r1, logit[:, :, :], over_e(top), ALU.is_equal))
            do(nc.vector.tensor_tensor(r1, r1, over_t(erev), ALU.mult))
            do(nc.vector.tensor_reduce(rm, r1, AX.X, ALU.max))
            do(nc.vector.tensor_tensor(r0, r1, over_e(rm), ALU.is_equal))
            assert c.n == 5
            dve.wait_ge(s_["route_pe"], 1)
            rank = bank[6][:, 0:NT * E].rearrange("p (t e) -> p t e", t=NT)
            total = bank[6][:, NT * E:2 * NT * E].rearrange("p (t e) -> p t e", t=NT)
            do(nc.vector.tensor_copy(r1, total))
            x3_lo(1, 1)
            src, dst = rt[1], rt[2]
            d = 1
            while d < NT:
                nc.vector.tensor_copy(dst[:, 0:d, :], src[:, 0:d, :])
                do(nc.vector.tensor_tensor(dst[:, d:, :], src[:, d:, :], src[:, 0:NT - d, :], ALU.add))
                src, dst = dst, src
                d *= 2
            upto = src[:, :, :]
            do(nc.vector.tensor_scalar(cnt_i[:, :], src[:, NT - 1, :], float(P - 1), None, ALU.add))
            do(nc.vector.tensor_scalar(cnt_i[:, :], cnt_i[:, :], 7, None, ALU.logical_shift_right))
            do(nc.vector.tensor_copy(cnt[0][:, :], cnt_i[:, :]))
            a, b_ = cnt[1], cnt[2]
            do(nc.vector.tensor_copy(a[:, :], cnt[0][:, :]))
            d = 1
            while d < E:
                nc.vector.tensor_copy(b_[:, 0:d], a[:, 0:d])
                do(nc.vector.tensor_tensor(b_[:, d:], a[:, d:], a[:, 0:E - d], ALU.add))
                a, b_ = b_, a
                d *= 2
            do(nc.vector.tensor_tensor(cnt[3][:, :], a[:, :], cnt[0][:, :], ALU.subtract))
            do(nc.vector.tensor_scalar(cnt[3][:, :], cnt[3][:, :], float(P), None, ALU.mult))
            do(nc.vector.tensor_tensor(r3, upto, total, ALU.subtract))
            do(nc.vector.tensor_tensor(r3, r3, rank, ALU.add))
            do(nc.vector.tensor_tensor(r3, r3, over_t(cnt[3][:, :]), ALU.add))
            do(nc.vector.tensor_tensor(r3, r3, r0, ALU.mult))
            do(nc.vector.tensor_reduce(rm, r3, AX.X, ALU.add))
            do(nc.vector.tensor_copy(slot[:, :], rm))
            dve.wait_ge(s_["route_act"], 1)
            scale(0, 0, 0, 1)
            scale(1, 0, 1, 1)
            split_lo(sd, sd_raw, 6)
            dve.wait_ge(s_["tnum_ld"], 16)
            do(nc.vector.tensor_tensor(tcmp, tnum,
                                       a[0:1, 0:E - 1].rearrange("p (a e) -> p a e", a=1).to_broadcast([1, NRT, E - 1]),
                                       ALU.is_ge))
            do(nc.vector.tensor_reduce(eid_f, tcmp, AX.X, ALU.add))
            nc.vector.tensor_copy(eid[:, :], eid_f).then_inc(s_["eid_done"], 1)
            scale(2, 0, 2, 2)
            scale(3, 0, 3, 2)
            sh_act(1, 1)
            x3_lo(2, 0)
            sh_act_lo(1, 1, 3)
            with dve.Fori(1, NA // 2) as i:
                for par in range(2):
                    s = 2 * i + par
                    x3_lo(s + 1, 1 - par)
                    for v in range(2):
                        sh_act(s, par, range(2 * v, 2 * v + 2))
                        if v:
                            sh_act_lo(s, par, 3)
                        scale(2 * s + v, i, 2 * par + v, s + 1)

            sh_act(NA, 0)
            sh_act_lo(NA, 0, 3)

            def r_att(t, par):
                dve.wait_ge(s_["r_at"], t + 1)
                if late(t, 2):
                    dve.wait_ge(s_["r_dn"], t - 1)
                nc.vector.tensor_copy(att_r[par][:, :, :], bank[4][:, :].rearrange("p (c n) -> p c n", c=4)).then_inc(s_["r_att"], 1)

            def r_act(t, par):
                dve.wait_ge(s_["r_silu"], t + 1)
                if late(t, 2):
                    dve.wait_ge(s_["r_at"], t - 1)
                nc.vector.tensor_tensor(act_r[par], sgr[par], bank[2 * par + 1][:, :], ALU.mult).then_inc(s_["r_act"], 1)

            def numbers(t, par):
                number = xs_t[par][:, D:DX]
                dve.wait_ge(s_["r_t"], t + 1)
                nc.vector.scalar_tensor_tensor(out=rid_a[:, bass.ds(t, 1)], in0=number, scalar=0.0,
                                               in1=cs[:, bass.ds(C_SLOT + t, 1)],
                                               op0=ALU.is_equal, op1=ALU.mult).then_inc(s_["rid_f"], 1)
                dve.wait_ge(s_["rid_f"], t + 1)
                nc.vector.scalar_tensor_tensor(out=rid[:, bass.ds(t, 1)], in0=rid_a[:, bass.ds(t, 1)], scalar=-1.0, in1=number,
                                               op0=ALU.add, op1=ALU.add).then_inc(s_["rid"], 1)

            def put_numbers(t, i, par):
                if late(i, 1):
                    dve.wait_ge(p_["rst"][par], 16 * i)
                nc.vector.tensor_copy(idx_r[par][:, :], rid[:, bass.ds(t, 1)]).then_inc(s_["idx_r"], 1)

            numbers(0, 0)
            numbers(1, 1)
            for par in range(2):
                dve.wait_ge(p_["yst"][par], 16 * (NA // 2))
            r_act(0, 0)
            numbers(2, 0)
            r_att(0, 0)
            put_numbers(0, 0, 0)
            r_act(1, 1)
            numbers(3, 1)
            r_att(1, 1)
            put_numbers(1, 0, 1)
            r_act(2, 0)
            with dve.Fori(2, (NRT - 1) // 2) as i:
                for par in range(2):
                    numbers(2 * i + par, par)
                    r_att(2 * i + par - 2, par)
                    put_numbers(2 * i + par - 2, i - 1, par)
                    r_act(2 * i + par - 1, 1 - par)
            numbers(NRT - 1, (NRT - 1) % 2)
            for t in (NRT - 3, NRT - 2):
                r_att(t, t % 2)
                put_numbers(t, t // 2, t % 2)
                r_act(t + 1, 1 - t % 2)
            r_att(NRT - 1, (NRT - 1) % 2)
            put_numbers(NRT - 1, NRT // 2, (NRT - 1) % 2)

            def fin_sum(v, j, par, more):
                c = Chain(dve, p_["fsum"][v], 5, j)
                if v:
                    dve.wait_ge(s_["sh_down"], NA + j + 1)
                    shared = two(bank[4 + par])
                else:
                    dve.wait_ge(s_["ysh_ld"], 16 * (j + 1))
                    shared = xin[0][:, :, :]
                dve.wait_ge(p_["gat"][v], 16 * (j + 1))
                if late(j, 1):
                    dve.wait_ge(p_["fadd"][v], j)
                    dve.wait_ge(p_["frs"][v], 2 * j)
                c.did(nc.vector.tensor_tensor(f3[v][:, :, :], shared, xn[v][:, :, :], ALU.add))
                c.settle()
                stats(c, "xn"[v], f3[v])

            def fin_out(v, j):
                c = Chain(dve, p_["fout"][v], 2, j)
                dve.wait_ge(p_["frs"][v], 2 * j + 2)
                normalise(c, "xn"[v], f3[v], f3[v])

            def last_step(j, par, acts, more):
                def part(n):
                    if acts:
                        sh_act(NA + j + 1, 1 - par, (n,))

                if acts and more != "last":
                    x3_lo(NA + j + 2, par)
                part(0)
                fin_sum(0, j, par, more)
                part(1)
                if late(j, 1):
                    fin_sum(1, j - 1, 1 - par, True)
                part(2)
                fin_out(0, j)
                part(3)
                if acts:
                    sh_act_lo(NA + j + 1, 1 - par, 3)
                if late(j, 1):
                    fin_out(1, j - 1)

            x3_lo(NA + 1, 1)
            last_step(0, 0, True, True)
            last_step(1, 1, True, True)
            with dve.Fori(1, NA // 2 - 1) as i:
                for par in range(2):
                    last_step(2 * i + par, par, True, True)
            last_step(NA - 2, 0, True, "last")
            last_step(NA - 1, 1, False, False)
            fin_sum(1, NA - 1, 1, False)
            fin_out(1, NA - 1)

        @block.tensor
        def _(pe):
            mm = nc.tensor.matmul

            def mm3(dst, a, b, start=True, stop=True):
                mm(dst, a[0], b[0], start=start, stop=False)
                mm(dst, a[1], b[0], start=False, stop=False)
                return mm(dst, a[0], b[1], start=False, stop=stop)

            def both(p, *ix):
                return p[0][(slice(None),) + ix], p[1][(slice(None),) + ix]

            def tok(u):
                return slice(u * P, (u + 1) * P)

            x1, y2, ht, kt, att = (x1_h, x1_l), (y2_h, y2_l), (ht_h, ht_l), (kt_h, kt_l), (att_h, att_l)
            every = slice(None)

            def tile(a, c, u):
                return a[:, c, u * P:(u + 1) * P]

            def score(k, j):
                u, q = divmod(j, 4)
                g = q // 2
                if late(k, 1) or j >= 2:
                    pe.wait_ge(s_["masks"], 8 * k + j - 1)
                mm3((S0, S1)[j % 2][:, :], both(kt, g, tok(u)),
                    [qx[:, a, g, u, 4 * (q % 2):4 * (q % 2) + 4, :].rearrange("p h n -> p (h n)") for a in range(2)]
                    ).then_inc(s_["pe_sc"], 1)

            def attend(k, j, b):
                u, q = divmod(j, 4)
                o = (X, Y)[u]
                if q == 0:
                    pe.wait_ge(s_["state"], 2 * (2 * k + u)) if late(k, 1) or u else pe.wait_ge(s_["pool_c"], 4)
                    if u == 0:
                        if b:
                            pe.wait_ge(s_["lny"], 14 * (k - 2) + 1)
                        elif late(k, 1):
                            pe.wait_ge(s_["o_done"], 2 * k - 1)
                    else:
                        if late(k, 1):
                            pe.wait_ge(s_["o_done"], 2 * k)
                pe.wait_ge(s_["masks"], 8 * k + j + 1)
                g = q // 2
                mm(o[:, q * P:(q + 1) * P], sx[u][:, g, 4 * (q % 2):4 * (q % 2) + 4, :].rearrange("p h n -> p (h n)"),
                   tile(qt, g, u), start=True, stop=False, skip_group_check=True)
                for h in range(G):
                    ins = mm(o[h * VW:(h + 1) * VW, q * P:(q + 1) * P], vx[:, u, 4 * q + h, :], st[j % 4][:, h, :],
                             start=False, stop=True, skip_group_check=True)
                ins.then_inc(s_["pe_av"], 1)

            def update(k, u, b):
                if b and not u and late(k, 3):
                    pe.wait_ge(s_["logit_done"], k - 2)
                if late(k, 1) or u:
                    pe.wait_ge(s_["state"], 2 * (2 * k + u) - 1)
                for g in range(2):
                    ins = mm(U[:, g * 8 * VU:(g + 1) * 8 * VU], kk[:, u, g * P:(g + 1) * P],
                             vx[:, u, 8 * g:8 * g + 8, 0:VU], start=True, stop=True, skip_group_check=True)
                ins.then_inc(s_["pe_u"], 1)

            def turn(dst, src):
                for c in range(2):
                    for u in range(2):
                        ins = nc.tensor.transpose(dst[:, c, u * P:(u + 1) * P], src[:, u, c * P:(c + 1) * P], ident)
                return ins

            def otr(k, u, m):
                pe.wait_ge(s_["o_done"], 2 * k + u + 1)
                if m:
                    pe.wait_ge(s_["gelu"], 4 * (k - 1) + 3 + u)
                for q in range(4):
                    ins = nc.tensor.transpose((R2, R0)[u][:, q * P:(q + 1) * P], ot[u][:, q, :], ident)
                ins.then_inc(s_["pe_otr"], 1)

            def logits_turn(k):
                hold(pe, s_["lt_done"], k - 1)
                for u in range(2):
                    ins = nc.tensor.transpose(U[:, LG + u * E:LG + (u + 1) * E], lt[:, u * P:(u + 1) * P], ident[0:E, 0:E])
                ins.then_inc(s_["pe_lt"], 1)

            TAIL = 6

            def w2_part(u, blocks):
                for n in blocks:
                    ins = mm3(two(X)[:, u, :], both(ht, n, tok(u)), both(w2_p, n, every), n == 0, n == MLP // P - 1)
                return ins

            def z_turn(k):
                pe.wait_ge(s_["lnn"], 6 * (k + 1))
                if late(k, 1):
                    pe.wait_ge(s_["norm"], 4 * k)
                turn(two(R0), z).then_inc(s_["pe_zt"], 1)

            def kv(n, bk, u):
                for c in range(KC):
                    ins = mm3(two(bk)[:, u, :], both(x1, c, tok(u)), both(wqkv, c, slice(n * D, (n + 1) * D)),
                              c == 0, c == KC - 1)
                return ins

            def sh_gate(s, i, par):
                pe.wait_ge(s_["sx_lo"], s + 1)
                for j in range(4):
                    if late(s, 1):
                        pe.wait_ge(s_["sh_f"], 4 * s - 4 + j + 1)
                    for a in range(2):
                        for c in range(KC):
                            ins = mm3(two(bank[j])[:, a, :], both(sgu, a, c, tok(j)), both(sx_p[par], c, every),
                                      c == 0, c == KC - 1)
                    ins.then_inc(s_["sh_g"], 1)

            def step(k, par, f, m, b, ahead):
                if not late(k, 1):
                    pe.wait_ge(s_["w_lo"], 1)
                if f:
                    pe.wait_ge(s_["x1l_done"], k + 1)
                    if late(k, 1):
                        pe.wait_ge(s_["al_done"], k)
                    for g in range(2):
                        for c in range(KC):
                            ins = mm3(two(R1)[:, g, :], both(wqkv, c, tok(g)), both(x1, c, every), c == 0, c == KC - 1)
                    ins.then_inc(s_["pe_q"], 1)
                    if late(k, 1):
                        pe.wait_ge(s_["lna"], 7 * (k - 1) + 1)
                    kv(1, R2, 0)
                    kv(1, R2, 1).then_inc(s_["pe_k"], 1)
                    kv(2, R0, 0)
                if m:
                    pe.wait_ge(s_["lna"], 7 * k)
                    pe.wait_ge(s_["qt_done"], k + 1) if f else pe.wait_ge(s_["al_done"], k)
                    turn(two(R1), z2).then_inc(s_["pe_y2t"], 1)
                if f:
                    kv(2, R0, 1).then_inc(s_["pe_v"], 1)
                    pe.wait_ge(s_["kk_done"], k + 1)
                    turn(two(R2), kk).then_inc(s_["pe_kt"], 1)
                if b:
                    w2_part(1, range(TAIL, MLP // P)).then_inc(s_["pe_w2"], 1)
                if f:
                    pe.wait_ge(s_["vx_done"], k + 1)
                    update(k, 0, b)
                if m:
                    pe.wait_ge(s_["y2l_done"], k)
                    if not late(k, 2):
                        pe.wait_ge(s_["w_lo"], 3)
                    for j in range(4):
                        if j == 0 and f:
                            pe.wait_ge(s_["vx_done"], k + 1)
                        if j == 2 and f:
                            pe.wait_ge(s_["kl_done"], k + 1)
                        if j == 3:
                            pe.wait_ge(s_["gelu"], 4 * (k - 1) + 1)
                        for a in range(2):
                            n = 2 * j + a
                            for c in range(KC):
                                ins = mm3(two((R0, R1, R2, R0)[j])[:, a, :], both(w1_p, c, tok(n)), both(y2, c, every),
                                          c == 0, c == KC - 1)
                        ins.then_inc(s_["pe_w1"], 1)
                def x3_turn():
                    pe.wait_ge(s_["lny"], 14 * (k - 1))
                    if m:
                        pe.wait_ge(s_["gelu"], 4 * (k - 1) + 2)
                    turn(two(R1 if m else Y), xm[par]).then_inc(s_["pe_x3t"], 1)

                if f:
                    pe.wait_ge(s_["expanded"], 128 * (k + 1))
                    pe.wait_ge(s_["kl_done"], k + 1)
                    score(k, 0)
                    score(k, 1)
                    update(k, 1, b)
                def logits():
                    pe.wait_ge(s_["x3t_done"], k - 1)
                    for c in range(KC):
                        ins = mm((R1 if m else Y)[0:E, 0:STEP], gw_s[:, c, :], x3t[par][:, c, :], start=(c == 0), stop=(c == KC - 1))
                    ins.then_inc(s_["pe_log"], 1)

                if b and not f and not m:
                    sh_gate(0, 0, 0)
                if b and not f:
                    x3_turn()
                    logits()
                    logits_turn(k)
                if f:
                    attend(k, 0, b)
                    for j in range(2, 8):
                        score(k, j)
                        attend(k, j - 1, b)
                        if j == 6 and b:
                            x3_turn()
                        if j == 7 and b:
                            logits()
                    otr(k, 0, m)
                    attend(k, 7, b)
                if m:
                    if f:
                        pe.wait_ge(s_["o_done"], 2 * k + 1)
                    pe.wait_ge(s_["htl_done"], 4 * k)
                    if not late(k, 2):
                        pe.wait_ge(s_["w_lo"], 4)
                    w2_part(0, range(8))
                if f and b:
                    pe.wait_ge(s_["state"], 4 * k + 3)
                    logits_turn(k)
                if f:
                    otr(k, 1, m)
                if m:
                    w2_part(1, range(2 if f else TAIL))
                if f:
                    pe.wait_ge(s_["norm"], 4 * k + 4)
                    if b:
                        pe.wait_ge(s_["x3t_done"], k - 1)
                    turn(two(R1), av).then_inc(s_["pe_att"], 1)
                if ahead:
                    z_turn(k + 1)
                if f and m:
                    w2_part(1, range(2, TAIL))
                if f:
                    pe.wait_ge(s_["al_done"], k + 1)
                    for u in range(2):
                        for c in range(KC):
                            ins = mm3(two(R2)[:, u, :], both(att, c, tok(u)), both(wo_p, c, every), c == 0, c == KC - 1)
                    ins.then_inc(s_["pe_wo"], 1)

            pe.wait_ge(s_["c_load"], 16 * C_LOADS)
            z_turn(0)
            for k in range(4):
                step(k, k % 2, True, k >= 1, k >= 2, True)
            with pe.Fori(2, NS // 2 - 1) as i:
                for par in range(2):
                    step(2 * i + par, par, True, True, True, True)
            step(NS - 2, 0, True, True, True, True)
            step(NS - 1, 1, True, True, True, False)
            step(NS, 0, False, True, True, False)
            step(NS + 1, 1, False, False, True, False)

            def sh_out(s, par, bank_read=None):
                pe.wait_ge(s_["sh_lo"], 4 * s + 4)
                if bank_read:
                    pe.wait_ge(*bank_read)
                elif late(s, 2):
                    pe.wait_ge(s_["sh_y"], s - 1)
                for u in range(2):
                    for n in range(I // P):
                        ins = mm3(two(bank[4 + par])[:, u, :], both(act_p[par], n, tok(u)), both(sd, n, every),
                                  n == 0, n == I // P - 1)
                ins.then_inc(s_["sh_down"], 1)

            pe.wait_ge(s_["route"], 5)
            hot = rt[0][:, :, :].rearrange("p t e -> p (t e)")
            mm(bank[6][:, 0:NT * E], strict, hot, start=True, stop=True)
            mm(bank[6][:, NT * E:2 * NT * E], ones, hot, start=True, stop=True).then_inc(s_["route_pe"], 1)
            sh_gate(1, 0, 1)
            pe.wait_ge(s_["w_lo"], 6)
            sh_out(0, 0)
            sh_gate(2, 1, 0)
            sh_out(1, 1)
            with pe.Fori(1, NA // 2 - 1) as i:
                for par in range(2):
                    sh_gate(2 * i + par + 1, i + par, 1 - par)
                    sh_out(2 * i + par, par)
            sh_gate(NA - 1, NA // 2 - 1, 1)
            sh_out(NA - 2, 0)
            sh_gate(NA, NA // 2, 0)
            sh_out(NA - 1, 1)

            pe.wait_ge(s_["eid_done"], 1)
            pe.wait_ge(s_["ex_w"], 16 * 3 * E)

            def r_turn(t, i, par):
                pe.wait_ge(p_["rld"][par], 16 * (i + 1))
                if late(t, 2):
                    pe.wait_ge(s_["r_xt"], t - 1)
                for c in range(KC):
                    ins = nc.tensor.transpose(bank[6 + par][:, c * P:(c + 1) * P], xs_t[par][:, c * P:(c + 1) * P], ident)
                ins.then_inc(s_["r_t"], 1)

            def weights(t):
                return ew[:, bass.ds(pe.value_load(eid[0:1, bass.ds(t, 1)], min_val=0, max_val=E - 1), 1), :].rearrange("p a n -> p (a n)")

            def r_gu(t, par, w):
                g, up, _ = parts(w)
                pe.wait_ge(s_["r_xt"], t + 1)
                if late(t, 2):
                    pe.wait_ge(s_["r_act"], t - 1)
                for a, w in enumerate((g, up)):
                    for c in range(KC):
                        ins = mm(bank[2 * par + a][:, :], xst[par][:, c, :], w[:, c, :], start=(c == 0), stop=(c == KC - 1))
                ins.then_inc(s_["r_gu"], 1)

            def r_at(t, par):
                pe.wait_ge(s_["r_act"], t + 1)
                if late(t, 1):
                    pe.wait_ge(s_["r_att"], t)
                for n in range(I // P):
                    ins = nc.tensor.transpose(bank[4][:, n * P:(n + 1) * P], act_r[par][:, n * P:(n + 1) * P], ident)
                ins.then_inc(s_["r_at"], 1)

            def r_dn(t, par, w):
                _, _, d = parts(w)
                pe.wait_ge(s_["r_att"], t + 1)
                if late(t, 1):
                    pe.wait_ge(s_["r_y"], t)
                for n in range(I // P):
                    ins = mm(bank[5][:, 0:D], att_r[par][:, n, :], d[:, n, :], start=(n == 0), stop=(n == I // P - 1))
                ins.then_inc(s_["r_dn"], 1)

            def r_step(t, i, par):
                w1, w2 = weights(t - 1), weights(t - 2)
                r_turn(t, i, par)
                r_at(t - 2, par)
                r_gu(t - 1, 1 - par, w1)
                r_dn(t - 2, par, w2)

            r_turn(0, 0, 0)
            r_turn(1, 0, 1)
            pe.wait_ge(s_["sh_f"], 4 * NA + 4)
            r_gu(0, 0, weights(0))
            for t in (2, 3):
                r_step(t, 1, t % 2)
            with pe.Fori(2, (NRT - 1) // 2) as i:
                for par in range(2):
                    r_step(2 * i + par, i, par)
            t = NRT - 1
            r_step(t, t // 2, t % 2)
            r_at(t - 1, 1 - t % 2)
            r_gu(t, t % 2, weights(t))
            r_dn(t - 1, 1 - t % 2, weights(t - 1))
            r_at(t, t % 2)
            r_dn(t, t % 2, weights(t))

            def summed(s):
                return p_["fsum"][1], 5 * (s - 2 - NA) + 1

            sh_gate(NA + 1, NA // 2, 1)
            sh_out(NA, 0, (s_["r_att"], NRT))
            sh_gate(NA + 2, NA // 2 + 1, 0)
            sh_out(NA + 1, 1, (s_["r_y"], NRT))
            with pe.Fori(NA // 2 + 1, NS // 2 - 1) as i:
                for par in range(2):
                    s = 2 * i + par
                    sh_gate(s + 1, i + par, 1 - par)
                    sh_out(s, par, summed(s))
            sh_gate(NS - 1, NS // 2 - 1, 1)
            sh_out(NS - 2, 0, summed(NS - 2))
            sh_out(NS - 1, 1, summed(NS - 1))


_INS = ['L0_attn_inputs', 'L0_attn_ln1_scale', 'L0_attn_ln1_bias', 'L0_attn_wq', 'L0_attn_wk', 'L0_attn_wv', 'L0_attn_wo',
        'L0_attn_ln2_scale', 'L0_attn_ln2_bias', 'L0_attn_w1', 'L0_attn_b1', 'L0_attn_w2', 'L0_attn_b2', 'L0_ffn_gate_w',
        'L0_ffn_sh_gate', 'L0_ffn_sh_up', 'L0_ffn_sh_down', 'L0_ffn_rt_gate', 'L0_ffn_rt_up', 'L0_ffn_rt_down']


def _constants():
    import numpy as np
    c = np.zeros((P, C_N), np.float32)
    p = np.arange(P)
    c[:, C_ID:C_ID + P] = np.eye(P)
    c[:, C_CAUSAL:C_CAUSAL + P] = p[None, :] >= p[:, None]
    c[:, C_STRICT:C_STRICT + P] = p[:, None] < p[None, :]
    c[:, C_ONES:C_ONES + P] = 1
    c[:, C_BLOCK:C_BLOCK + 8 * VU] = np.arange(8 * VU)[None, :] // VU == p[:, None] // DH
    c[:, C_KEEP:C_KEEP + NS] = np.arange(NS) % STEPS_PER_BATCH != STEPS_PER_BATCH - 1
    c[:, C_EREV:C_EREV + E] = E - np.arange(E)
    c[:, C_TOKEN:C_TOKEN + NT] = np.arange(NT)[None, :] * P + p[:, None] + 1
    c[:, C_SLOT:C_SLOT + NRT] = np.arange(NRT)[None, :] * P + p[:, None] + 1 + TOK
    c[:, C_TILE:] = np.arange(NRT * (E - 1)) // (E - 1)
    return c


def kernel(**inputs):
    import numpy as _np
    import concourse.bacc as _bacc
    from concourse.bass_utils import run_bass_kernel_spmd as _run

    nc = _bacc.Bacc("TRN2", target_bir_lowering=False, num_devices=1)
    arrays, args = {}, []
    for name in _INS:
        a = _np.ascontiguousarray(inputs[name])
        arrays[f"in_{name}"] = a
        args.append(nc.dram_tensor(f"in_{name}", a.shape, F32, kind="ExternalInput").ap())
    arrays["in_constants"] = _constants()
    args.append(nc.dram_tensor("in_constants", (P, C_N), F32, kind="ExternalInput").ap())
    for name, shape in (("h", (TOK, D)), ("xn2", (TOK, D)), ("xt", (NS, P, KC * STEP)), ("xs", (NRT * P, DX)),
                        ("ysh", (TOK, D)), ("yr", (TOK + NRT * P, D))):
        args.append(nc.dram_tensor("scratch_" + name, shape, F32, kind="Internal").ap())
    args.append(nc.dram_tensor("out_0", (B, S, D), F32, kind="ExternalOutput").ap())
    build(nc, *args)
    r = _run(nc, [arrays], core_ids=[0])
    return r.results[0]["out_0"]
```
